# Optimizing a Trainium2 kernel written in Bass

```python
import numpy as np
import jax
import jax.numpy as jnp

def _softmax(x, axis=-1):
    return jax.nn.softmax(x, axis=axis)

def _gelu(x):
    return jax.nn.gelu(x, approximate=True)

def _silu(x):
    return jax.nn.silu(x)

def _sigmoid(x):
    return jax.nn.sigmoid(x)

def _layernorm(x, axis=-1, eps=1e-05):
    m = jnp.mean(x, axis=axis, keepdims=True)
    v = jnp.var(x, axis=axis, keepdims=True)
    return (x - m) / jnp.sqrt(v + eps)

def _scatter_add(tgt, idx, src, axis=0):
    return tgt.at[idx].add(src)

def _segment_sum(src, seg, n):
    return jax.ops.segment_sum(src, seg, n)
kernel_name = 'mk_gnn_resnorm_d4_gnn_r8_53d14e'

def setup_inputs(seed: int=0):
    np.random.seed(seed)
    _w = jnp.asarray

    def _rec_inputs():
        import jax
        import jax.numpy as jnp
        _gk = jax.random.key(seed)
        x = -0.000202 + 1 * jax.random.normal(jax.random.fold_in(_gk, 1), (12500, 64), jnp.float32)
        src = jax.random.randint(jax.random.fold_in(_gk, 2), (200000,), 0, 12500, jnp.int32)
        dst = jnp.minimum((12500 * jax.random.uniform(jax.random.fold_in(_gk, 3), (200000,)) ** 2.0).astype(jnp.int32), 99999)
        _o = jnp.argsort(dst, stable=True)
        src = src[_o]
        dst = dst[_o]
        edge_attr_32 = 0.000189758 + 1.00013 * jax.random.normal(jax.random.fold_in(_gk, 11), (200000, 32), jnp.float32)
        edge_type_32 = jax.random.randint(jax.random.fold_in(_gk, 13), (200000,), 0, 32, jnp.int32)
        return (x, src, dst, edge_attr_32, edge_type_32)
    x, src, dst, edge_attr_32, edge_type_32 = _rec_inputs()

    def _L0_gnn_setup():
        import jax, jax.numpy as jnp
        import numpy as np
        N_NODES = 12500
        N_EDGES = 200000
        IN_F = 64
        HID = 64
        OUT = 64

        def _sage_conv(h, src, dst, n_nodes, W_l, b, W_r):
            msg = h[src]
            summed = jax.ops.segment_sum(msg, dst, num_segments=n_nodes)
            cnt = jax.ops.segment_sum(jnp.ones((src.shape[0],), h.dtype), dst, num_segments=n_nodes)
            agg = summed / jnp.maximum(cnt, 1.0)[:, None]
            return agg @ W_l.T + b + h @ W_r.T
        key = jax.random.key(seed)
        ks = jax.random.split(key, 8)
        x = jax.random.normal(ks[0], (N_NODES, IN_F), dtype=jnp.float32)
        edge_index = jax.random.randint(ks[1], (2, N_EDGES), 0, N_NODES, dtype=jnp.int64)

        def glorot(k, fan_out, fan_in):
            s = jnp.sqrt(6.0 / (fan_in + fan_out))
            return jax.random.uniform(k, (fan_out, fan_in), dtype=jnp.float32, minval=-s, maxval=s)
        return {'x': x, 'edge_index': edge_index, 'W1_l': glorot(ks[2], HID, IN_F), 'b1': jnp.zeros((HID,), jnp.float32), 'W1_r': glorot(ks[3], HID, IN_F), 'W2_l': glorot(ks[4], OUT, HID), 'b2': jnp.zeros((OUT,), jnp.float32), 'W2_r': glorot(ks[5], OUT, HID)}
    _L0_gnn_all = _L0_gnn_setup()
    _L0_gnn_in = {k: v for k, v in _L0_gnn_all.items() if k in ('W1_l', 'b1', 'W1_r', 'W2_l', 'b2', 'W2_r')}
    del _L0_gnn_all

    def _L1_gnn_setup():
        import jax, jax.numpy as jnp
        import numpy as np
        NUM_NODES = 12500
        EMBED_DIM = 64
        NUM_LAYERS = 3
        NUM_EDGES = 125000
        EPS = 1e-12

        def _propagate(edge_index, x):
            row, col = (edge_index[0], edge_index[1])
            n = x.shape[0]
            deg = jax.ops.segment_sum(jnp.ones_like(col, dtype=x.dtype), col, num_segments=n)
            deg = jnp.maximum(deg, 1.0)
            norm = 1.0 / jnp.sqrt(deg[row] * deg[col])
            messages = norm[:, None] * x[col]
            return jax.ops.segment_sum(messages, row, num_segments=n)

        def _l2_normalize(x):
            nrm = jnp.linalg.norm(x, axis=1, keepdims=True)
            return x / jnp.maximum(nrm, EPS)
        key = jax.random.key(seed)
        k1, k2 = jax.random.split(key)
        edge_index = jax.random.randint(k1, (2, NUM_EDGES), 0, NUM_NODES, dtype=jnp.int64)
        emb = jax.random.normal(k2, (NUM_NODES, EMBED_DIM), dtype=jnp.float32) / EMBED_DIM ** 0.5
        return {'edge_index': edge_index, 'emb': emb}
    _L1_gnn_all = _L1_gnn_setup()
    _L1_gnn_in = {k: v for k, v in _L1_gnn_all.items() if k in ()}
    del _L1_gnn_all

    def _L2_gnn_setup():
        import jax, jax.numpy as jnp
        import numpy as np
        N_ENTITIES = 25000
        N_EDGES = 150000
        N_RELATIONS = 32
        LATDIM = 64
        N_HOPS = 2
        RES_LAMBDA = 0.5
        LEAKY_SLOPE = 0.2
        EPS = 1e-12

        def _l2_normalize(x):
            n = jnp.sqrt(jnp.sum(x * x, axis=-1, keepdims=True))
            return x / jnp.maximum(n, EPS)

        def _agg(entity_emb, relation_emb, W, head, tail, edge_type):
            n = entity_emb.shape[0]
            a_input = jnp.concatenate([entity_emb[head], entity_emb[tail]], axis=-1)
            e = jnp.sum(a_input @ W * relation_emb[edge_type], axis=-1)
            e = jax.nn.leaky_relu(e, LEAKY_SLOPE)
            m = jax.ops.segment_max(e, head, num_segments=n)
            ex = jnp.exp(e - m[head])
            denom = jax.ops.segment_sum(ex, head, num_segments=n)
            alpha = ex / denom[head]
            agg_emb = jax.ops.segment_sum(entity_emb[tail] * alpha[:, None], head, num_segments=n)
            return agg_emb + entity_emb
        key = jax.random.key(seed)
        k1, k2, k3, k4, k5 = jax.random.split(key, 5)
        entity_emb = jax.random.normal(k1, (N_ENTITIES, LATDIM), dtype=jnp.float32)
        relation_emb = jax.random.normal(k2, (N_RELATIONS, LATDIM), dtype=jnp.float32)
        W = jax.random.normal(k3, (2 * LATDIM, LATDIM), dtype=jnp.float32) * (1.0 / np.sqrt(2 * LATDIM))
        edge_index = jax.random.randint(k4, (2, N_EDGES), 0, N_ENTITIES, dtype=jnp.int64)
        edge_type = jax.random.randint(k5, (N_EDGES,), 0, N_RELATIONS, dtype=jnp.int64)
        return {'entity_emb': entity_emb, 'relation_emb': relation_emb, 'W': W, 'edge_index': edge_index, 'edge_type': edge_type}
    _L2_gnn_all = _L2_gnn_setup()
    _L2_gnn_in = {k: v for k, v in _L2_gnn_all.items() if k in ('relation_emb', 'W')}
    del _L2_gnn_all

    def _L3_gnn_setup():
        import jax, jax.numpy as jnp
        import numpy as np
        N = 6250
        E = 200000
        NODE_DIM = 64
        EDGE_DIM = 32
        HIDDEN = 64
        key = jax.random.key(seed)
        ks = jax.random.split(key, 7)
        x = jax.random.normal(ks[0], (N, NODE_DIM), dtype=jnp.float32)
        edge_index = jax.random.randint(ks[1], (2, E), 0, N, dtype=jnp.int64)
        edge_attr = jax.random.normal(ks[2], (E, EDGE_DIM), dtype=jnp.float32)
        in_dim = NODE_DIM + EDGE_DIM
        W1 = jax.random.normal(ks[3], (in_dim, HIDDEN), dtype=jnp.float32) / np.sqrt(in_dim)
        b1 = jnp.zeros((HIDDEN,), dtype=jnp.float32)
        W2 = jax.random.normal(ks[4], (HIDDEN, NODE_DIM), dtype=jnp.float32) / np.sqrt(HIDDEN)
        b2 = jnp.zeros((NODE_DIM,), dtype=jnp.float32)
        return {'x': x, 'edge_index': edge_index, 'edge_attr': edge_attr, 'W1': W1, 'b1': b1, 'W2': W2, 'b2': b2}
    _L3_gnn_all = _L3_gnn_setup()
    _L3_gnn_in = {k: v for k, v in _L3_gnn_all.items() if k in ('W1', 'b1', 'W2', 'b2')}
    del _L3_gnn_all
    return {'x': x, 'src': src, 'dst': dst, 'edge_attr_32': edge_attr_32, 'edge_type_32': edge_type_32, 'L0_gnn_W1_l': _L0_gnn_in['W1_l'], 'L0_gnn_b1': _L0_gnn_in['b1'], 'L0_gnn_W1_r': _L0_gnn_in['W1_r'], 'L0_gnn_W2_l': _L0_gnn_in['W2_l'], 'L0_gnn_b2': _L0_gnn_in['b2'], 'L0_gnn_W2_r': _L0_gnn_in['W2_r'], 'L2_gnn_relation_emb': _L2_gnn_in['relation_emb'], 'L2_gnn_W': _L2_gnn_in['W'], 'L3_gnn_W1': _L3_gnn_in['W1'], 'L3_gnn_b1': _L3_gnn_in['b1'], 'L3_gnn_W2': _L3_gnn_in['W2'], 'L3_gnn_b2': _L3_gnn_in['b2']}

def reference(x, src, dst, edge_attr_32, edge_type_32, L0_gnn_W1_l, L0_gnn_b1, L0_gnn_W1_r, L0_gnn_W2_l, L0_gnn_b2, L0_gnn_W2_r, L2_gnn_relation_emb, L2_gnn_W, L3_gnn_W1, L3_gnn_b1, L3_gnn_W2, L3_gnn_b2):
    import jax
    import jax.numpy as jnp

    def _L0_gnn_ref(x, edge_index, W1_l, b1, W1_r, W2_l, b2, W2_r):
        import jax, jax.numpy as jnp
        import numpy as np
        N_NODES = 12500
        N_EDGES = 200000
        IN_F = 64
        HID = 64
        OUT = 64

        def _sage_conv(h, src, dst, n_nodes, W_l, b, W_r):
            msg = h[src]
            summed = jax.ops.segment_sum(msg, dst, num_segments=n_nodes)
            cnt = jax.ops.segment_sum(jnp.ones((src.shape[0],), h.dtype), dst, num_segments=n_nodes)
            agg = summed / jnp.maximum(cnt, 1.0)[:, None]
            return agg @ W_l.T + b + h @ W_r.T
        src, dst = (edge_index[0], edge_index[1])
        n = x.shape[0]
        h = jax.nn.relu(_sage_conv(x, src, dst, n, W1_l, b1, W1_r))
        return _sage_conv(h, src, dst, n, W2_l, b2, W2_r)

    def _L1_gnn_ref(edge_index, emb):
        import jax, jax.numpy as jnp
        import numpy as np
        NUM_NODES = 12500
        EMBED_DIM = 64
        NUM_LAYERS = 3
        NUM_EDGES = 125000
        EPS = 1e-12

        def _propagate(edge_index, x):
            row, col = (edge_index[0], edge_index[1])
            n = x.shape[0]
            deg = jax.ops.segment_sum(jnp.ones_like(col, dtype=x.dtype), col, num_segments=n)
            deg = jnp.maximum(deg, 1.0)
            norm = 1.0 / jnp.sqrt(deg[row] * deg[col])
            messages = norm[:, None] * x[col]
            return jax.ops.segment_sum(messages, row, num_segments=n)

        def _l2_normalize(x):
            nrm = jnp.linalg.norm(x, axis=1, keepdims=True)
            return x / jnp.maximum(nrm, EPS)
        x = emb
        outs = [x]
        for _ in range(NUM_LAYERS):
            x = _propagate(edge_index, x)
            x = x + outs[-1]
            x = _l2_normalize(x)
            outs.append(x)
        return jnp.mean(jnp.stack(outs, axis=0), axis=0)

    def _L2_gnn_ref(entity_emb, relation_emb, W, edge_index, edge_type):
        import jax, jax.numpy as jnp
        import numpy as np
        N_ENTITIES = 25000
        N_EDGES = 150000
        N_RELATIONS = 32
        LATDIM = 64
        N_HOPS = 2
        RES_LAMBDA = 0.5
        LEAKY_SLOPE = 0.2
        EPS = 1e-12

        def _l2_normalize(x):
            n = jnp.sqrt(jnp.sum(x * x, axis=-1, keepdims=True))
            return x / jnp.maximum(n, EPS)

        def _agg(entity_emb, relation_emb, W, head, tail, edge_type):
            n = entity_emb.shape[0]
            a_input = jnp.concatenate([entity_emb[head], entity_emb[tail]], axis=-1)
            e = jnp.sum(a_input @ W * relation_emb[edge_type], axis=-1)
            e = jax.nn.leaky_relu(e, LEAKY_SLOPE)
            m = jax.ops.segment_max(e, head, num_segments=n)
            ex = jnp.exp(e - m[head])
            denom = jax.ops.segment_sum(ex, head, num_segments=n)
            alpha = ex / denom[head]
            agg_emb = jax.ops.segment_sum(entity_emb[tail] * alpha[:, None], head, num_segments=n)
            return agg_emb + entity_emb
        head, tail = (edge_index[0], edge_index[1])
        entity_res_emb = entity_emb
        ent = entity_emb
        for _ in range(N_HOPS):
            ent = _agg(ent, relation_emb, W, head, tail, edge_type)
            ent = _l2_normalize(ent)
            entity_res_emb = RES_LAMBDA * entity_res_emb + ent
        return entity_res_emb

    def _L3_gnn_ref(x, edge_index, edge_attr, W1, b1, W2, b2):
        import jax, jax.numpy as jnp
        import numpy as np
        N = 6250
        E = 200000
        NODE_DIM = 64
        EDGE_DIM = 32
        HIDDEN = 64
        dst = edge_index[1]
        x_i = x[dst]
        msg_in = jnp.concatenate([x_i, edge_attr], -1)
        h = jax.nn.relu(msg_in @ W1 + b1)
        m = jax.nn.relu(h @ W2 + b2)
        n = x.shape[0]
        summed = jax.ops.segment_sum(m, dst, num_segments=n)
        cnt = jax.ops.segment_sum(jnp.ones((m.shape[0],), m.dtype), dst, num_segments=n)
        aggr = summed / jnp.maximum(cnt, 1.0)[:, None]
        return aggr + x
    edge_index = jnp.stack([src, dst])
    x = _layernorm(x + _L0_gnn_ref(x, edge_index, L0_gnn_W1_l, L0_gnn_b1, L0_gnn_W1_r, L0_gnn_W2_l, L0_gnn_b2, L0_gnn_W2_r), axis=-1)
    x = _layernorm(x + _L1_gnn_ref(edge_index, x), axis=-1)
    x = _layernorm(x + _L2_gnn_ref(x, L2_gnn_relation_emb, L2_gnn_W, edge_index, edge_type_32), axis=-1)
    x = _layernorm(x + _L3_gnn_ref(x, edge_index, edge_attr_32, L3_gnn_W1, L3_gnn_b1, L3_gnn_W2, L3_gnn_b2), axis=-1)
    return x

_drawn_inputs = setup_inputs


def setup_inputs(seed=0):
    import zlib

    import numpy as np

    out = dict(_drawn_inputs(seed))
    spreads = {'L0_gnn_b1': (0.0, 0.1),
     'L0_gnn_b2': (0.0, 0.1),
     'L3_gnn_b1': (0.0, 0.423),
     'L3_gnn_b2': (0.0, 0.273)}
    factors = {}
    for name, (base, spread) in spreads.items():
        noise = np.random.default_rng([zlib.crc32(name.encode()), seed]).standard_normal(out[name].shape)
        drawn = base * np.exp(spread * noise) if base else spread * noise
        out[name] = jnp.asarray(drawn.astype(out[name].dtype))
    for name, factor in factors.items():
        out[name] = (out[name] * factor).astype(out[name].dtype)
    return out
```

```python
from contextlib import ExitStack

import concourse.bass as bass
from concourse import mybir

ALU = mybir.AluOpType
ACT = mybir.ActivationFunctionType
AX = mybir.AxisListType.X
F32 = mybir.dt.float32
I32 = mybir.dt.int32

P = 128
NODES = 12500
EDGES = 200000
D = 64
EA = 32
REL = 32
NB = 100
ROWS = P * NB
PAD_NODE = 98 * P
G = 7
J = 1568
JG = J // G
T = (P * J + 99 * (P - 1)) // P
TG = T // G
BIG = 1.0e30
EPS_LN = 1e-5
EPS_L2 = 1e-12
assert T == 1666 and T % (2 * G) == 0 and J % (2 * G) == 0


class Chain:

    def __init__(self, eng, sem):
        self.eng, self.sem, self.n, self.loop = eng, sem, 0, 0

    def inc(self, ins):
        ins.then_inc(self.sem, 1)
        self.n += 1

    def wait(self):
        self.eng.wait_ge(self.sem, self.loop + self.n)

    def link(self, ins):
        self.inc(ins)
        self.wait()

    def enter(self, i, steps):
        self.loop, self.steps, self.at = i * steps, steps, self.n

    def leave(self, trips):
        assert self.n - self.at == self.steps, (self.n - self.at, self.steps)
        self.loop = 0
        self.n = self.at + self.steps * trips


def build(nc, A, out, debug=None):
    with ExitStack() as ctx:
        def sb(name, shape, dt=F32):
            return ctx.enter_context(nc.sbuf_tensor(name, shape, dt))

        def sem(name):
            return ctx.enter_context(nc.semaphore(name))

        def dram(name, shape, dt=F32):
            return nc.dram_tensor(name, shape, dt, kind="Internal").ap()

        NA = NB * D
        nodes = [sb(f"nodes{i}", [P, NB * (D + 1) if i == 3 else NA]) for i in range(5)]
        far = {o: sb(f"far_{o}", [P, T], I32) for o in "ds"}
        loc = {o: sb(f"loc_{o}", [P, T]) for o in "ds"}
        rel = sb("rel", [P, T])
        tblk_sb = sb("tblk", [33, TG * 8], I32)
        tblk = {"d": tblk_sb[0:1, :], "s": tblk_sb[32:33, :]}
        ident = sb("ident", [P, P])
        before = sb("before", [P, P])
        ones = sb("ones", [P, P])
        iota_n = sb("iota_n", [P, P])
        small = sb("small", [P, 8])
        cnt = sb("cnt", [P, NB])
        base = sb("base", [P, NB])
        S = [sb(f"S{h}", [P, G * P]) for h in range(2)]
        ST = [sb(f"ST{h}", [P, G * P]) for h in range(2)]
        M = [sb(f"M{h}", [P, G * 96]) for h in range(2)]
        M2 = [sb(f"M2{h}", [P, G * 65]) for h in range(2)]
        nidx = [sb(f"nidx{h}", [P, G], I32) for h in range(2)]
        ps = [ctx.enter_context(nc.psum_tensor(f"ps{i}", [P, 512], F32)) for i in range(8)]

        rec_d = dram("rec_d", [P * T, 2 + EA])
        rec_s = dram("rec_s", [P * T, 3])
        table = [dram(f"table{i}", [ROWS, 96 if i >= 2 else D]) for i in range(4)]

        s_const = sem("s_const")
        s_dma = sem("s_dma")
        dma_n = [0]
        s_v = sem("s_v")
        vn = [0]
        s_nop = sem("s_nop")
        s_scat = [sem(f"s_scat{h}") for h in range(2)]
        s_st = [sem(f"s_st{h}") for h in range(2)]
        s_ea = [sem(f"s_ea{h}") for h in range(2)]
        s_rd = [sem(f"s_rd{h}") for h in range(2)]
        s_cp = [sem(f"s_cp{h}") for h in range(2)]
        s_ac = [sem(f"s_ac{h}") for h in range(2)]
        s_pe = sem("s_pe")
        pen = [0]
        n_sort = {"ac": 0, "scat": 0, "st": 0, "rd": 0, "ea": 0}

        def pool_wait(pool, s, v):
            pool.wait_ge(s, v)
            pool.sem_inc(s_nop, 1)

        with nc.Block() as block:
            @block.gpsimd
            def _(pool):
                nc.gpsimd.iota(iota_n[:], pattern=[[1, P]], base=0, channel_multiplier=0,
                               allow_small_or_imprecise_dtypes=True).then_inc(s_const, 1)
                nc.gpsimd.memset(ident[:], 0.0).then_inc(s_const, 1)
                nc.gpsimd.memset(before[:], 0.0).then_inc(s_const, 1)
                nc.gpsimd.memset(ones[:], 1.0).then_inc(s_const, 1)
                pool.wait_ge(s_const, 4)
                nc.gpsimd.affine_select(out=ident[:], in_=ident[:], compare_op=ALU.not_equal, fill=1.0,
                                        base=0, pattern=[[-1, P]], channel_multiplier=1).then_inc(s_const, 1)
                nc.gpsimd.affine_select(out=before[:], in_=before[:], compare_op=ALU.is_ge, fill=1.0,
                                        base=0, pattern=[[-1, P]], channel_multiplier=1).then_inc(s_const, 1)
                pool.wait_ge(s_const, 6)
                nc.gpsimd.memset(tblk_sb[:], 0).then_inc(s_const, 1)
                pool.wait_ge(s_const, 7)

        def sort(o):
            W = 2 + EA if o == "d" else 3
            rec = rec_d if o == "d" else rec_s
            near_in, far_in = (A["dst"], A["src"]) if o == "d" else (A["src"], A["dst"])
            def view(a, k):
                return nodes[a][:, k * J:(k + 1) * J]
            nearI, farI, relI = view(0, 0).bitcast(I32), view(0, 1).bitcast(I32), view(0, 2).bitcast(I32)
            blkF, mask, scan, pos = view(1, 0), view(1, 1), view(1, 2), view(1, 3)
            posI, tmpI = view(2, 0).bitcast(I32), view(2, 1).bitcast(I32)
            PW = 3 if o == "s" else 2
            pay = nodes[3][:, 0:J * PW].rearrange("p (j w) -> p j w", w=PW)
            payI = nodes[3][:, 0:J * PW].bitcast(I32).rearrange("p (j w) -> p j w", w=PW)
            iota_t = nodes[2][:, 2 * J:2 * J + T]
            cmp = nodes[2][:, 2 * J:2 * J + T]
            fill = nodes[2][:, 0:6 * G * W]
            fillI = fill.bitcast(I32)
            bval = small[:, 0:1]
            stage = [M[h][:, 0:G * W].rearrange("p (g w) -> p g w", w=W) if W <= 13 else
                     M2[h][:, 0:G * W].rearrange("p (g w) -> p g w", w=W) for h in range(2)]
            eabuf = [M[h][:, 0:G * EA].rearrange("p (g w) -> p g w", w=EA) for h in range(2)]
            d0 = dma_n[0]
            v0 = vn[0]
            p0 = pen[0]
            nload = 3 if o == "s" else 2
            chain_at = {}
            with nc.Block() as block:
                NFILL = TG // 6 + 1

                @block.sync
                def _(sp):
                    sp.dma_start(nearI, near_in).then_inc(s_dma, 16)
                    sp.dma_start(farI, far_in).then_inc(s_dma, 16)
                    if o == "s":
                        sp.dma_start(relI, A["typ"]).then_inc(s_dma, 16)
                    sp.wait_ge(s_v, v0 + 2)
                    rv = rec.rearrange("(p t) w -> p (t w)", p=P)
                    n = 0
                    for k in range(0, TG, 6):
                        w = min(6, TG - k) * G * W
                        sp.dma_start(rv[:, k * G * W:k * G * W + w], fill[:, 0:w]).then_inc(s_dma, 16)
                        n += 1
                    sp.wait_ge(s_dma, d0 + 16 * (nload + n))
                    chain_at["fills"] = n

                @block.gpsimd
                def _(pool):
                    pool.wait_ge(s_v, v0 + 1)
                    nc.gpsimd.iota(iota_t, pattern=[[1, T]], base=0, channel_multiplier=0,
                                   allow_small_or_imprecise_dtypes=True).then_inc(s_pe, 1)

                @block.vector
                def _(dve):
                    c = Chain(dve, s_v)
                    c.n = vn[0]
                    fr = fillI.rearrange("p (t w) -> p t w", w=W)
                    c.link(nc.vector.memset(fill, 0.0))
                    c.link(nc.vector.memset(fill.rearrange("p (t w) -> p t w", w=W)[:, :, 1], -1.0))
                    dve.wait_ge(s_dma, d0 + 16 * (nload + 40))
                    c.inc(nc.vector.tensor_scalar(tmpI, nearI, P - 1, None, ALU.bitwise_and))
                    c.link(nc.vector.tensor_scalar(posI, nearI, 7, None, ALU.logical_shift_right))
                    c.inc(nc.vector.tensor_copy(pay[:, :, 1], tmpI))
                    c.inc(nc.vector.tensor_copy(blkF, posI))
                    if o == "s":
                        c.inc(nc.vector.tensor_copy(pay[:, :, 2], relI))
                    c.wait()
                    c.inc(nc.vector.tensor_scalar(tmpI, farI, P - 1, None, ALU.bitwise_and))
                    c.link(nc.vector.tensor_scalar(posI, farI, 7, None, ALU.logical_shift_right))
                    c.inc(nc.vector.tensor_copy(scan, tmpI))
                    c.link(nc.vector.tensor_copy(mask, posI))
                    c.link(nc.vector.scalar_tensor_tensor(out=scan, in0=scan, scalar=float(NB), in1=mask,
                                                          op0=ALU.mult, op1=ALU.add))
                    c.link(nc.vector.tensor_copy(payI[:, :, 0], scan))
                    c.link(nc.vector.memset(bval, 0.0))
                    with dve.Fori(0, NB, 1) as b:
                        c.enter(b, 3)
                        c.link(nc.vector.tensor_scalar(mask, blkF, bval, None, ALU.is_equal))
                        c.inc(nc.vector.tensor_reduce(cnt[:, bass.ds(b, 1)], mask, AX, ALU.add))
                        c.link(nc.vector.tensor_scalar(bval, bval, 1.0, None, ALU.add))
                    c.leave(NB)
                    chain_at["cnt"] = c.n
                    dve.wait_ge(s_pe, p0 + 2)
                    totI = small[0:NB, 2:3].bitcast(I32)
                    c.link(nc.vector.tensor_scalar(totI, ps[0][0:NB, 0:1], float(P - 1), None, ALU.add))
                    c.link(nc.vector.tensor_scalar(totI, totI, 7, None, ALU.logical_shift_right))
                    c.link(nc.vector.tensor_copy(small[0:NB, 3:4], totI))
                    chain_at["tiles"] = c.n
                    dve.wait_ge(s_pe, p0 + 3)
                    c.link(nc.vector.tensor_copy(small[0:NB, 4:5], ps[1][0:NB, 0:1]))
                    c.inc(nc.vector.tensor_scalar(cmp[0:NB, :], iota_t[0:NB, :], small[0:NB, 4:5], None, ALU.is_ge))
                    c.link(nc.vector.tensor_scalar(S[0][0:NB, 0:NB], ident[0:NB, 0:NB], small[0:NB, 4:5], float(P),
                                                   ALU.mult, ALU.mult))
                    chain_at["diag"] = c.n
                    dve.wait_ge(s_pe, p0 + 4)
                    c.inc(nc.vector.tensor_scalar(base[:], ps[2][:, 0:NB], -1.0, None, ALU.add))
                    for q in range(7):
                        row = tblk[o].rearrange("p (g w) -> p g w", w=8)[:, 34 * q:34 * q + 34, 0:G]
                        src = ps[3 + q // 2][0:1, (q % 2) * 256:(q % 2) * 256 + 238].rearrange("p (g w) -> p g w", w=G)
                        c.inc(nc.vector.tensor_scalar(row, src, -1.0, None, ALU.add))
                    c.inc(nc.vector.memset(pos, 0.0))
                    c.link(nc.vector.memset(bval, 0.0))
                    with dve.Fori(0, NB, 1) as b:
                        c.enter(b, 5)
                        c.link(nc.vector.tensor_scalar(mask, blkF, bval, None, ALU.is_equal))
                        c.link(nc.vector.tensor_tensor_scan(scan, ones[:, 0:1].to_broadcast([P, J]), mask,
                                                            base[:, bass.ds(b, 1)], ALU.mult, ALU.add))
                        c.link(nc.vector.scalar_tensor_tensor(out=mask, in0=blkF, scalar=bval, in1=scan,
                                                              op0=ALU.is_equal, op1=ALU.mult))
                        c.inc(nc.vector.tensor_tensor(pos, pos, mask, ALU.add))
                        c.link(nc.vector.tensor_scalar(bval, bval, 1.0, None, ALU.add))
                    c.leave(NB)
                    c.link(nc.vector.tensor_copy(posI, pos))
                    c.inc(nc.vector.tensor_scalar(tmpI, posI, 7, None, ALU.logical_shift_right))
                    c.link(nc.vector.tensor_scalar(posI, posI, P - 1, None, ALU.bitwise_and))
                    c.inc(nc.vector.tensor_copy(scan, tmpI))
                    c.link(nc.vector.tensor_copy(mask, posI))
                    c.link(nc.vector.scalar_tensor_tensor(out=scan, in0=mask, scalar=float(T), in1=scan,
                                                          op0=ALU.mult, op1=ALU.add))
                    c.link(nc.vector.tensor_copy(posI, scan))
                    chain_at["end"] = c.n

                @block.tensor
                def _(pe):
                    pe.wait_ge(s_pe, p0 + 1)
                    pe.wait_ge(s_v, chain_at["cnt"])
                    nc.tensor.matmul(ps[0][0:NB, 0:1], cnt[:], ones[:, 0:1], start=True, stop=True).then_inc(s_pe, 1)
                    pe.wait_ge(s_v, chain_at["tiles"])
                    nc.tensor.matmul(ps[1][0:NB, 0:1], before[0:NB, 0:NB], small[0:NB, 3:4], start=True,
                                     stop=True).then_inc(s_pe, 1)
                    pe.wait_ge(s_v, chain_at["diag"])
                    nc.tensor.matmul(ps[2][:, 0:NB], ones[0:NB, :], S[0][0:NB, 0:NB], start=True, stop=False)
                    nc.tensor.matmul(ps[2][:, 0:NB], before[:], cnt[:], start=False, stop=True)
                    for q in range(7):
                        last = nc.tensor.matmul(ps[3 + q // 2][0:1, (q % 2) * 256:(q % 2) * 256 + 238],
                                                ones[0:NB, 0:1], cmp[0:NB, 238 * q:238 * q + 238],
                                                start=True, stop=True)
                    last.then_inc(s_pe, 1)
            dma_n[0] += 16 * (nload + chain_at["fills"])
            vn[0] = chain_at["end"]
            pen[0] += 4

            st0, sc0, ea0 = n_sort["st"], n_sort["scat"], n_sort["ea"]
            TR = JG // 2
            NC = 3 if o == "d" else 2
            ac0 = n_sort["ac"]
            with nc.Block() as block:
                @block.sync
                def _(sp):
                    if o == "d":
                        ea_v = A["ea"].rearrange("(p j) w -> p (j w)", p=P)

                        def load(i, h, first):
                            if not first:
                                sp.wait_ge(s_st[h], st0 + i)
                            sp.dma_start(M[h][:, 0:G * EA], ea_v[:, bass.ds((2 * i + h) * (G * EA), G * EA)]
                                         ).then_inc(s_ea[h], 16)

                        for h in range(2):
                            load(0, h, True)
                        with sp.Fori(1, TR, 1) as i:
                            for h in range(2):
                                load(i, h, False)

                @block.scalar
                def _(act):
                    def stage_group(i, h, first):
                        if not first:
                            act.wait_ge(s_scat[h], sc0 + i * (16 * G))
                        g = 2 * i + h
                        nc.scalar.copy(nidx[h][:], posI[:, bass.ds(g * G, G)]).then_inc(s_ac[h], 1)
                        nc.scalar.copy(stage[h][:, :, 0:PW], pay[:, bass.ds(g * G, G), :]).then_inc(s_ac[h], 1)
                        if o == "d":
                            act.wait_ge(s_ea[h], ea0 + 16 * i + 16)
                            nc.scalar.copy(stage[h][:, :, 2:W], eabuf[h]).then_inc(s_ac[h], 1)
                        act.wait_ge(s_ac[h], ac0 + NC * i + NC)
                        act.sem_inc(s_st[h], 1)

                    for h in range(2):
                        stage_group(0, h, True)
                    with act.Fori(1, TR, 1) as i:
                        for h in range(2):
                            stage_group(i, h, False)

                @block.gpsimd
                def _(pool):
                    with pool.Fori(0, TR, 1) as i:
                        for h in range(2):
                            pool_wait(pool, s_st[h], st0 + i + 1)
                            for k in range(G):
                                pool.indirect_dma_start(rec[:, :], bass.IndirectOffsetOnAxis(nidx[h][:, k:k + 1], 0),
                                                        stage[h][:, k, :], None).then_inc(s_scat[h], 16)
                    for h in range(2):
                        pool.wait_ge(s_scat[h], sc0 + 16 * G * TR)
            n_sort["st"] += TR
            n_sort["scat"] += 16 * G * TR
            n_sort["ea"] += 16 * TR if o == "d" else 0
            n_sort["ac"] += NC * TR

            rd0 = n_sort["rd"]
            CT = 49
            buf = [nodes[h][:, 0:CT * W] for h in range(2)]
            rv = rec.rearrange("(p t) w -> p (t w)", p=P)
            with nc.Block() as block:
                @block.sync
                def _(sp):
                    with sp.Fori(0, T // CT // 2, 1) as i:
                        for h in range(2):
                            sp.wait_ge(s_cp[h], cp0[0] + i * (PW) + 1)
                            sp.dma_start(buf[h], rv[:, bass.ds((2 * i + h) * (CT * W), CT * W)]).then_inc(s_rd[h], 16)

                @block.vector
                def _(dve):
                    for h in range(2):
                        dve.sem_inc(s_cp[h], 1)
                    with dve.Fori(0, T // CT // 2, 1) as i:
                        for h in range(2):
                            dve.wait_ge(s_rd[h], rd0 + 16 * i + 16)
                            col = bass.ds((2 * i + h) * CT, CT)
                            bI = buf[h].bitcast(I32).rearrange("p (t w) -> p t w", w=W)
                            bF = buf[h].rearrange("p (t w) -> p t w", w=W)
                            nc.vector.tensor_copy(far[o][:, col], bI[:, :, 0]).then_inc(s_cp[h], 1)
                            nc.vector.tensor_copy(loc[o][:, col], bF[:, :, 1]).then_inc(s_cp[h], 1)
                            if o == "s":
                                nc.vector.tensor_copy(rel[:, col], bF[:, :, 2]).then_inc(s_cp[h], 1)
            n_sort["rd"] += 16 * (T // CT // 2)
            cp0[0] += 1 + PW * (T // CT // 2)

        cp0 = [0]
        acc = nodes[3][:, 0:NB * (D + 1)].rearrange("p (b w) -> p b w", w=D + 1)
        X, H, Y, Z = (nodes[i][:, 0:NA].rearrange("p (b w) -> p b w", w=D) for i in (0, 1, 2, 4))

        ct = sb("ct", [P, 4, P])
        ctT = sb("ctT", [P, 512])
        wts = {n: sb(f"w_{n}", list(A[n].shape)) for n in ("w0a", "w0b", "w3a", "w3b", "w3c", "WT", "relT")}
        bias = {n: sb(f"b_{n}", [P, D]) for n in ("b0a", "b0b", "b3a")}
        pq_w = sb("pq_w", [D, 2 * REL])
        rcnt = cnt
        nv = [sb(f"nv{i}", [P, NB]) for i in range(3)]
        dinv = sb("dinv", [P, NB])
        s_lc, s_lt, s_la, s_lm, s_lo = (sem(n) for n in ("s_lc", "s_lt", "s_la", "s_lm", "s_lo"))
        lin_n = [0]

        def node_linear(inA, scale, inB, w, bias_ap, relu, dst):
            K = P if inB is not None else D
            base_n = lin_n[0]
            R = NB // 4
            with nc.Block() as block:
                @block.vector
                def _(dve):
                    def gather_cat(i, first):
                        if not first:
                            dve.wait_ge(s_lt, base_n + i)
                        b4 = bass.ds(i * 4, 4)
                        if scale is None:
                            a = nc.vector.tensor_copy(ct[:, :, 0:D], inA[:, b4, 0:D])
                        else:
                            a = nc.vector.tensor_tensor(ct[:, :, 0:D], inA[:, b4, 0:D],
                                                        scale[:, b4].unsqueeze(2).to_broadcast([P, 4, D]), ALU.mult)
                        a.then_inc(s_lc, 1)
                        if inB is not None:
                            nc.vector.tensor_copy(ct[:, :, D:P], inB[:, b4, 0:D]).then_inc(s_lc, 1)
                        else:
                            dve.sem_inc(s_lc, 1)

                    gather_cat(0, True)

                    def finish(i):
                        dve.wait_ge(s_lm, base_n + i + 1)
                        b4 = bass.ds(i * 4, 4)
                        src = ps[2][:, 0:4 * D].rearrange("p (b w) -> p b w", w=D)
                        if bias_ap is not None:
                            ins = nc.vector.tensor_tensor(dst[:, b4, :], src, bias_ap.unsqueeze(1).to_broadcast([P, 4, D]), ALU.add)
                        else:
                            ins = nc.vector.tensor_copy(dst[:, b4, :], src)
                        ins.then_inc(s_lo, 1)

                    with dve.Fori(1, R, 1) as i:
                        gather_cat(i, False)
                        finish(i - 1)
                    finish(R - 1)
                    if relu:
                        dve.wait_ge(s_lo, base_n + R)
                        nc.vector.tensor_scalar(dst[:, :, :], dst[:, :, :], 0.0, None, ALU.max)

                @block.tensor
                def _(pe):
                    def blocks(i, first):
                        pe.wait_ge(s_lc, 2 * base_n + 2 * i + 2)
                        if not first:
                            pe.wait_ge(s_la, base_n + i)
                        for k in range(4):
                            last = nc.tensor.transpose(ps[0][:, k * P:(k + 1) * P], ct[:, k, :], ident[:])
                        last.then_inc(s_lt, 1)
                        pe.wait_ge(s_la, base_n + i + 1)
                        if not first:
                            pe.wait_ge(s_lo, base_n + i)
                        for k in range(4):
                            last = nc.tensor.matmul(ps[2][:, k * D:(k + 1) * D], ctT[0:K, k * P:(k + 1) * P], w,
                                                    start=True, stop=True)
                        last.then_inc(s_lm, 1)
                    blocks(0, True)
                    with pe.Fori(1, R, 1) as i:
                        blocks(i, False)

                @block.scalar
                def _(act):
                    def copy(i, first):
                        act.wait_ge(s_lt, base_n + i + 1)
                        if not first:
                            act.wait_ge(s_lm, base_n + i)
                        nc.scalar.copy(ctT[0:K, :], ps[0][0:K, :]).then_inc(s_la, 1)
                    copy(0, True)
                    with act.Fori(1, R, 1) as i:
                        copy(i, False)
            lin_n[0] += R

        def vector_steps(f):
            with nc.Block() as block:
                @block.vector
                def _(dve):
                    c = Chain(dve, s_v)
                    c.n = vn[0]
                    f(c)
                    vn[0] = c.n

        def bc(v):
            return v[:, :].unsqueeze(2).to_broadcast([P, NB, D])

        s_sq = sem("s_sq")
        sq_n = [0]

        def root(v, r):
            with nc.Block() as block:
                @block.scalar
                def _(act):
                    nc.scalar.activation(r[:], v[:], ACT.Sqrt).then_inc(s_sq, 1)

                @block.vector
                def _(dve):
                    dve.wait_ge(s_sq, sq_n[0] + 1)
                    c = Chain(dve, s_v)
                    c.n = vn[0]
                    c.link(nc.vector.tensor_scalar(r[:], r[:], 1e-30, None, ALU.max))
                    c.link(nc.vector.reciprocal(nv[2][:], r[:]))
                    c.link(nc.vector.tensor_tensor(nv[2][:], v[:], nv[2][:], ALU.mult))
                    c.link(nc.vector.tensor_tensor(r[:], r[:], nv[2][:], ALU.add))
                    c.link(nc.vector.tensor_scalar(r[:], r[:], 0.5, None, ALU.mult))
                    vn[0] = c.n
            sq_n[0] += 1

        def layernorm(a, b, dst):
            def moments(c):
                c.link(nc.vector.tensor_reduce(nv[0][:], a, AX, ALU.add))
                c.link(nc.vector.tensor_scalar(nv[0][:], nv[0][:], 1.0 / D, None, ALU.mult))
                c.link(nc.vector.tensor_tensor(a, a, bc(nv[0]), ALU.subtract))
                c.link(nc.vector.tensor_tensor(b, a, a, ALU.mult))
                c.link(nc.vector.tensor_reduce(nv[0][:], b, AX, ALU.add))
                c.link(nc.vector.tensor_scalar(nv[0][:], nv[0][:], 1.0 / D, EPS_LN, ALU.mult, ALU.add))

            def scale(c):
                c.link(nc.vector.reciprocal(nv[1][:], nv[1][:]))
                c.link(nc.vector.tensor_tensor(dst, a, bc(nv[1]), ALU.mult))
            vector_steps(moments)
            root(nv[0], nv[1])
            vector_steps(scale)

        def l2norm(a, b, dst):
            def squares(c):
                c.link(nc.vector.tensor_tensor(b, a, a, ALU.mult))
                c.link(nc.vector.tensor_reduce(nv[0][:], b, AX, ALU.add))

            def scale(c):
                c.link(nc.vector.tensor_scalar(nv[1][:], nv[1][:], EPS_L2, None, ALU.max))
                c.link(nc.vector.reciprocal(nv[1][:], nv[1][:]))
                c.link(nc.vector.tensor_tensor(dst, a, bc(nv[1]), ALU.mult))
            vector_steps(squares)
            root(nv[0], nv[1])
            vector_steps(scale)

        def store_table(tab, parts):
            with nc.Block() as block:
                @block.sync
                def _(sp):
                    tv = tab.rearrange("(p b) w -> p b w", p=P)
                    for src, lo, hi in parts:
                        sp.dma_start(tv[:, :, lo:hi], src).then_inc(s_dma, 16)
                    sp.wait_ge(s_dma, dma_n[0] + 16 * len(parts))
            dma_n[0] += 16 * len(parts)

        s_ix = [sem(f"s_ix{h}") for h in range(2)]
        ga = [[sem(f"s_ga{n}_{h}") for h in range(2)] for n in range(7)]
        s_oh, s_grp, s_acc, s_add = sem("s_oh"), sem("s_grp"), sem("s_acc"), sem("s_add")
        n_ix, n_pass, n_g, n_acc = [0], [0], [0], [0]
        R = TG // 2
        iota_b = iota_n[:, :].unsqueeze(1).to_broadcast([P, G, P])

        def tile_blocks(engine, o, g):
            return nc.values_load_multi_w_load_instructions(
                tblk[o][:, bass.ds(g * 8, G)], engines=[engine], min_val=0, max_val=NB - 1,
                skip_runtime_bounds_check_because="a tile's block is a count of buckets minus one")[1]

        def stage_indices(act, o, i, h, first):
            g = 2 * i + h
            if not first:
                act.wait_ge(s_grp, n_g[0] + 2 * i + h - 1)
            nc.scalar.copy(nidx[h][:], far[o][:, bass.ds(g * G, G)]).then_inc(s_ix[h], 1)

        def gather_rows(pool, s_ga, tab, i, h, stride, w):
            pool_wait(pool, s_ix[h], n_ix[0] + i + 1)
            for k in range(G):
                pool.indirect_dma_start(M[h][:, k * stride:k * stride + w], None, tab[:, :],
                                        bass.IndirectOffsetOnAxis(nidx[h][:, k:k + 1], 0)).then_inc(s_ga[h], 16)

        def onehot(dve, o, i, h, first):
            g = 2 * i + h
            if not first:
                dve.wait_ge(s_grp, n_g[0] + 2 * i + h - 1)
            near = loc[o][:, bass.ds(g * G, G)].unsqueeze(2).to_broadcast([P, G, P])
            nc.vector.tensor_tensor(S[h][:].rearrange("p (g n) -> p g n", g=G), iota_b, near,
                                    ALU.is_equal).then_inc(s_oh, 1)

        def add_tiles(dve, o, i, h, bank):
            g = 2 * i + h
            blk = tile_blocks(mybir.EngineType.DVE, o, g)
            dve.wait_ge(s_grp, n_g[0] + g + 1)
            for k in range(G):
                a = acc[:, bass.ds(blk[k], 1), :]
                nc.vector.tensor_tensor(a, a, bank[:, k * 65:(k + 1) * 65].unsqueeze(1), ALU.add).then_inc(s_add, 1)
                dve.wait_ge(s_add, (n_acc[0] + g) * G + k + 1)
            dve.sem_inc(s_acc, 1)

        def seg_pass(o, tab):
            s_ga = ga[n_pass[0]]
            with nc.Block() as block:
                @block.scalar
                def _(act):
                    for h in range(2):
                        stage_indices(act, o, 0, h, True)
                    with act.Fori(1, R, 1) as i:
                        for h in range(2):
                            stage_indices(act, o, i, h, False)

                @block.gpsimd
                def _(pool):
                    with pool.Fori(0, R, 1) as i:
                        for h in range(2):
                            gather_rows(pool, s_ga, tab, i, h, 65, D)
                    for h in range(2):
                        pool.wait_ge(s_ga[h], 16 * G * R)

                @block.vector
                def _(dve):
                    onehot(dve, o, 0, 0, True)
                    onehot(dve, o, 0, 1, True)
                    add_tiles(dve, o, 0, 0, ps[0])
                    with dve.Fori(1, R, 1) as i:
                        onehot(dve, o, i, 0, False)
                        add_tiles(dve, o, i - 1, 1, ps[1])
                        onehot(dve, o, i, 1, False)
                        add_tiles(dve, o, i, 0, ps[0])
                    add_tiles(dve, o, R - 1, 1, ps[1])

                @block.tensor
                def _(pe):
                    def group(i, h, first):
                        g = 2 * i + h
                        pe.wait_ge(s_oh, n_g[0] + g + 1)
                        if not first:
                            pe.wait_ge(s_acc, n_acc[0] + g - 1)
                        pe.wait_ge(s_ga[h], 16 * G * (i + 1))
                        for k in range(G):
                            last = nc.tensor.matmul(ps[h][:, k * 65:(k + 1) * 65], S[h][:, k * P:(k + 1) * P],
                                                    M[h][:, k * 65:(k + 1) * 65], start=True, stop=True)
                        last.then_inc(s_grp, 1)
                    for h in range(2):
                        group(0, h, True)
                    with pe.Fori(1, R, 1) as i:
                        for h in range(2):
                            group(i, h, False)
            n_ix[0] += R
            n_pass[0] += 1
            n_g[0] += TG
            n_acc[0] += TG

        def clear_acc(c):
            c.inc(nc.vector.memset(nodes[3][:], 0.0))

        def ones_column(c):
            for h in range(2):
                c.inc(nc.vector.memset(M[h][:, 0:G * 65].rearrange("p (g w) -> p g w", w=65)[:, :, D], 1.0))

        sort("d")
        sort("s")

        with nc.Block() as block:
            @block.sync
            def _(sp):
                sp.dma_start(X, A["x"].rearrange("(b p) w -> p b w", p=P)).then_inc(s_dma, 16)
                for n in wts:
                    sp.dma_start(wts[n][:], A[n]).then_inc(s_dma, 16)
                for n in bias:
                    sp.dma_start(bias[n][:], A[n].partition_broadcast(P)).then_inc(s_dma, 16)
                sp.wait_ge(s_dma, dma_n[0] + 16 * (1 + len(wts) + len(bias)))
        dma_n[0] += 16 * (1 + len(wts) + len(bias))

        store_table(table[0], [(X, 0, D)])
        vector_steps(lambda c: (clear_acc(c), ones_column(c)))
        seg_pass("d", table[0])

        def counts(c):
            c.link(nc.vector.tensor_scalar(cnt[:, :], acc[:, :, D], 1.0, None, ALU.max))

        def count_roots(c):
            c.inc(nc.vector.reciprocal(dinv[:, :], nv[1][:, :]))
            c.link(nc.vector.reciprocal(rcnt[:, :], cnt[:, :]))
        vector_steps(counts)
        root(cnt, nv[1])
        vector_steps(count_roots)
        node_linear(acc, rcnt, X, wts["w0a"][:], bias["b0a"][:], True, H)
        store_table(table[1], [(H, 0, D)])
        vector_steps(clear_acc)
        seg_pass("d", table[1])
        node_linear(acc, rcnt, H, wts["w0b"][:], bias["b0b"][:], False, Y)

        vector_steps(lambda c: c.link(nc.vector.tensor_tensor(Y, Y, X, ALU.add)))
        layernorm(Y, H, X)

        if debug != "l0":
            def l1_start(c):
                c.inc(nc.vector.tensor_copy(Y, X))
                c.inc(nc.vector.tensor_copy(H, X))
                c.link(nc.vector.tensor_tensor(Z, X, bc(dinv), ALU.mult))
                clear_acc(c)
            vector_steps(l1_start)
            for layer in range(3):
                store_table(table[layer % 2], [(Z, 0, D)])
                seg_pass("s", table[layer % 2])

                def l1_step(c):
                    c.link(nc.vector.tensor_tensor(acc[:, :, 0:D], acc[:, :, 0:D], bc(dinv), ALU.mult))
                    c.link(nc.vector.tensor_tensor(H, acc[:, :, 0:D], H, ALU.add))

                def l1_next(c):
                    c.inc(nc.vector.tensor_tensor(Y, Y, H, ALU.add))
                    c.link(nc.vector.tensor_tensor(Z, H, bc(dinv), ALU.mult))
                    clear_acc(c)
                vector_steps(l1_step)
                l2norm(H, Z, H)
                vector_steps(l1_next)

            def l1_end(c):
                c.link(nc.vector.scalar_tensor_tensor(out=Y, in0=Y, scalar=0.25, in1=X, op0=ALU.mult, op1=ALU.add))
            vector_steps(l1_end)
            layernorm(Y, H, X)

        V = [sb(f"V{h}", [P, G * P]) for h in range(1)] * 2
        ty = sb("ty", [P, G * REL])
        sc = sb("sc", [P, G])
        ex = sb("ex", [P, G])
        mt = sb("mt", [P, G])
        mn = sb("mn", [P, G])
        fac = sb("fac", [P, 2 * G])
        mx = sb("mx", [P, NB])
        s_at = {n: sem("s_at_" + n) for n in ("st", "stc", "pe", "neg", "v", "vt", "mt", "me", "arg", "ex", "w", "agg",
                                              "d", "f", "own", "done")}
        n_at = [0]
        OWN = 11 + 5 * G

        def attention_pass(tab, PQ):
            s_ga = ga[n_pass[0]]
            q = s_at
            b0 = n_at[0]
            with nc.Block() as block:
                @block.gpsimd
                def _(pool):
                    with pool.Fori(0, R, 1) as i:
                        for h in range(2):
                            gather_rows(pool, s_ga, tab, i, h, 96, 96)
                    for h in range(2):
                        pool.wait_ge(s_ga[h], 16 * G * R)

                @block.scalar
                def _(act):
                    def group(i, h, first):
                        g = 2 * i + h
                        act.wait_ge(s_oh, n_g[0] + g + 1)
                        if not (first and h == 0):
                            act.wait_ge(q["vt"], b0 + g)
                        nc.scalar.activation(V[h][:], S[h][:], ACT.Copy, bias=-BIG, scale=BIG).then_inc(q["neg"], 1)
                        act.wait_ge(q["st"], b0 + g + 1)
                        nc.scalar.copy(ST[h][:, 0:512], ps[0][:, 0:512]).then_inc(q["stc"], 1)
                        nc.scalar.copy(ST[h][:, 512:G * P], ps[1][:, 0:G * P - 512]).then_inc(q["stc"], 1)
                        act.wait_ge(q["arg"], b0 + g + 1)
                        nc.scalar.activation(ex[:], sc[:], ACT.Exp).then_inc(q["ex"], 1)
                        act.wait_ge(q["d"], b0 + g + 1)
                        nc.scalar.activation(fac[:], fac[:], ACT.Exp).then_inc(q["f"], 1)

                    for h in range(2):
                        stage_indices(act, "s", 0, h, True)
                    for h in range(2):
                        group(0, h, True)
                    with act.Fori(1, R, 1) as i:
                        for h in range(2):
                            stage_indices(act, "s", i, h, False)
                            group(i, h, False)

                @block.tensor
                def _(pe):
                    def group(i, h, first):
                        g = 2 * i + h
                        blk = tile_blocks(mybir.EngineType.PE, "s", g)
                        pe.wait_ge(s_oh, n_g[0] + g + 1)
                        if not (first and h == 0):
                            pe.wait_ge(q["stc"], 2 * (b0 + g))
                        for k in range(G):
                            last = nc.tensor.transpose(ps[k // 4][:, (k % 4) * P:(k % 4 + 1) * P],
                                                       S[h][:, k * P:(k + 1) * P], ident[:])
                        last.then_inc(q["st"], 1)
                        pe.wait_ge(q["stc"], 2 * (b0 + g + 1))
                        if not (first and h == 0):
                            pe.wait_ge(q["arg"], b0 + g)
                        for k in range(G):
                            last = nc.tensor.matmul(ps[4][:, k * REL:(k + 1) * REL], ST[h][:, k * P:(k + 1) * P],
                                                    PQ[:, bass.ds(blk[k], 1), 0:REL], start=True, stop=True)
                        last.then_inc(q["pe"], 1)
                        pe.wait_ge(q["v"], b0 + g + 1)
                        for k in range(G):
                            last = nc.tensor.transpose(ps[2 + k // 4][:, (k % 4) * P:(k % 4 + 1) * P],
                                                       V[h][:, k * P:(k + 1) * P], ident[:])
                        last.then_inc(q["vt"], 1)
                        pe.wait_ge(q["mt"], b0 + g + 1)
                        for k in range(G):
                            last = nc.tensor.matmul(ps[4][:, 256 + k:257 + k], ST[h][:, k * P:(k + 1) * P],
                                                    mt[:, k:k + 1], start=True, stop=True)
                        last.then_inc(q["me"], 1)
                        pe.wait_ge(q["w"], b0 + g + 1)
                        for k in range(G):
                            last = nc.tensor.matmul(ps[5][:, k * 65:(k + 1) * 65], S[h][:, k * P:(k + 1) * P],
                                                    M2[h][:, k * 65:(k + 1) * 65], start=True, stop=True)
                        last.then_inc(s_grp, 1)

                    for h in range(2):
                        group(0, h, True)
                    with pe.Fori(1, R, 1) as i:
                        for h in range(2):
                            group(i, h, False)

                @block.vector
                def _(dve):
                    c = Chain(dve, q["own"])
                    own0 = b0 * OWN

                    def group(i, h, first):
                        g = 2 * i + h
                        c.loop, c.n = own0 + g * OWN, 0
                        blk = tile_blocks(mybir.EngineType.DVE, "s", g)
                        Mv = M[h][:, 0:G * 96].rearrange("p (g w) -> p g w", w=96)
                        tv = ty[:].rearrange("p (g r) -> p g r", r=REL)
                        Wv = M2[h][:, 0:G * 65].rearrange("p (g w) -> p g w", w=65)
                        one = [P, G, REL]
                        col = bass.ds(g * G, G)
                        c.link(nc.vector.tensor_tensor(tv, iota_n[:, 0:REL].unsqueeze(1).to_broadcast(one),
                                                       rel[:, col].unsqueeze(2).to_broadcast(one), ALU.is_equal))
                        dve.wait_ge(s_ga[h], 16 * G * (i + 1))
                        dve.wait_ge(q["pe"], b0 + g + 1)
                        u = V2[:, 0:G * REL].rearrange("p (g r) -> p g r", r=REL)
                        c.link(nc.vector.tensor_tensor(u, Mv[:, :, D:D + REL],
                                                       ps[4][:, 0:G * REL].rearrange("p (g r) -> p g r", r=REL), ALU.add))
                        c.link(nc.vector.tensor_tensor(u, u, tv, ALU.mult))
                        c.link(nc.vector.tensor_reduce(sc[:], u, AX, ALU.add))
                        c.link(nc.vector.scalar_tensor_tensor(out=sc[:], in0=sc[:], scalar=0.2, in1=sc[:],
                                                              op0=ALU.mult, op1=ALU.max))
                        dve.wait_ge(q["neg"], b0 + g + 1)
                        Vv = V[h][:].rearrange("p (g n) -> p g n", n=P)
                        nc.vector.tensor_tensor(Vv, Vv, sc[:].unsqueeze(2).to_broadcast([P, G, P]),
                                                ALU.add).then_inc(q["v"], 1)
                        dve.wait_ge(q["vt"], b0 + g + 1)
                        c.inc(nc.vector.tensor_reduce(mt[:, 0:4], ps[2][:, 0:512].rearrange("p (g n) -> p g n", n=P),
                                                      AX, ALU.max))
                        c.link(nc.vector.tensor_reduce(mt[:, 4:G], ps[3][:, 0:3 * P].rearrange("p (g n) -> p g n", n=P),
                                                       AX, ALU.max))
                        dve.sem_inc(q["mt"], 1)
                        dve.wait_ge(q["me"], b0 + g + 1)
                        c.link(nc.vector.tensor_tensor(sc[:], sc[:], ps[4][:, 256:256 + G], ALU.subtract))
                        nc.vector.tensor_scalar(sc[:], sc[:], 0.0, None, ALU.min).then_inc(q["arg"], 1)
                        for k in range(G):
                            m = mx[:, bass.ds(blk[k], 1)]
                            c.inc(nc.vector.tensor_scalar(fac[:, k:k + 1], m, 0.0, None, ALU.add))
                            c.link(nc.vector.tensor_tensor(mn[:, k:k + 1], m, mt[:, k:k + 1], ALU.max))
                            c.link(nc.vector.tensor_scalar(m, mn[:, k:k + 1], 0.0, None, ALU.add))
                        c.link(nc.vector.tensor_tensor(fac[:, 0:G], fac[:, 0:G], mn[:], ALU.subtract))
                        c.link(nc.vector.tensor_tensor(fac[:, G:2 * G], mt[:], mn[:], ALU.subtract))
                        dve.sem_inc(q["d"], 1)
                        dve.wait_ge(q["ex"], b0 + g + 1)
                        c.inc(nc.vector.tensor_copy(Wv[:, :, D], ex[:]))
                        nc.vector.tensor_tensor(Wv[:, :, 0:D], Mv[:, :, 0:D],
                                                ex[:].unsqueeze(2).to_broadcast([P, G, D]), ALU.mult).then_inc(q["w"], 1)
                        c.wait()
                        dve.wait_ge(q["w"], b0 + g + 1)
                        dve.sem_inc(q["done"], 1)
                        dve.wait_ge(q["f"], b0 + g + 1)
                        dve.wait_ge(s_grp, n_g[0] + g + 1)
                        for k in range(G):
                            a = acc[:, bass.ds(blk[k], 1), :]
                            w = ps[5][:, k * 65:(k + 1) * 65].unsqueeze(1)
                            c.link(nc.vector.tensor_scalar(a, a, fac[:, k:k + 1], None, ALU.mult))
                            c.link(nc.vector.scalar_tensor_tensor(out=a, in0=w, scalar=fac[:, G + k:G + k + 1], in1=a,
                                                                  op0=ALU.mult, op1=ALU.add))
                        assert c.n == OWN, c.n

                    onehot(dve, "s", 0, 0, True)
                    onehot(dve, "s", 0, 1, True)
                    group(0, 0, True)
                    with dve.Fori(1, R, 1) as i:
                        onehot(dve, "s", i, 0, False)
                        group(i - 1, 1, False)
                        onehot(dve, "s", i, 1, False)
                        group(i, 0, False)
                    group(R - 1, 1, False)
            n_ix[0] += R
            n_pass[0] += 1
            n_g[0] += TG
            n_at[0] += TG

        V2 = sb("V2", [P, G * REL])
        with nc.Block() as block:
            @block.tensor
            def _(pe):
                nc.tensor.matmul(ps[0][0:D, 0:REL], wts["WT"][:, 0:D], wts["relT"][:], start=True, stop=True)
                nc.tensor.matmul(ps[0][0:D, REL:2 * REL], wts["WT"][:, D:2 * D], wts["relT"][:], start=True,
                                 stop=True).then_inc(s_pe, 1)

            @block.vector
            def _(dve):
                dve.wait_ge(s_pe, pen[0] + 1)
                nc.vector.tensor_copy(pq_w[:], ps[0][0:D, 0:2 * REL]).then_inc(s_v, 1)
                dve.wait_ge(s_v, vn[0] + 1)
        pen[0] += 1
        vn[0] += 1

        def l2_start(c):
            c.inc(nc.vector.tensor_copy(Y, X))
            c.inc(nc.vector.tensor_copy(H, X))
            c.wait()
        vector_steps(l2_start)
        for hop in range(2):
            node_linear(Y, None, None, pq_w[:], None, False, Z)
            t2 = table[2 + hop]
            store_table(t2, [(Y, 0, D), (Z[:, :, REL:2 * REL], D, D + REL)])

            def hop_start(c):
                clear_acc(c)
                c.link(nc.vector.memset(mx[:], -BIG))
            vector_steps(hop_start)
            attention_pass(t2, Z)

            def hop_sum(c):
                c.link(nc.vector.tensor_scalar(nv[0][:, :], acc[:, :, D], 1e-30, None, ALU.max))
                c.link(nc.vector.reciprocal(nv[0][:], nv[0][:]))
                c.link(nc.vector.tensor_tensor(Z, acc[:, :, 0:D], bc(nv[0]), ALU.mult))
                c.link(nc.vector.tensor_tensor(Y, Y, Z, ALU.add))
            vector_steps(hop_sum)
            l2norm(Y, Z, Y)
            vector_steps(lambda c: c.link(nc.vector.scalar_tensor_tensor(out=H, in0=H, scalar=0.5, in1=Y, op0=ALU.mult,
                                                                         op1=ALU.add)))
        vector_steps(lambda c: c.link(nc.vector.tensor_tensor(Y, X, H, ALU.add)))
        layernorm(Y, H, X)

        EW = G * (2 + EA)
        eb = [M[0][:, h * EW:(h + 1) * EW] for h in range(2)]
        eT, hT, uc = V[0], ST[1][0:D + 1, :], M[1][:, 0:G * D]
        q3 = {n: sem("s_m_" + n) for n in ("eb", "eb1", "st", "stc", "uc", "h", "hc", "m", "mc")}
        s_eb = [q3["eb"], q3["eb1"]]

        def edge_mlp_pass(U):
            q = q3
            rv = rec_d.rearrange("(p t) w -> p (t w)", p=P)
            WR = 2 + EA
            with nc.Block() as block:
                @block.sync
                def _(sp):
                    def load(i, h, first):
                        g = 2 * i + h
                        if not first:
                            sp.wait_ge(q["st"], g - 1)
                        sp.dma_start(eb[h], rv[:, bass.ds(g * (G * WR), G * WR)]).then_inc(s_eb[h], 16)
                    for h in range(2):
                        load(0, h, True)
                    with sp.Fori(1, R, 1) as i:
                        for h in range(2):
                            load(i, h, False)

                @block.vector
                def _(dve):
                    onehot(dve, "d", 0, 0, True)
                    onehot(dve, "d", 0, 1, True)
                    add_tiles(dve, "d", 0, 0, ps[7])
                    with dve.Fori(1, R, 1) as i:
                        onehot(dve, "d", i, 0, False)
                        add_tiles(dve, "d", i - 1, 1, ps[7])
                        onehot(dve, "d", i, 1, False)
                        add_tiles(dve, "d", i, 0, ps[7])
                    add_tiles(dve, "d", R - 1, 1, ps[7])

                @block.scalar
                def _(act):
                    def group(i, h, first):
                        g = 2 * i + h
                        blk = tile_blocks(mybir.EngineType.Activation, "d", g)
                        if not first:
                            act.wait_ge(q["h"], g)
                        for k in range(G):
                            nc.scalar.copy(uc[:, k * D:(k + 1) * D].unsqueeze(1),
                                           U[:, bass.ds(blk[k], 1), :]).then_inc(q["uc"], 1)
                        act.wait_ge(q["st"], g + 1)
                        nc.scalar.copy(ST[0][:, 0:512], ps[0][:, 0:512]).then_inc(q["stc"], 1)
                        nc.scalar.copy(ST[0][:, 512:G * P], ps[1][:, 0:G * P - 512]).then_inc(q["stc"], 1)
                        nc.scalar.copy(eT[0:EA, 0:512], ps[2][0:EA, 0:512]).then_inc(q["stc"], 1)
                        nc.scalar.copy(eT[0:EA, 512:G * P], ps[3][0:EA, 0:G * P - 512]).then_inc(q["stc"], 1)
                        act.wait_ge(q["h"], g + 1)
                        if not first:
                            act.wait_ge(q["m"], g)
                        nc.scalar.activation(hT[0:D, 0:512], ps[4][0:D, 0:512], ACT.Relu).then_inc(q["hc"], 1)
                        nc.scalar.activation(hT[0:D, 512:G * P], ps[5][0:D, 0:G * P - 512], ACT.Relu).then_inc(q["hc"], 1)
                        act.wait_ge(q["m"], g + 1)
                        if not first:
                            act.wait_ge(s_grp, n_g[0] + g)
                        nc.scalar.activation(M2[0][:, 0:G * 65].rearrange("p (g w) -> p g w", w=65)[:, :, 0:D],
                                             ps[6][:, 0:G * D].rearrange("p (g w) -> p g w", w=D),
                                             ACT.Relu).then_inc(q["mc"], 1)
                    group(0, 0, True)
                    group(0, 1, False)
                    with act.Fori(1, R, 1) as i:
                        for h in range(2):
                            group(i, h, False)

                @block.tensor
                def _(pe):
                    def group(i, h, first):
                        g = 2 * i + h
                        pe.wait_ge(s_oh, n_g[0] + g + 1)
                        pe.wait_ge(s_eb[h], 16 * (i + 1))
                        if not first:
                            pe.wait_ge(q["stc"], 4 * g)
                        for k in range(G):
                            nc.tensor.transpose(ps[k // 4][:, (k % 4) * P:(k % 4 + 1) * P],
                                                S[h][:, k * P:(k + 1) * P], ident[:])
                        for k in range(G):
                            last = nc.tensor.transpose(ps[2 + k // 4][0:EA, (k % 4) * P:(k % 4 + 1) * P],
                                                       eb[h][:, k * WR + 2:(k + 1) * WR], ident[:])
                        last.then_inc(q["st"], 1)
                        pe.wait_ge(q["stc"], 4 * (g + 1))
                        pe.wait_ge(q["uc"], G * (g + 1))
                        if not first:
                            pe.wait_ge(q["hc"], 2 * g)
                        for k in range(G):
                            o_ap = ps[4 + k // 4][0:D, (k % 4) * P:(k % 4 + 1) * P]
                            nc.tensor.matmul(o_ap, uc[:, k * D:(k + 1) * D], ST[0][:, k * P:(k + 1) * P],
                                             start=True, stop=False)
                            last = nc.tensor.matmul(o_ap, wts["w3b"][:], eT[0:EA, k * P:(k + 1) * P],
                                                    start=False, stop=True)
                        last.then_inc(q["h"], 1)
                        pe.wait_ge(q["hc"], 2 * (g + 1))
                        if not first:
                            pe.wait_ge(q["mc"], g)
                        for k in range(G):
                            last = nc.tensor.matmul(ps[6][:, k * D:(k + 1) * D], hT[:, k * P:(k + 1) * P],
                                                    wts["w3c"][:], start=True, stop=True)
                        last.then_inc(q["m"], 1)
                        pe.wait_ge(q["mc"], g + 1)
                        if not first:
                            pe.wait_ge(s_acc, n_acc[0] + g)
                        for k in range(G):
                            last = nc.tensor.matmul(ps[7][:, k * 65:(k + 1) * 65], S[h][:, k * P:(k + 1) * P],
                                                    M2[0][:, k * 65:(k + 1) * 65], start=True, stop=True)
                        last.then_inc(s_grp, 1)
                    group(0, 0, True)
                    group(0, 1, False)
                    with pe.Fori(1, R, 1) as i:
                        for h in range(2):
                            group(i, h, False)
            n_g[0] += TG

        node_linear(X, None, None, wts["w3a"][:], bias["b3a"][:], False, Z)

        def l3_start(c):
            clear_acc(c)
            c.inc(nc.vector.memset(hT[D:D + 1, :], 1.0))
            c.inc(nc.vector.memset(M2[0][:, 0:G * 65].rearrange("p (g w) -> p g w", w=65)[:, :, D], 1.0))
        vector_steps(l3_start)
        edge_mlp_pass(Z)

        def l3_end(c):
            c.link(nc.vector.tensor_tensor(Y, acc[:, :, 0:D], bc(rcnt), ALU.mult))
            c.link(nc.vector.scalar_tensor_tensor(out=Y, in0=X, scalar=2.0, in1=Y, op0=ALU.mult, op1=ALU.add))
        vector_steps(l3_end)
        layernorm(Y, H, X)

        with nc.Block() as block:
            @block.sync
            def _(sp):
                sp.dma_start(out[0:97 * P, :].rearrange("(b p) w -> p b w", p=P), X[:, 0:97, :]).then_inc(s_dma, 16)
                sp.dma_start(out[97 * P:NODES, :], X[0:NODES - 97 * P, 97, :]).then_inc(s_dma, 16)
                sp.wait_ge(s_dma, dma_n[0] + 32)


def kernel(**inputs):
    import numpy as np
    import concourse.bacc as bacc
    from concourse.bass_utils import run_bass_kernel_spmd as run

    def pad(a, n, v):
        a = np.ascontiguousarray(a)
        return np.concatenate([a, np.full((n - a.shape[0],) + a.shape[1:], v, a.dtype)])

    nc = bacc.Bacc("TRN2", target_bir_lowering=False, num_devices=1)
    E = P * J
    arrays = {
        "x": pad(inputs["x"], ROWS, 0),
        "src": pad(inputs["src"], E, PAD_NODE).reshape(P, J),
        "dst": pad(inputs["dst"], E, PAD_NODE).reshape(P, J),
        "typ": pad(inputs["edge_type_32"], E, 0).reshape(P, J),
        "ea": pad(inputs["edge_attr_32"], E, 0),
        "w0a": np.concatenate([np.asarray(inputs["L0_gnn_W1_l"]).T, np.asarray(inputs["L0_gnn_W1_r"]).T]),
        "w0b": np.concatenate([np.asarray(inputs["L0_gnn_W2_l"]).T, np.asarray(inputs["L0_gnn_W2_r"]).T]),
        "b0a": np.ascontiguousarray(inputs["L0_gnn_b1"]),
        "b0b": np.ascontiguousarray(inputs["L0_gnn_b2"]),
        "relT": np.ascontiguousarray(np.asarray(inputs["L2_gnn_relation_emb"]).T),
        "WT": np.ascontiguousarray(np.asarray(inputs["L2_gnn_W"]).T),
        "w3a": np.ascontiguousarray(np.asarray(inputs["L3_gnn_W1"])[0:D]),
        "w3b": np.ascontiguousarray(np.asarray(inputs["L3_gnn_W1"])[D:]),
        "b3a": np.ascontiguousarray(inputs["L3_gnn_b1"]),
        "w3c": np.concatenate([np.asarray(inputs["L3_gnn_W2"]), np.asarray(inputs["L3_gnn_b2"])[None]]),
    }
    args, feed = {}, {}
    for name, a in arrays.items():
        feed[f"in_{name}"] = a
        args[name] = nc.dram_tensor(f"in_{name}", a.shape, mybir.dt.from_np(a.dtype), kind="ExternalInput").ap()
    out = nc.dram_tensor("out_x", (NODES, D), F32, kind="ExternalOutput").ap()
    build(nc, args, out, None)
    r = run(nc, [feed], core_ids=[0])
    return r.results[0]["out_x"]
```

```python
from contextlib import ExitStack

import concourse.bass as bass
from concourse import mybir

ALU = mybir.AluOpType
ACT = mybir.ActivationFunctionType
AX = mybir.AxisListType.X
F32 = mybir.dt.float32
I32 = mybir.dt.int32

P = 128
NODES = 12500
EDGES = 200000
D = 64
EA = 32
REL = 32
NB = 100
ROWS = P * NB
PAD_NODE = 98 * P
G = 7
J = 1568
JG = J // G
T = (P * J + 99 * (P - 1)) // P
TG = T // G
BIG = 1.0e30
EPS_LN = 1e-5
EPS_L2 = 1e-12
assert T == 1666 and T % (2 * G) == 0 and J % (2 * G) == 0


class Chain:

    def __init__(self, eng, sem):
        self.eng, self.sem, self.n, self.loop = eng, sem, 0, 0

    def inc(self, ins):
        ins.then_inc(self.sem, 1)
        self.n += 1

    def wait(self):
        self.eng.wait_ge(self.sem, self.loop + self.n)

    def link(self, ins):
        self.inc(ins)
        self.wait()

    def enter(self, i, steps):
        self.loop, self.steps, self.at = i * steps, steps, self.n

    def leave(self, trips):
        assert self.n - self.at == self.steps, (self.n - self.at, self.steps)
        self.loop = 0
        self.n = self.at + self.steps * trips


def build(nc, A, out, debug=None):
    with ExitStack() as ctx:
        def sb(name, shape, dt=F32):
            return ctx.enter_context(nc.sbuf_tensor(name, shape, dt))

        def sem(name):
            return ctx.enter_context(nc.semaphore(name))

        def dram(name, shape, dt=F32):
            return nc.dram_tensor(name, shape, dt, kind="Internal").ap()

        NA = NB * D
        nodes = [sb(f"nodes{i}", [P, NB * (D + 1) if i == 3 else NA]) for i in range(5)]
        far = {o: sb(f"far_{o}", [P, T], I32) for o in "ds"}
        loc = {o: sb(f"loc_{o}", [P, T]) for o in "ds"}
        rel = sb("rel", [P, T])
        tblk_sb = sb("tblk", [33, TG * 8], I32)
        tblk = {"d": tblk_sb[0:1, :], "s": tblk_sb[32:33, :]}
        ident = sb("ident", [P, P])
        before = sb("before", [P, P])
        ones = sb("ones", [P, P])
        iota_n = sb("iota_n", [P, P])
        small = sb("small", [P, 8])
        cnt = sb("cnt", [P, NB])
        base = sb("base", [P, NB])
        S = [sb(f"S{h}", [P, G * P]) for h in range(2)]
        ST = [sb(f"ST{h}", [P, G * P]) for h in range(2)]
        M = [sb(f"M{h}", [P, G * 96]) for h in range(2)]
        spare = [nodes[0][:, k * (G * P):(k + 1) * (G * P)] for k in range(7)]
        S4 = [S[0][:], S[1][:], spare[0], spare[1]]
        ST4 = [ST[0][:], ST[1][:], spare[2], spare[3]]
        M4 = [M[0][:], M[1][:], spare[4][:, 0:G * 96], spare[5][:, 0:G * 96]]
        M2 = [sb(f"M2{h}", [P, G * 65]) for h in range(2)]
        nidx = [sb(f"nidx{h}", [P, G], I32) for h in range(4)]
        ps = [ctx.enter_context(nc.psum_tensor(f"ps{i}", [P, 512], F32)) for i in range(8)]

        rec_d = dram("rec_d", [P * T, 2 + EA])
        rec_s = dram("rec_s", [P * T, 3])
        table = [dram(f"table{i}", [ROWS, 96 if i >= 2 else D]) for i in range(4)]

        s_const = sem("s_const")
        s_dma = sem("s_dma")
        dma_n = [0]
        s_v = sem("s_v")
        vn = [0]
        s_nop = sem("s_nop")
        s_scat = [sem(f"s_scat{h}") for h in range(2)]
        s_st = [sem(f"s_st{h}") for h in range(2)]
        s_ea = [sem(f"s_ea{h}") for h in range(2)]
        s_rd = [sem(f"s_rd{h}") for h in range(2)]
        s_cp = [sem(f"s_cp{h}") for h in range(2)]
        s_ac = [sem(f"s_ac{h}") for h in range(2)]
        s_pe = sem("s_pe")
        pen = [0]
        n_sort = {"ac": 0, "cp": 0, "scat": 0, "st": 0, "rd": 0, "ea": 0}

        def pool_wait(pool, s, v):
            pool.wait_ge(s, v)
            pool.sem_inc(s_nop, 1)

        with nc.Block() as block:
            @block.gpsimd
            def _(pool):
                nc.gpsimd.iota(iota_n[:], pattern=[[1, P]], base=0, channel_multiplier=0,
                               allow_small_or_imprecise_dtypes=True).then_inc(s_const, 1)
                nc.gpsimd.memset(ident[:], 0.0).then_inc(s_const, 1)
                nc.gpsimd.memset(before[:], 0.0).then_inc(s_const, 1)
                nc.gpsimd.memset(ones[:], 1.0).then_inc(s_const, 1)
                pool.wait_ge(s_const, 4)
                nc.gpsimd.affine_select(out=ident[:], in_=ident[:], compare_op=ALU.not_equal, fill=1.0,
                                        base=0, pattern=[[-1, P]], channel_multiplier=1).then_inc(s_const, 1)
                nc.gpsimd.affine_select(out=before[:], in_=before[:], compare_op=ALU.is_ge, fill=1.0,
                                        base=0, pattern=[[-1, P]], channel_multiplier=1).then_inc(s_const, 1)
                pool.wait_ge(s_const, 6)
                nc.gpsimd.memset(tblk_sb[:], 0).then_inc(s_const, 1)
                pool.wait_ge(s_const, 7)

        width = {"d": 2 + EA, "s": 3}
        pay_width = {"d": 2, "s": 3}
        recs = {"d": rec_d, "s": rec_s}

        def view(a, k):
            return nodes[a][:, k * J:(k + 1) * J]
        slot_row = {"d": view(4, 0).bitcast(I32), "s": view(2, 0).bitcast(I32)}
        pay_at = {"d": nodes[4][:, J:3 * J], "s": nodes[3][:, 0:3 * J]}

        def rank(o):
            W, PW, rec = width[o], pay_width[o], recs[o]
            near_in, far_in = (A["dst"], A["src"]) if o == "d" else (A["src"], A["dst"])
            nearI, farI, relI = view(0, 0).bitcast(I32), view(0, 1).bitcast(I32), view(0, 2).bitcast(I32)
            blkF, mask, scan, pos = view(1, 0), view(1, 1), view(1, 2), view(1, 3)
            posI, tmpI = slot_row[o], view(2, 1).bitcast(I32)
            pay = pay_at[o].rearrange("p (j w) -> p j w", w=PW)
            payI = pay_at[o].bitcast(I32).rearrange("p (j w) -> p j w", w=PW)
            iota_t = cmp = nodes[2][:, 2 * J:2 * J + T]
            FG = 6
            fill = nodes[2][:, 0:FG * G * W]
            fills = len(range(0, TG, FG))
            bval = small[:, 0:1]
            d0, v0, p0 = dma_n[0], vn[0], pen[0]
            nload = 3 if o == "s" else 2
            after = {}

            def sync(sp):
                sp.dma_start(nearI, near_in).then_inc(s_dma, 16)
                sp.dma_start(farI, far_in).then_inc(s_dma, 16)
                if o == "s":
                    sp.dma_start(relI, A["typ"]).then_inc(s_dma, 16)
                sp.wait_ge(s_v, v0 + 2)
                rv = rec.rearrange("(p t) w -> p (t w)", p=P)
                for k in range(0, TG, FG):
                    w = min(FG, TG - k) * G * W
                    sp.dma_start(rv[:, k * G * W:k * G * W + w], fill[:, 0:w]).then_inc(s_dma, 16)
                sp.wait_ge(s_dma, d0 + 16 * (nload + fills))

            def pool(pl):
                pl.wait_ge(s_v, v0 + 1)
                nc.gpsimd.iota(iota_t, pattern=[[1, T]], base=0, channel_multiplier=0,
                               allow_small_or_imprecise_dtypes=True).then_inc(s_pe, 1)

            def vector(dve):
                c = Chain(dve, s_v)
                c.n = v0
                c.link(nc.vector.memset(fill, 0.0))
                c.link(nc.vector.memset(fill.rearrange("p (t w) -> p t w", w=W)[:, :, 1], -1.0))
                dve.wait_ge(s_dma, d0 + 16 * (nload + fills))
                c.inc(nc.vector.tensor_scalar(tmpI, nearI, P - 1, None, ALU.bitwise_and))
                c.link(nc.vector.tensor_scalar(posI, nearI, 7, None, ALU.logical_shift_right))
                c.inc(nc.vector.tensor_copy(pay[:, :, 1], tmpI))
                c.inc(nc.vector.tensor_copy(blkF, posI))
                if o == "s":
                    c.inc(nc.vector.tensor_copy(pay[:, :, 2], relI))
                c.wait()
                c.inc(nc.vector.tensor_scalar(tmpI, farI, P - 1, None, ALU.bitwise_and))
                c.link(nc.vector.tensor_scalar(posI, farI, 7, None, ALU.logical_shift_right))
                c.inc(nc.vector.tensor_copy(scan, tmpI))
                c.link(nc.vector.tensor_copy(mask, posI))
                c.link(nc.vector.scalar_tensor_tensor(out=scan, in0=scan, scalar=float(NB), in1=mask,
                                                      op0=ALU.mult, op1=ALU.add))
                c.link(nc.vector.tensor_copy(payI[:, :, 0], scan))
                c.link(nc.vector.memset(bval, 0.0))
                with dve.Fori(0, NB, 1) as b:
                    c.enter(b, 3)
                    c.link(nc.vector.tensor_scalar(mask, blkF, bval, None, ALU.is_equal))
                    c.inc(nc.vector.tensor_reduce(cnt[:, bass.ds(b, 1)], mask, AX, ALU.add))
                    c.link(nc.vector.tensor_scalar(bval, bval, 1.0, None, ALU.add))
                c.leave(NB)
                after["cnt"] = c.n
                dve.wait_ge(s_pe, p0 + 2)
                totI = small[0:NB, 2:3].bitcast(I32)
                c.link(nc.vector.tensor_scalar(totI, ps[0][0:NB, 0:1], float(P - 1), None, ALU.add))
                c.link(nc.vector.tensor_scalar(totI, totI, 7, None, ALU.logical_shift_right))
                c.link(nc.vector.tensor_copy(small[0:NB, 3:4], totI))
                after["tiles"] = c.n
                dve.wait_ge(s_pe, p0 + 3)
                c.link(nc.vector.tensor_copy(small[0:NB, 4:5], ps[1][0:NB, 0:1]))
                c.inc(nc.vector.tensor_scalar(cmp[0:NB, :], iota_t[0:NB, :], small[0:NB, 4:5], None, ALU.is_ge))
                c.link(nc.vector.tensor_scalar(S[0][0:NB, 0:NB], ident[0:NB, 0:NB], small[0:NB, 4:5], float(P),
                                               ALU.mult, ALU.mult))
                after["diag"] = c.n
                dve.wait_ge(s_pe, p0 + 4)
                c.inc(nc.vector.tensor_scalar(base[:], ps[2][:, 0:NB], -1.0, None, ALU.add))
                for q in range(7):
                    row = tblk[o].rearrange("p (g w) -> p g w", w=8)[:, 34 * q:34 * q + 34, 0:G]
                    src = ps[3 + q // 2][0:1, (q % 2) * 256:(q % 2) * 256 + 238].rearrange("p (g w) -> p g w", w=G)
                    c.inc(nc.vector.tensor_scalar(row, src, -1.0, None, ALU.add))
                c.inc(nc.vector.memset(pos, 0.0))
                c.link(nc.vector.memset(bval, 0.0))
                with dve.Fori(0, NB, 1) as b:
                    c.enter(b, 5)
                    c.link(nc.vector.tensor_scalar(mask, blkF, bval, None, ALU.is_equal))
                    c.link(nc.vector.tensor_tensor_scan(scan, ones[:, 0:1].to_broadcast([P, J]), mask,
                                                        base[:, bass.ds(b, 1)], ALU.mult, ALU.add))
                    c.link(nc.vector.scalar_tensor_tensor(out=mask, in0=blkF, scalar=bval, in1=scan,
                                                          op0=ALU.is_equal, op1=ALU.mult))
                    c.inc(nc.vector.tensor_tensor(pos, pos, mask, ALU.add))
                    c.link(nc.vector.tensor_scalar(bval, bval, 1.0, None, ALU.add))
                c.leave(NB)
                c.link(nc.vector.tensor_copy(posI, pos))
                c.inc(nc.vector.tensor_scalar(tmpI, posI, 7, None, ALU.logical_shift_right))
                c.link(nc.vector.tensor_scalar(posI, posI, P - 1, None, ALU.bitwise_and))
                c.inc(nc.vector.tensor_copy(scan, tmpI))
                c.link(nc.vector.tensor_copy(mask, posI))
                c.link(nc.vector.scalar_tensor_tensor(out=scan, in0=mask, scalar=float(T), in1=scan,
                                                      op0=ALU.mult, op1=ALU.add))
                c.link(nc.vector.tensor_copy(posI, scan))
                vn[0] = c.n

            def tensor(pe):
                pe.wait_ge(s_pe, p0 + 1)
                pe.wait_ge(s_v, after["cnt"])
                nc.tensor.matmul(ps[0][0:NB, 0:1], cnt[:], ones[:, 0:1], start=True, stop=True).then_inc(s_pe, 1)
                pe.wait_ge(s_v, after["tiles"])
                nc.tensor.matmul(ps[1][0:NB, 0:1], before[0:NB, 0:NB], small[0:NB, 3:4], start=True,
                                 stop=True).then_inc(s_pe, 1)
                pe.wait_ge(s_v, after["diag"])
                nc.tensor.matmul(ps[2][:, 0:NB], ones[0:NB, :], S[0][0:NB, 0:NB], start=True, stop=False)
                nc.tensor.matmul(ps[2][:, 0:NB], before[:], cnt[:], start=False, stop=True)
                for q in range(7):
                    last = nc.tensor.matmul(ps[3 + q // 2][0:1, (q % 2) * 256:(q % 2) * 256 + 238],
                                            ones[0:NB, 0:1], cmp[0:NB, 238 * q:238 * q + 238],
                                            start=True, stop=True)
                last.then_inc(s_pe, 1)

            dma_n[0] += 16 * (nload + fills)
            pen[0] += 4
            return sync, pool, vector, tensor

        def scatter(o):
            W, PW, rec = width[o], pay_width[o], recs[o]
            posI = slot_row[o]
            pay = pay_at[o].rearrange("p (j w) -> p j w", w=PW)
            stage = [M2[h][:, 0:G * W].rearrange("p (g w) -> p g w", w=W) for h in range(2)]
            eabuf = [M[h][:, 0:G * EA].rearrange("p (g w) -> p g w", w=EA) for h in range(2)]
            st0, sc0, ea0, ac0 = n_sort["st"], n_sort["scat"], n_sort["ea"], n_sort["ac"]
            TR = JG // 2
            NC = 3 if o == "d" else 2

            def sync(sp):
                ea_v = A["ea"].rearrange("(p j) w -> p (j w)", p=P)

                def load(i, h, first):
                    if not first:
                        sp.wait_ge(s_st[h], st0 + i)
                    sp.dma_start(M[h][:, 0:G * EA], ea_v[:, bass.ds((2 * i + h) * (G * EA), G * EA)]
                                 ).then_inc(s_ea[h], 16)

                for h in range(2):
                    load(0, h, True)
                with sp.Fori(1, TR, 1) as i:
                    for h in range(2):
                        load(i, h, False)

            def scalar(act):
                def stage_group(i, h, first):
                    if not first:
                        act.wait_ge(s_scat[h], sc0 + i * (16 * G))
                    g = 2 * i + h
                    nc.scalar.copy(nidx[h][:], posI[:, bass.ds(g * G, G)]).then_inc(s_ac[h], 1)
                    nc.scalar.copy(stage[h][:, :, 0:PW], pay[:, bass.ds(g * G, G), :]).then_inc(s_ac[h], 1)
                    if o == "d":
                        act.wait_ge(s_ea[h], ea0 + 16 * i + 16)
                        nc.scalar.copy(stage[h][:, :, 2:W], eabuf[h]).then_inc(s_ac[h], 1)
                    act.wait_ge(s_ac[h], ac0 + NC * i + NC)
                    act.sem_inc(s_st[h], 1)

                for h in range(2):
                    stage_group(0, h, True)
                with act.Fori(1, TR, 1) as i:
                    for h in range(2):
                        stage_group(i, h, False)

            def pool(pl):
                with pl.Fori(0, TR, 1) as i:
                    for h in range(2):
                        pool_wait(pl, s_st[h], st0 + i + 1)
                        for k in range(G):
                            pl.indirect_dma_start(rec[:, :], bass.IndirectOffsetOnAxis(nidx[h][:, k:k + 1], 0),
                                                  stage[h][:, k, :], None).then_inc(s_scat[h], 16)
                for h in range(2):
                    pl.wait_ge(s_scat[h], sc0 + 16 * G * TR)

            n_sort["st"] += TR
            n_sort["scat"] += 16 * G * TR
            n_sort["ea"] += 16 * TR if o == "d" else 0
            n_sort["ac"] += NC * TR
            return sync, scalar, pool

        def readback(o):
            W, PW, rec = width[o], pay_width[o], recs[o]
            rd0, c0 = n_sort["rd"], n_sort["cp"]
            CT = 49
            trips = T // CT // 2
            buf = [nodes[h][:, 0:CT * W] for h in range(2)]
            rv = rec.rearrange("(p t) w -> p (t w)", p=P)

            def sync(sp):
                def load(i, h, first):
                    if not first:
                        sp.wait_ge(s_cp[h], c0 + i * PW)
                    sp.dma_start(buf[h], rv[:, bass.ds((2 * i + h) * (CT * W), CT * W)]).then_inc(s_rd[h], 16)
                for h in range(2):
                    load(0, h, True)
                with sp.Fori(1, trips, 1) as i:
                    for h in range(2):
                        load(i, h, False)

            def vector(dve):
                with dve.Fori(0, trips, 1) as i:
                    for h in range(2):
                        dve.wait_ge(s_rd[h], rd0 + 16 * i + 16)
                        col = bass.ds((2 * i + h) * CT, CT)
                        bI = buf[h].bitcast(I32).rearrange("p (t w) -> p t w", w=W)
                        bF = buf[h].rearrange("p (t w) -> p t w", w=W)
                        nc.vector.tensor_copy(far[o][:, col], bI[:, :, 0]).then_inc(s_cp[h], 1)
                        nc.vector.tensor_copy(loc[o][:, col], bF[:, :, 1]).then_inc(s_cp[h], 1)
                        if o == "s":
                            nc.vector.tensor_copy(rel[:, col], bF[:, :, 2]).then_inc(s_cp[h], 1)

            n_sort["rd"] += 16 * trips
            n_sort["cp"] += PW * trips
            return sync, vector

        acc = nodes[3][:, 0:NB * (D + 1)].rearrange("p (b w) -> p b w", w=D + 1)
        X, H, Y, Z = (nodes[i][:, 0:NA].rearrange("p (b w) -> p b w", w=D) for i in (0, 1, 2, 4))

        ct = sb("ct", [P, 4, P])
        ctT = sb("ctT", [P, 512])
        wts = {n: sb(f"w_{n}", list(A[n].shape)) for n in ("w0a", "w0b", "w3a", "w3b", "w3c", "WT", "relT")}
        bias = {n: sb(f"b_{n}", [P, D]) for n in ("b0a", "b0b", "b3a")}
        pq_w = sb("pq_w", [D, 2 * REL])
        rcnt = cnt
        nv = [sb(f"nv{i}", [P, NB]) for i in range(3)]
        dinv = sb("dinv", [P, NB])
        s_lc, s_lt, s_la, s_lm, s_lo = (sem(n) for n in ("s_lc", "s_lt", "s_la", "s_lm", "s_lo"))
        lin_n = [0]

        def node_linear(inA, scale, inB, w, bias_ap, relu, dst):
            K = P if inB is not None else D
            base_n = lin_n[0]
            R = NB // 4
            with nc.Block() as block:
                @block.vector
                def _(dve):
                    def gather_cat(i, first):
                        if not first:
                            dve.wait_ge(s_lt, base_n + i)
                        b4 = bass.ds(i * 4, 4)
                        if scale is None:
                            a = nc.vector.tensor_copy(ct[:, :, 0:D], inA[:, b4, 0:D])
                        else:
                            a = nc.vector.tensor_tensor(ct[:, :, 0:D], inA[:, b4, 0:D],
                                                        scale[:, b4].unsqueeze(2).to_broadcast([P, 4, D]), ALU.mult)
                        a.then_inc(s_lc, 1)
                        if inB is not None:
                            nc.vector.tensor_copy(ct[:, :, D:P], inB[:, b4, 0:D]).then_inc(s_lc, 1)
                        else:
                            dve.sem_inc(s_lc, 1)

                    gather_cat(0, True)

                    def finish(i):
                        dve.wait_ge(s_lm, base_n + i + 1)
                        b4 = bass.ds(i * 4, 4)
                        src = ps[2][:, 0:4 * D].rearrange("p (b w) -> p b w", w=D)
                        if bias_ap is not None:
                            ins = nc.vector.tensor_tensor(dst[:, b4, :], src, bias_ap.unsqueeze(1).to_broadcast([P, 4, D]), ALU.add)
                        else:
                            ins = nc.vector.tensor_copy(dst[:, b4, :], src)
                        ins.then_inc(s_lo, 1)

                    with dve.Fori(1, R, 1) as i:
                        gather_cat(i, False)
                        finish(i - 1)
                    finish(R - 1)
                    if relu:
                        dve.wait_ge(s_lo, base_n + R)
                        nc.vector.tensor_scalar(dst[:, :, :], dst[:, :, :], 0.0, None, ALU.max)

                @block.tensor
                def _(pe):
                    def blocks(i, first):
                        pe.wait_ge(s_lc, 2 * base_n + 2 * i + 2)
                        if not first:
                            pe.wait_ge(s_la, base_n + i)
                        for k in range(4):
                            last = nc.tensor.transpose(ps[0][:, k * P:(k + 1) * P], ct[:, k, :], ident[:])
                        last.then_inc(s_lt, 1)
                        pe.wait_ge(s_la, base_n + i + 1)
                        if not first:
                            pe.wait_ge(s_lo, base_n + i)
                        for k in range(4):
                            last = nc.tensor.matmul(ps[2][:, k * D:(k + 1) * D], ctT[0:K, k * P:(k + 1) * P], w,
                                                    start=True, stop=True)
                        last.then_inc(s_lm, 1)
                    blocks(0, True)
                    with pe.Fori(1, R, 1) as i:
                        blocks(i, False)

                @block.scalar
                def _(act):
                    def copy(i, first):
                        act.wait_ge(s_lt, base_n + i + 1)
                        if not first:
                            act.wait_ge(s_lm, base_n + i)
                        nc.scalar.copy(ctT[0:K, :], ps[0][0:K, :]).then_inc(s_la, 1)
                    copy(0, True)
                    with act.Fori(1, R, 1) as i:
                        copy(i, False)
            lin_n[0] += R

        def vector_steps(f):
            with nc.Block() as block:
                @block.vector
                def _(dve):
                    c = Chain(dve, s_v)
                    c.n = vn[0]
                    f(c)
                    vn[0] = c.n

        def bc(v):
            return v[:, :].unsqueeze(2).to_broadcast([P, NB, D])

        s_sq = sem("s_sq")
        sq_n = [0]

        def root(v, r):
            with nc.Block() as block:
                @block.scalar
                def _(act):
                    nc.scalar.activation(r[:], v[:], ACT.Sqrt).then_inc(s_sq, 1)

                @block.vector
                def _(dve):
                    dve.wait_ge(s_sq, sq_n[0] + 1)
                    c = Chain(dve, s_v)
                    c.n = vn[0]
                    c.link(nc.vector.tensor_scalar(r[:], r[:], 1e-30, None, ALU.max))
                    c.link(nc.vector.reciprocal(nv[2][:], r[:]))
                    c.link(nc.vector.tensor_tensor(nv[2][:], v[:], nv[2][:], ALU.mult))
                    c.link(nc.vector.tensor_tensor(r[:], r[:], nv[2][:], ALU.add))
                    c.link(nc.vector.tensor_scalar(r[:], r[:], 0.5, None, ALU.mult))
                    vn[0] = c.n
            sq_n[0] += 1

        def layernorm(a, b, dst):
            def moments(c):
                c.link(nc.vector.tensor_reduce(nv[0][:], a, AX, ALU.add))
                c.link(nc.vector.tensor_scalar(nv[0][:], nv[0][:], 1.0 / D, None, ALU.mult))
                c.link(nc.vector.tensor_tensor(a, a, bc(nv[0]), ALU.subtract))
                c.link(nc.vector.tensor_tensor(b, a, a, ALU.mult))
                c.link(nc.vector.tensor_reduce(nv[0][:], b, AX, ALU.add))
                c.link(nc.vector.tensor_scalar(nv[0][:], nv[0][:], 1.0 / D, EPS_LN, ALU.mult, ALU.add))

            def scale(c):
                c.link(nc.vector.reciprocal(nv[1][:], nv[1][:]))
                c.link(nc.vector.tensor_tensor(dst, a, bc(nv[1]), ALU.mult))
            vector_steps(moments)
            root(nv[0], nv[1])
            vector_steps(scale)

        def l2norm(a, b, dst):
            def squares(c):
                c.link(nc.vector.tensor_tensor(b, a, a, ALU.mult))
                c.link(nc.vector.tensor_reduce(nv[0][:], b, AX, ALU.add))

            def scale(c):
                c.link(nc.vector.tensor_scalar(nv[1][:], nv[1][:], EPS_L2, None, ALU.max))
                c.link(nc.vector.reciprocal(nv[1][:], nv[1][:]))
                c.link(nc.vector.tensor_tensor(dst, a, bc(nv[1]), ALU.mult))
            vector_steps(squares)
            root(nv[0], nv[1])
            vector_steps(scale)

        def store_table(tab, parts):
            with nc.Block() as block:
                @block.sync
                def _(sp):
                    tv = tab.rearrange("(p b) w -> p b w", p=P)
                    for src, lo, hi in parts:
                        sp.dma_start(tv[:, :, lo:hi], src).then_inc(s_dma, 16)
                    sp.wait_ge(s_dma, dma_n[0] + 16 * len(parts))
            dma_n[0] += 16 * len(parts)

        s_ix = [sem(f"s_ix{h}") for h in range(2)]
        ga = [[sem(f"s_ga{n}_{h}") for h in range(2)] for n in range(5)]
        s_oh, s_grp, s_acc, s_add = sem("s_oh"), sem("s_grp"), sem("s_acc"), sem("s_add")
        n_ix, n_pass, n_g, n_acc = [0], [0], [0], [0]
        R = TG // 2
        iota_b = iota_n[:, :].unsqueeze(1).to_broadcast([P, G, P])

        def tile_blocks(engine, o, g):
            return nc.values_load_multi_w_load_instructions(
                tblk[o][:, bass.ds(g * 8, G)], engines=[engine], min_val=0, max_val=NB - 1,
                skip_runtime_bounds_check_because="a tile's block is a count of buckets minus one")[1]

        def stage_indices(act, o, i, h, first):
            g = 2 * i + h
            if not first:
                act.wait_ge(s_grp, n_g[0] + 2 * i + h - 1)
            nc.scalar.copy(nidx[h][:], far[o][:, bass.ds(g * G, G)]).then_inc(s_ix[h], 1)

        def gather_rows(pool, s_ga, tab, i, h, stride, w):
            pool_wait(pool, s_ix[h], n_ix[0] + i + 1)
            for k in range(G):
                pool.indirect_dma_start(M[h][:, k * stride:k * stride + w], None, tab[:, :],
                                        bass.IndirectOffsetOnAxis(nidx[h][:, k:k + 1], 0)).then_inc(s_ga[h], 16)

        def onehot(dve, o, i, h, first):
            g = 2 * i + h
            if not first:
                dve.wait_ge(s_grp, n_g[0] + 2 * i + h - 1)
            near = loc[o][:, bass.ds(g * G, G)].unsqueeze(2).to_broadcast([P, G, P])
            nc.vector.tensor_tensor(S[h][:].rearrange("p (g n) -> p g n", g=G), iota_b, near,
                                    ALU.is_equal).then_inc(s_oh, 1)

        def add_tiles(dve, o, i, h, bank):
            g = 2 * i + h
            blk = tile_blocks(mybir.EngineType.DVE, o, g)
            dve.wait_ge(s_grp, n_g[0] + g + 1)
            for k in range(G):
                a = acc[:, bass.ds(blk[k], 1), :]
                nc.vector.tensor_tensor(a, a, bank[:, k * 65:(k + 1) * 65].unsqueeze(1), ALU.add).then_inc(s_add, 1)
                dve.wait_ge(s_add, (n_acc[0] + g) * G + k + 1)
            dve.sem_inc(s_acc, 1)

        def seg_pass(o, tab):
            s_ga = ga[n_pass[0]]
            with nc.Block() as block:
                @block.scalar
                def _(act):
                    for h in range(2):
                        stage_indices(act, o, 0, h, True)
                    with act.Fori(1, R, 1) as i:
                        for h in range(2):
                            stage_indices(act, o, i, h, False)

                @block.gpsimd
                def _(pool):
                    with pool.Fori(0, R, 1) as i:
                        for h in range(2):
                            gather_rows(pool, s_ga, tab, i, h, 65, D)
                    for h in range(2):
                        pool.wait_ge(s_ga[h], 16 * G * R)

                @block.vector
                def _(dve):
                    onehot(dve, o, 0, 0, True)
                    onehot(dve, o, 0, 1, True)
                    add_tiles(dve, o, 0, 0, ps[0])
                    with dve.Fori(1, R, 1) as i:
                        onehot(dve, o, i, 0, False)
                        add_tiles(dve, o, i - 1, 1, ps[1])
                        onehot(dve, o, i, 1, False)
                        add_tiles(dve, o, i, 0, ps[0])
                    add_tiles(dve, o, R - 1, 1, ps[1])

                @block.tensor
                def _(pe):
                    def group(i, h, first):
                        g = 2 * i + h
                        pe.wait_ge(s_oh, n_g[0] + g + 1)
                        if not first:
                            pe.wait_ge(s_acc, n_acc[0] + g - 1)
                        pe.wait_ge(s_ga[h], 16 * G * (i + 1))
                        for k in range(G):
                            last = nc.tensor.matmul(ps[h][:, k * 65:(k + 1) * 65], S[h][:, k * P:(k + 1) * P],
                                                    M[h][:, k * 65:(k + 1) * 65], start=True, stop=True)
                        last.then_inc(s_grp, 1)
                    for h in range(2):
                        group(0, h, True)
                    with pe.Fori(1, R, 1) as i:
                        for h in range(2):
                            group(i, h, False)
            n_ix[0] += R
            n_pass[0] += 1
            n_g[0] += TG
            n_acc[0] += TG

        def clear_acc(c):
            c.inc(nc.vector.memset(nodes[3][:], 0.0))

        def ones_column(c):
            for h in range(2):
                c.inc(nc.vector.memset(M[h][:, 0:G * 65].rearrange("p (g w) -> p g w", w=65)[:, :, D], 1.0))

        rank_sync, rank_pool, rank_vector, rank_tensor = rank("d")
        with nc.Block() as block:
            block.sync(rank_sync)
            block.gpsimd(rank_pool)
            block.vector(rank_vector)
            block.tensor(rank_tensor)

        scat_sync, scat_scalar, scat_pool = scatter("d")
        rank_sync, rank_pool, rank_vector, rank_tensor = rank("s")
        with nc.Block() as block:
            @block.sync
            def _(sp):
                rank_sync(sp)
                scat_sync(sp)

            @block.gpsimd
            def _(pool):
                rank_pool(pool)
                scat_pool(pool)
            block.scalar(scat_scalar)
            block.vector(rank_vector)
            block.tensor(rank_tensor)

        _, scat_scalar, scat_pool = scatter("s")
        read_sync, read_vector = readback("d")
        with nc.Block() as block:
            block.sync(read_sync)
            block.scalar(scat_scalar)
            block.gpsimd(scat_pool)
            block.vector(read_vector)

        read_sync, read_vector = readback("s")
        with nc.Block() as block:
            block.sync(read_sync)
            block.vector(read_vector)

        with nc.Block() as block:
            @block.sync
            def _(sp):
                sp.dma_start(X, A["x"].rearrange("(b p) w -> p b w", p=P)).then_inc(s_dma, 16)
                for n in wts:
                    sp.dma_start(wts[n][:], A[n]).then_inc(s_dma, 16)
                for n in bias:
                    sp.dma_start(bias[n][:], A[n].partition_broadcast(P)).then_inc(s_dma, 16)
                sp.wait_ge(s_dma, dma_n[0] + 16 * (1 + len(wts) + len(bias)))
        dma_n[0] += 16 * (1 + len(wts) + len(bias))

        store_table(table[0], [(X, 0, D)])
        vector_steps(lambda c: (clear_acc(c), ones_column(c)))
        seg_pass("d", table[0])

        def counts(c):
            c.link(nc.vector.tensor_scalar(cnt[:, :], acc[:, :, D], 1.0, None, ALU.max))

        def count_roots(c):
            c.inc(nc.vector.reciprocal(dinv[:, :], nv[1][:, :]))
            c.link(nc.vector.reciprocal(rcnt[:, :], cnt[:, :]))
        vector_steps(counts)
        root(cnt, nv[1])
        vector_steps(count_roots)
        node_linear(acc, rcnt, X, wts["w0a"][:], bias["b0a"][:], True, H)
        store_table(table[1], [(H, 0, D)])
        vector_steps(clear_acc)
        seg_pass("d", table[1])
        node_linear(acc, rcnt, H, wts["w0b"][:], bias["b0b"][:], False, Y)

        vector_steps(lambda c: c.link(nc.vector.tensor_tensor(Y, Y, X, ALU.add)))
        layernorm(Y, H, X)

        if debug != "l0":
            def l1_start(c):
                c.inc(nc.vector.tensor_copy(Y, X))
                c.inc(nc.vector.tensor_copy(H, X))
                c.link(nc.vector.tensor_tensor(Z, X, bc(dinv), ALU.mult))
                clear_acc(c)
            vector_steps(l1_start)
            for layer in range(3):
                store_table(table[layer % 2], [(Z, 0, D)])
                seg_pass("s", table[layer % 2])

                def l1_step(c):
                    c.link(nc.vector.tensor_tensor(acc[:, :, 0:D], acc[:, :, 0:D], bc(dinv), ALU.mult))
                    c.link(nc.vector.tensor_tensor(H, acc[:, :, 0:D], H, ALU.add))

                def l1_next(c):
                    c.inc(nc.vector.tensor_tensor(Y, Y, H, ALU.add))
                    c.link(nc.vector.tensor_tensor(Z, H, bc(dinv), ALU.mult))
                    clear_acc(c)
                vector_steps(l1_step)
                l2norm(H, Z, H)
                vector_steps(l1_next)

            def l1_end(c):
                c.link(nc.vector.scalar_tensor_tensor(out=Y, in0=Y, scalar=0.25, in1=X, op0=ALU.mult, op1=ALU.add))
            vector_steps(l1_end)
            layernorm(Y, H, X)

        V = [sb("V0", [P, G * P])[:], spare[6]]
        ty = sb("ty", [P, G * REL])
        sc = [sb(f"sc{h}", [P, G]) for h in range(2)]
        mt = sb("mt", [P, G])
        run = [sb(f"run{h}", [P, G + 1]) for h in range(2)]
        fac = [sb(f"fac{h}", [P, G]) for h in range(2)]
        fresh = far["d"][:].bitcast(F32)
        s_at = {n: sem("s_at_" + n) for n in ("st", "stc", "p", "mask", "v", "vt", "max", "me", "arg", "ex", "w", "agg",
                                              "fac", "own", "acc")}
        n_at = [0, 0]
        SL = 4
        ga4 = [[sem(f"s_gb{n}_{h}") for h in range(SL)] for n in range(2)]
        s_ix4 = [sem(f"s_iy{h}") for h in range(SL)]

        def need(eng, s, v):
            if not isinstance(v, int) or v > 0:
                eng.wait_ge(s, v)

        def schedule(eng, step, extra, enter=None, leave=None):
            for t in range(2):
                step(t, t % SL, t // SL)
            LOOPS = (TG - 2) // SL - 1
            with eng.Fori(0, LOOPS, 1) as i:
                if enter:
                    enter(i)
                for u in range(SL):
                    step(i * SL + (2 + u), (2 + u) % SL, i + (2 + u) // SL)
            if leave:
                leave(LOOPS)
            for t in range(2 + SL * LOOPS, TG + extra):
                step(t, t % SL, t // SL)

        def there(t, lo=0, hi=TG):
            return not isinstance(t, int) or lo <= t < hi

        def attention_pass(hop, tab, Pn):
            s_ga = ga4[hop]
            q = s_at
            b0, own0 = n_at
            ix0 = [hop * len(range(u, TG, SL)) for u in range(SL)]

            with nc.Block() as block:
                @block.gpsimd
                def _(pool):
                    def step(t, u, turn):
                        pool_wait(pool, s_ix4[u], ix0[u] + turn + 1)
                        for k in range(G):
                            pool.indirect_dma_start(M4[u][:, k * 96:(k + 1) * 96], None, tab[:, :],
                                                    bass.IndirectOffsetOnAxis(nidx[u][:, k:k + 1], 0)
                                                    ).then_inc(s_ga[u], 16)
                    schedule(pool, step, 0)
                    for u in range(SL):
                        pool.wait_ge(s_ga[u], 16 * G * len(range(u, TG, SL)))

                @block.scalar
                def _(act):
                    def stage(g, u):
                        need(act, q["w"], b0 + g - SL + 1 if not isinstance(g, int) or g >= SL else 0)
                        nc.scalar.copy(nidx[u][:], far["s"][:, bass.ds(g * G, G)]).then_inc(s_ix4[u], 1)

                    def step(t, u, turn):
                        v = (u + 3) % SL
                        w = (u + 1) % SL
                        if there(t + 1):
                            act.wait_ge(q["st"], b0 + t + 2)
                            nc.scalar.copy(ST4[w][:, 0:512], ps[0][:, 0:512]).then_inc(q["stc"], 1)
                            nc.scalar.copy(ST4[w][:, 512:G * P], ps[1][:, 0:G * P - 512]).then_inc(q["stc"], 1)
                            act.wait_ge(s_oh, n_g[0] + t + 2)
                            if there(t - 1):
                                act.wait_ge(q["vt"], b0 + t)
                            nc.scalar.activation(V[w % 2], S4[w], ACT.Copy, bias=-BIG,
                                                 scale=BIG).then_inc(q["mask"], 1)
                        if there(t - 1):
                            act.wait_ge(q["max"], b0 + t)
                            nc.scalar.activation(fac[v % 2][:], fac[v % 2][:], ACT.Exp).then_inc(q["fac"], 1)
                            act.wait_ge(q["arg"], b0 + t)
                            if there(t - 3):
                                act.wait_ge(s_grp, n_g[0] + t - 2)
                            Wv = M2[v % 2][:, 0:G * 65].rearrange("p (g w) -> p g w", w=65)
                            nc.scalar.activation(Wv[:, :, D], sc[v % 2][:], ACT.Exp).then_inc(q["ex"], 1)
                            act.wait_ge(q["ex"], b0 + t)
                            for k in range(G):
                                ins = nc.scalar.activation(Wv[:, k, 0:D], M4[v][:, k * 96:k * 96 + D], ACT.Copy,
                                                           scale=Wv[:, k, D:D + 1])
                            ins.then_inc(q["w"], 1)
                            if there(t + 3):
                                stage(t + 3, v)

                    def stage_first(act):
                        act.wait_ge(q["st"], b0 + 1)
                        nc.scalar.copy(ST4[0][:, 0:512], ps[0][:, 0:512]).then_inc(q["stc"], 1)
                        nc.scalar.copy(ST4[0][:, 512:G * P], ps[1][:, 0:G * P - 512]).then_inc(q["stc"], 1)
                        act.wait_ge(s_oh, n_g[0] + 1)
                        nc.scalar.activation(V[0], S4[0], ACT.Copy, bias=-BIG, scale=BIG).then_inc(q["mask"], 1)

                    for g in range(SL):
                        stage(g, g)
                    stage_first(act)
                    schedule(act, step, 1)

                @block.tensor
                def _(pe):
                    def turn_onehots(g, u):
                        pe.wait_ge(s_oh, n_g[0] + g + 1)
                        need(pe, q["stc"], 2 * (b0 + g))
                        for k in range(G):
                            last = nc.tensor.transpose(ps[k // 4][:, (k % 4) * P:(k % 4 + 1) * P],
                                                       S4[u][:, k * P:(k + 1) * P], ident[:])
                        last.then_inc(q["st"], 1)

                    def near_part(g, u):
                        blk = tile_blocks(mybir.EngineType.PE, "s", g)
                        pe.wait_ge(q["stc"], 2 * (b0 + g + 1))
                        if there(g - 2):
                            pe.wait_ge(q["v"], b0 + g - 1)
                        for k in range(G):
                            last = nc.tensor.matmul(ps[4 + u % 2][:, k * REL:(k + 1) * REL], ST4[u][:, k * P:(k + 1) * P],
                                                    Pn[:, bass.ds(blk[k], 1), 0:REL], start=True, stop=True)
                        last.then_inc(q["p"], 1)

                    def step(t, u, turn):
                        v, w = (u + 3) % SL, (u + 1) % SL
                        if there(t + 1):
                            turn_onehots(t + 1, w)
                        if there(t - 1):
                            pe.wait_ge(q["max"], b0 + t)
                            for k in range(G):
                                last = nc.tensor.matmul(ps[4 + v % 2][:, 256 + k:257 + k], ST4[v][:, k * P:(k + 1) * P],
                                                        run[v % 2][:, k + 1:k + 2], start=True, stop=True)
                            last.then_inc(q["me"], 1)
                        if there(t + 1):
                            near_part(t + 1, w)
                        if there(t):
                            pe.wait_ge(q["v"], b0 + t + 1)
                            for k in range(G):
                                last = nc.tensor.transpose(ps[2 + k // 4][:, (k % 4) * P:(k % 4 + 1) * P],
                                                           V[u % 2][:, k * P:(k + 1) * P], ident[:])
                            last.then_inc(q["vt"], 1)
                        if there(t - 1):
                            pe.wait_ge(q["w"], b0 + t)
                            if there(t - 3):
                                pe.wait_ge(q["acc"], b0 + t - 2)
                            for k in range(G):
                                last = nc.tensor.matmul(ps[6 + v % 2][:, k * 65:(k + 1) * 65],
                                                        S4[v][:, k * P:(k + 1) * P],
                                                        M2[v % 2][:, k * 65:(k + 1) * 65], start=True, stop=True)
                            last.then_inc(s_grp, 1)

                    turn_onehots(0, 0)
                    near_part(0, 0)
                    schedule(pe, step, 1)

                @block.vector
                def _(dve):
                    c = Chain(dve, q["own"])
                    c.n = own0

                    def onehot4(g, u):
                        if there(g - SL):
                            dve.wait_ge(s_grp, n_g[0] + g - SL + 1)
                            dve.wait_ge(q["mask"], b0 + g - SL + 1)
                        near = loc["s"][:, bass.ds(g * G, G)].unsqueeze(2).to_broadcast([P, G, P])
                        nc.vector.tensor_tensor(S4[u].rearrange("p (g n) -> p g n", g=G), iota_b, near,
                                                ALU.is_equal).then_inc(s_oh, 1)

                    def scores(g, u, turn):
                        Mv = M4[u].rearrange("p (g w) -> p g w", w=96)
                        tv = ty[:].rearrange("p (g r) -> p g r", r=REL)
                        uv = V2[:].rearrange("p (g r) -> p g r", r=REL)
                        one = [P, G, REL]
                        c.inc(nc.vector.tensor_tensor(tv, iota_n[:, 0:REL].unsqueeze(1).to_broadcast(one),
                                                      rel[:, bass.ds(g * G, G)].unsqueeze(2).to_broadcast(one),
                                                      ALU.is_equal))
                        dve.wait_ge(s_ga[u], 16 * G * (turn + 1))
                        dve.wait_ge(q["p"], b0 + g + 1)
                        c.link(nc.vector.tensor_tensor(uv, Mv[:, :, D:D + REL],
                                                       ps[4 + u % 2][:, 0:G * REL].rearrange("p (g r) -> p g r", r=REL),
                                                       ALU.add))
                        c.link(nc.vector.tensor_tensor(uv, uv, tv, ALU.mult))
                        s1 = sc[u % 2]
                        if there(g - 2):
                            dve.wait_ge(q["ex"], b0 + g - 1)
                        c.link(nc.vector.tensor_reduce(s1[:], uv, AX, ALU.add))
                        c.link(nc.vector.scalar_tensor_tensor(out=s1[:], in0=s1[:], scalar=0.2, in1=s1[:],
                                                              op0=ALU.mult, op1=ALU.max))
                        dve.wait_ge(q["mask"], b0 + g + 1)
                        Vv = V[u % 2].rearrange("p (g n) -> p g n", n=P)
                        nc.vector.tensor_tensor(Vv, Vv, s1[:].unsqueeze(2).to_broadcast([P, G, P]),
                                                ALU.add).then_inc(q["v"], 1)

                    def maxima(g, u):
                        new, old = run[u % 2], run[1 - u % 2]
                        dve.wait_ge(q["vt"], b0 + g + 1)
                        c.inc(nc.vector.tensor_copy(new[:, 0:1], old[:, G:G + 1]))
                        c.inc(nc.vector.tensor_reduce(mt[:, 0:4], ps[2][:, 0:512].rearrange("p (g n) -> p g n", n=P),
                                                      AX, ALU.max))
                        c.link(nc.vector.tensor_reduce(mt[:, 4:G], ps[3][:, 0:3 * P].rearrange("p (g n) -> p g n", n=P),
                                                       AX, ALU.max))
                        fr = fresh[:, bass.ds(g * G, G)]
                        c.link(nc.vector.tensor_tensor_scan(new[:, 1:G + 1], fr, mt[:], new[:, 0:1], ALU.add, ALU.max))
                        if there(g - 2):
                            dve.wait_ge(q["acc"], b0 + g - 1)
                        c.link(nc.vector.tensor_tensor(fac[u % 2][:], new[:, 0:G], fr, ALU.add))
                        nc.vector.tensor_tensor(fac[u % 2][:], fac[u % 2][:], new[:, 1:G + 1],
                                                ALU.subtract).then_inc(q["max"], 1)

                    def exponents(g, u):
                        s1 = sc[u % 2]
                        dve.wait_ge(q["me"], b0 + g + 1)
                        if there(g + 2):
                            dve.wait_ge(q["p"], b0 + g + 3)
                        c.link(nc.vector.tensor_tensor(s1[:], s1[:], ps[4 + u % 2][:, 256:256 + G],
                                                       ALU.subtract))
                        nc.vector.tensor_scalar(s1[:], s1[:], 0.0, None, ALU.min).then_inc(q["arg"], 1)

                    def accumulate(g, u):
                        blk = tile_blocks(mybir.EngineType.DVE, "s", g)
                        dve.wait_ge(q["fac"], b0 + g + 1)
                        dve.wait_ge(s_grp, n_g[0] + g + 1)
                        for k in range(G):
                            a = acc[:, bass.ds(blk[k], 1), :]
                            c.link(nc.vector.scalar_tensor_tensor(
                                out=a, in0=a, scalar=fac[u % 2][:, k:k + 1],
                                in1=ps[6 + u % 2][:, k * 65:(k + 1) * 65].unsqueeze(1), op0=ALU.mult, op1=ALU.add))
                        dve.sem_inc(q["acc"], 1)

                    def step(t, u, turn):
                        if there(t + 1):
                            onehot4(t + 1, (u + 1) % SL)
                        if there(t - 1):
                            maxima(t - 1, (u + 3) % SL)
                        if there(t):
                            scores(t, u, turn)
                        if there(t - 1):
                            exponents(t - 1, (u + 3) % SL)
                        if there(t - 2):
                            accumulate(t - 2, (u + 2) % SL)

                    steps = SL * (1 + 4 + 3 + 2 + 1 + G)
                    onehot4(0, 0)
                    schedule(dve, step, 2, lambda i: c.enter(i, steps), lambda n: c.leave(n))
                    n_at[1] = c.n
            n_g[0] += TG
            n_at[0] += TG

        V2 = sb("V2", [P, G * REL])
        with nc.Block() as block:
            @block.tensor
            def _(pe):
                nc.tensor.matmul(ps[0][0:D, 0:REL], wts["WT"][:, 0:D], wts["relT"][:], start=True, stop=True)
                nc.tensor.matmul(ps[0][0:D, REL:2 * REL], wts["WT"][:, D:2 * D], wts["relT"][:], start=True,
                                 stop=True).then_inc(s_pe, 1)

            @block.vector
            def _(dve):
                dve.wait_ge(s_pe, pen[0] + 1)
                nc.vector.tensor_copy(pq_w[:], ps[0][0:D, 0:2 * REL]).then_inc(s_v, 1)
                dve.wait_ge(s_v, vn[0] + 1)
        pen[0] += 1
        vn[0] += 1

        def l2_start(c):
            c.inc(nc.vector.tensor_copy(Y, X))
            c.inc(nc.vector.tensor_copy(H, X))
            row = nodes[4][0:1, 0:T]
            c.link(nc.vector.tensor_copy(row.rearrange("p (g w) -> p g w", w=G),
                                         tblk["s"].rearrange("p (g w) -> p g w", w=8)[:, :, 0:G]))
            c.link(nc.vector.tensor_tensor(nodes[4][0:1, T + 1:2 * T], row[:, 1:T], row[:, 0:T - 1], ALU.not_equal))
            c.link(nc.vector.memset(nodes[4][0:1, T:T + 1], 1.0))
        vector_steps(l2_start)
        with nc.Block() as block:
            CH = 476

            @block.tensor
            def _(pe):
                for n, k in enumerate(range(0, T, CH)):
                    w = min(CH, T - k)
                    nc.tensor.matmul(ps[n][:, 0:w], ones[0:1, :], nodes[4][0:1, T + k:T + k + w], start=True,
                                     stop=True).then_inc(s_pe, 1)

            @block.vector
            def _(dve):
                for n, k in enumerate(range(0, T, CH)):
                    w = min(CH, T - k)
                    dve.wait_ge(s_pe, pen[0] + n + 1)
                    nc.vector.tensor_scalar(fresh[:, k:k + w], ps[n][:, 0:w], -BIG, None, ALU.mult)
        pen[0] += 4
        for hop in range(2):
            node_linear(Y, None, None, pq_w[:], None, False, Z)
            t2 = table[2 + hop]
            store_table(t2, [(Y, 0, D), (Z[:, :, REL:2 * REL], D, D + REL)])

            def hop_start(c):
                clear_acc(c)
                c.link(nc.vector.memset(run[1][:], -BIG))
            vector_steps(hop_start)
            attention_pass(hop, t2, Z)

            def hop_sum(c):
                c.link(nc.vector.tensor_scalar(nv[0][:, :], acc[:, :, D], 1e-30, None, ALU.max))
                c.link(nc.vector.reciprocal(nv[0][:], nv[0][:]))
                c.link(nc.vector.tensor_tensor(Z, acc[:, :, 0:D], bc(nv[0]), ALU.mult))
                c.link(nc.vector.tensor_tensor(Y, Y, Z, ALU.add))
            vector_steps(hop_sum)
            l2norm(Y, Z, Y)
            vector_steps(lambda c: c.link(nc.vector.scalar_tensor_tensor(out=H, in0=H, scalar=0.5, in1=Y, op0=ALU.mult,
                                                                         op1=ALU.add)))
        with nc.Block() as block:
            @block.sync
            def _(sp):
                sp.dma_start(X, table[2].rearrange("(p b) w -> p b w", p=P)[:, :, 0:D]).then_inc(s_dma, 16)
                sp.wait_ge(s_dma, dma_n[0] + 16)
        dma_n[0] += 16
        vector_steps(lambda c: c.link(nc.vector.tensor_tensor(Y, X, H, ALU.add)))
        layernorm(Y, H, X)

        EW = G * (2 + EA)
        eb = [M[0][:, h * EW:(h + 1) * EW] for h in range(2)]
        eT, hT, uc = V[0], ST[1][0:D + 1, :], M[1][:, 0:G * D]
        q3 = {n: sem("s_m_" + n) for n in ("eb", "eb1", "st", "stc", "uc", "h", "hc", "m", "mc")}
        s_eb = [q3["eb"], q3["eb1"]]

        def edge_mlp_pass(U):
            q = q3
            rv = rec_d.rearrange("(p t) w -> p (t w)", p=P)
            WR = 2 + EA
            with nc.Block() as block:
                @block.sync
                def _(sp):
                    def load(i, h, first):
                        g = 2 * i + h
                        if not first:
                            sp.wait_ge(q["st"], g - 1)
                        sp.dma_start(eb[h], rv[:, bass.ds(g * (G * WR), G * WR)]).then_inc(s_eb[h], 16)
                    for h in range(2):
                        load(0, h, True)
                    with sp.Fori(1, R, 1) as i:
                        for h in range(2):
                            load(i, h, False)

                @block.vector
                def _(dve):
                    onehot(dve, "d", 0, 0, True)
                    onehot(dve, "d", 0, 1, True)
                    add_tiles(dve, "d", 0, 0, ps[7])
                    with dve.Fori(1, R, 1) as i:
                        onehot(dve, "d", i, 0, False)
                        add_tiles(dve, "d", i - 1, 1, ps[7])
                        onehot(dve, "d", i, 1, False)
                        add_tiles(dve, "d", i, 0, ps[7])
                    add_tiles(dve, "d", R - 1, 1, ps[7])

                @block.scalar
                def _(act):
                    def group(i, h, first):
                        g = 2 * i + h
                        blk = tile_blocks(mybir.EngineType.Activation, "d", g)
                        if not first:
                            act.wait_ge(q["h"], g)
                        for k in range(G):
                            nc.scalar.copy(uc[:, k * D:(k + 1) * D].unsqueeze(1),
                                           U[:, bass.ds(blk[k], 1), :]).then_inc(q["uc"], 1)
                        act.wait_ge(q["st"], g + 1)
                        nc.scalar.copy(ST[0][:, 0:512], ps[0][:, 0:512]).then_inc(q["stc"], 1)
                        nc.scalar.copy(ST[0][:, 512:G * P], ps[1][:, 0:G * P - 512]).then_inc(q["stc"], 1)
                        nc.scalar.copy(eT[0:EA, 0:512], ps[2][0:EA, 0:512]).then_inc(q["stc"], 1)
                        nc.scalar.copy(eT[0:EA, 512:G * P], ps[3][0:EA, 0:G * P - 512]).then_inc(q["stc"], 1)
                        act.wait_ge(q["h"], g + 1)
                        if not first:
                            act.wait_ge(q["m"], g)
                        nc.scalar.activation(hT[0:D, 0:512], ps[4][0:D, 0:512], ACT.Relu).then_inc(q["hc"], 1)
                        nc.scalar.activation(hT[0:D, 512:G * P], ps[5][0:D, 0:G * P - 512], ACT.Relu).then_inc(q["hc"], 1)
                        act.wait_ge(q["m"], g + 1)
                        if not first:
                            act.wait_ge(s_grp, n_g[0] + g)
                        nc.scalar.activation(M2[0][:, 0:G * 65].rearrange("p (g w) -> p g w", w=65)[:, :, 0:D],
                                             ps[6][:, 0:G * D].rearrange("p (g w) -> p g w", w=D),
                                             ACT.Relu).then_inc(q["mc"], 1)
                    group(0, 0, True)
                    group(0, 1, False)
                    with act.Fori(1, R, 1) as i:
                        for h in range(2):
                            group(i, h, False)

                @block.tensor
                def _(pe):
                    def group(i, h, first):
                        g = 2 * i + h
                        pe.wait_ge(s_oh, n_g[0] + g + 1)
                        pe.wait_ge(s_eb[h], 16 * (i + 1))
                        if not first:
                            pe.wait_ge(q["stc"], 4 * g)
                        for k in range(G):
                            nc.tensor.transpose(ps[k // 4][:, (k % 4) * P:(k % 4 + 1) * P],
                                                S[h][:, k * P:(k + 1) * P], ident[:])
                        for k in range(G):
                            last = nc.tensor.transpose(ps[2 + k // 4][0:EA, (k % 4) * P:(k % 4 + 1) * P],
                                                       eb[h][:, k * WR + 2:(k + 1) * WR], ident[:])
                        last.then_inc(q["st"], 1)
                        pe.wait_ge(q["stc"], 4 * (g + 1))
                        pe.wait_ge(q["uc"], G * (g + 1))
                        if not first:
                            pe.wait_ge(q["hc"], 2 * g)
                        for k in range(G):
                            o_ap = ps[4 + k // 4][0:D, (k % 4) * P:(k % 4 + 1) * P]
                            nc.tensor.matmul(o_ap, uc[:, k * D:(k + 1) * D], ST[0][:, k * P:(k + 1) * P],
                                             start=True, stop=False)
                            last = nc.tensor.matmul(o_ap, wts["w3b"][:], eT[0:EA, k * P:(k + 1) * P],
                                                    start=False, stop=True)
                        last.then_inc(q["h"], 1)
                        pe.wait_ge(q["hc"], 2 * (g + 1))
                        if not first:
                            pe.wait_ge(q["mc"], g)
                        for k in range(G):
                            last = nc.tensor.matmul(ps[6][:, k * D:(k + 1) * D], hT[:, k * P:(k + 1) * P],
                                                    wts["w3c"][:], start=True, stop=True)
                        last.then_inc(q["m"], 1)
                        pe.wait_ge(q["mc"], g + 1)
                        if not first:
                            pe.wait_ge(s_acc, n_acc[0] + g)
                        for k in range(G):
                            last = nc.tensor.matmul(ps[7][:, k * 65:(k + 1) * 65], S[h][:, k * P:(k + 1) * P],
                                                    M2[0][:, k * 65:(k + 1) * 65], start=True, stop=True)
                        last.then_inc(s_grp, 1)
                    group(0, 0, True)
                    group(0, 1, False)
                    with pe.Fori(1, R, 1) as i:
                        for h in range(2):
                            group(i, h, False)
            n_g[0] += TG

        node_linear(X, None, None, wts["w3a"][:], bias["b3a"][:], False, Z)

        def l3_start(c):
            clear_acc(c)
            c.inc(nc.vector.memset(hT[D:D + 1, :], 1.0))
            c.inc(nc.vector.memset(M2[0][:, 0:G * 65].rearrange("p (g w) -> p g w", w=65)[:, :, D], 1.0))
        vector_steps(l3_start)
        edge_mlp_pass(Z)

        def l3_end(c):
            c.link(nc.vector.tensor_tensor(Y, acc[:, :, 0:D], bc(rcnt), ALU.mult))
            c.link(nc.vector.scalar_tensor_tensor(out=Y, in0=X, scalar=2.0, in1=Y, op0=ALU.mult, op1=ALU.add))
        vector_steps(l3_end)
        layernorm(Y, H, X)

        with nc.Block() as block:
            @block.sync
            def _(sp):
                sp.dma_start(out[0:97 * P, :].rearrange("(b p) w -> p b w", p=P), X[:, 0:97, :]).then_inc(s_dma, 16)
                sp.dma_start(out[97 * P:NODES, :], X[0:NODES - 97 * P, 97, :]).then_inc(s_dma, 16)
                sp.wait_ge(s_dma, dma_n[0] + 32)


def kernel(**inputs):
    import numpy as np
    import concourse.bacc as bacc
    from concourse.bass_utils import run_bass_kernel_spmd as run

    def pad(a, n, v):
        a = np.ascontiguousarray(a)
        return np.concatenate([a, np.full((n - a.shape[0],) + a.shape[1:], v, a.dtype)])

    nc = bacc.Bacc("TRN2", target_bir_lowering=False, num_devices=1)
    E = P * J
    arrays = {
        "x": pad(inputs["x"], ROWS, 0),
        "src": pad(inputs["src"], E, PAD_NODE).reshape(P, J),
        "dst": pad(inputs["dst"], E, PAD_NODE).reshape(P, J),
        "typ": pad(inputs["edge_type_32"], E, 0).reshape(P, J),
        "ea": pad(inputs["edge_attr_32"], E, 0),
        "w0a": np.concatenate([np.asarray(inputs["L0_gnn_W1_l"]).T, np.asarray(inputs["L0_gnn_W1_r"]).T]),
        "w0b": np.concatenate([np.asarray(inputs["L0_gnn_W2_l"]).T, np.asarray(inputs["L0_gnn_W2_r"]).T]),
        "b0a": np.ascontiguousarray(inputs["L0_gnn_b1"]),
        "b0b": np.ascontiguousarray(inputs["L0_gnn_b2"]),
        "relT": np.ascontiguousarray(np.asarray(inputs["L2_gnn_relation_emb"]).T),
        "WT": np.ascontiguousarray(np.asarray(inputs["L2_gnn_W"]).T),
        "w3a": np.ascontiguousarray(np.asarray(inputs["L3_gnn_W1"])[0:D]),
        "w3b": np.ascontiguousarray(np.asarray(inputs["L3_gnn_W1"])[D:]),
        "b3a": np.ascontiguousarray(inputs["L3_gnn_b1"]),
        "w3c": np.concatenate([np.asarray(inputs["L3_gnn_W2"]), np.asarray(inputs["L3_gnn_b2"])[None]]),
    }
    args, feed = {}, {}
    for name, a in arrays.items():
        feed[f"in_{name}"] = a
        args[name] = nc.dram_tensor(f"in_{name}", a.shape, mybir.dt.from_np(a.dtype), kind="ExternalInput").ap()
    out = nc.dram_tensor("out_x", (NODES, D), F32, kind="ExternalOutput").ap()
    build(nc, args, out, None)
    r = run(nc, [feed], core_ids=[0])
    return r.results[0]["out_x"]
```

```python
from contextlib import ExitStack

import concourse.bass as bass
from concourse import mybir

ALU = mybir.AluOpType
ACT = mybir.ActivationFunctionType
AX = mybir.AxisListType.X
F32 = mybir.dt.float32
I32 = mybir.dt.int32
BF16 = mybir.dt.bfloat16

P = 128
NODES = 12500
EDGES = 200000
D = 64
EA = 32
REL = 32
NB = 100
ROWS = P * NB
PAD_NODE = 98 * P
G = 7
J = 1568
JG = J // G
T = (P * J + 99 * (P - 1)) // P
TG = T // G
PAIRS = NB // 2
UP = 5
PACK_BITS = 12
PACK = 1 << PACK_BITS
BIG = 1.0e30
EPS_LN = 1e-5
EPS_L2 = 1e-12
assert T == 1666 and T % (2 * G) == 0 and J % (2 * G) == 0
assert J < PACK and J * (PACK + 1) < 1 << 24 and PAIRS % UP == 0


class Chain:

    def __init__(self, eng, sem):
        self.eng, self.sem, self.n, self.loop = eng, sem, 0, 0

    def inc(self, ins):
        ins.then_inc(self.sem, 1)
        self.n += 1
        return self.n

    def wait_for(self, n):
        self.eng.wait_ge(self.sem, self.loop + n)

    def wait(self):
        self.eng.wait_ge(self.sem, self.loop + self.n)

    def link(self, ins):
        self.inc(ins)
        self.wait()

    def enter(self, i, steps):
        self.loop, self.steps, self.at = i * steps, steps, self.n

    def leave(self, trips):
        assert self.n - self.at == self.steps, (self.n - self.at, self.steps)
        self.loop = 0
        self.n = self.at + self.steps * trips


def build(nc, A, out):
    with ExitStack() as ctx:
        def sb(name, shape, dt=F32):
            return ctx.enter_context(nc.sbuf_tensor(name, shape, dt))

        def sem(name):
            return ctx.enter_context(nc.semaphore(name))

        def dram(name, shape, dt=F32):
            return nc.dram_tensor(name, shape, dt, kind="Internal").ap()

        NA = NB * D
        nodes12 = sb("nodes12", [P, 2 * NA])
        nodes = [sb("nodes0", [P, NA]), nodes12[:, 0:NA], nodes12[:, NA:2 * NA], sb("nodes3", [P, NB * (D + 1)]),
                 sb("nodes4", [P, NA])]
        far = {o: sb(f"far_{o}", [P, T], I32) for o in "ds"}
        loc = {o: sb(f"loc_{o}", [P, T], BF16) for o in "ds"}
        rel = sb("rel", [P, T])
        tblk_sb = sb("tblk", [33, TG * 8], I32)
        tblk = {"d": tblk_sb[0:1, :], "s": tblk_sb[32:33, :]}
        ident = sb("ident", [P, P])
        ident16 = sb("ident16", [P, P], BF16)
        before = sb("before", [P, P])
        ones = sb("ones", [P, P])
        iota_n = sb("iota_n", [P, P])
        iota16 = sb("iota16", [P, P], BF16)
        small = sb("small", [P, 8])
        cnt = sb("cnt", [P, NB])
        base = sb("base", [P, NB])
        counts2 = sb("counts2", [P, PAIRS])
        pair_no = sb("pair_no", [P, UP])
        S = [sb(f"S{h}", [P, G * P]) for h in range(2)]
        ST = [sb(f"ST{h}", [P, G * P]) for h in range(2)]
        M = [sb(f"M{h}", [P, G * 96]) for h in range(2)]
        GP = G * P
        ST16 = [ST[k // 2][:].bitcast(BF16)[:, (k % 2) * GP:(k % 2 + 1) * GP] for k in range(4)]

        def slots(array):
            s16 = [array[:, 2 * GP:4 * GP].bitcast(BF16)[:, k * GP:(k + 1) * GP] for k in range(4)]
            return [S[0][:], S[1][:], array[:, 0:GP], array[:, GP:2 * GP]], s16, array[:, 4 * GP:NA]
        M2 = [sb(f"M2{h}", [P, G * 65]) for h in range(2)]
        nidx = [sb(f"nidx{h}", [P, G], I32) for h in range(4)]
        ps = [ctx.enter_context(nc.psum_tensor(f"ps{i}", [P, 512], F32)) for i in range(8)]

        rec_d = dram("rec_d", [P * T, 2 + EA])
        rec_s = dram("rec_s", [P * T, 3])
        table = [dram(f"table{i}", [ROWS, 96 if i >= 2 else D]) for i in range(4)]

        s_const = sem("s_const")
        s_dma = sem("s_dma")
        dma_n = [0]
        s_load = sem("s_load")
        load_n = [0]
        s_v = sem("s_v")
        vn = [0]
        s_nop = sem("s_nop")
        s_scat = [sem(f"s_scat{h}") for h in range(2)]
        s_st = [sem(f"s_st{h}") for h in range(2)]
        s_ea = [sem(f"s_ea{h}") for h in range(2)]
        s_rd = [sem(f"s_rd{h}") for h in range(2)]
        s_cp = [sem(f"s_cp{h}") for h in range(2)]
        s_ac = [sem(f"s_ac{h}") for h in range(2)]
        s_pe = sem("s_pe")
        pen = [0]
        n_sort = {"ac": 0, "scat": 0, "st": 0, "ea": 0}

        def pool_wait(pool, s, v):
            pool.wait_ge(s, v)
            pool.sem_inc(s_nop, 1)

        with nc.Block() as block:
            @block.gpsimd
            def _(pool):
                nc.gpsimd.iota(iota_n[:], pattern=[[1, P]], base=0, channel_multiplier=0,
                               allow_small_or_imprecise_dtypes=True).then_inc(s_const, 1)
                nc.gpsimd.memset(ident[:], 0.0).then_inc(s_const, 1)
                nc.gpsimd.memset(before[:], 0.0).then_inc(s_const, 1)
                nc.gpsimd.memset(ones[:], 1.0).then_inc(s_const, 1)
                pool.wait_ge(s_const, 4)
                nc.gpsimd.affine_select(out=ident[:], in_=ident[:], compare_op=ALU.not_equal, fill=1.0,
                                        base=0, pattern=[[-1, P]], channel_multiplier=1).then_inc(s_const, 1)
                nc.gpsimd.affine_select(out=before[:], in_=before[:], compare_op=ALU.is_ge, fill=1.0,
                                        base=0, pattern=[[-1, P]], channel_multiplier=1).then_inc(s_const, 1)
                pool.wait_ge(s_const, 6)
                nc.gpsimd.memset(tblk_sb[:], 0).then_inc(s_const, 1)
                pool.wait_ge(s_const, 7)

        width = {"d": 2 + EA, "s": 3}
        pay_width = {"d": 2, "s": 3}
        recs = {"d": rec_d, "s": rec_s}

        def view(a, k):
            return nodes[a][:, k * J:(k + 1) * J]
        slot_row = {"d": view(4, 0).bitcast(I32), "s": view(2, 0).bitcast(I32)}
        pay_at = {"d": nodes[4][:, J:3 * J], "s": nodes[3][:, 0:3 * J]}

        def rank(o):
            W, PW, rec = width[o], pay_width[o], recs[o]
            near_in, far_in = (A["dst"], A["src"]) if o == "d" else (A["src"], A["dst"])
            nearI, farI, relI = view(0, 0).bitcast(I32), view(0, 1).bitcast(I32), view(0, 2).bitcast(I32)
            pair, mask, scan, pos = view(1, 0), view(1, 1), view(1, 2), view(1, 3)
            weight, first, odd = view(0, 0), view(0, 1), view(0, 2)
            packed, low, high, step_up = (S[1][:, 64 * k:64 * k + PAIRS] for k in range(4))
            posI, tmpI = slot_row[o], view(2, 1).bitcast(I32)
            pay = pay_at[o].rearrange("p (j w) -> p j w", w=PW)
            payI = pay_at[o].bitcast(I32).rearrange("p (j w) -> p j w", w=PW)
            iota_t = cmp = nodes[2][:, 2 * J:2 * J + T]
            FG = 6
            fill = nodes[3][:, 3 * J:3 * J + FG * G * W]
            fills = len(range(0, TG, FG))
            zero = small[:, 0:1]
            d0, l0, v0, p0 = dma_n[0], load_n[0], vn[0], pen[0]
            nload = 3 if o == "s" else 2
            after = {}

            def sync(sp):
                sp.dma_start(nearI, near_in).then_inc(s_load, 16)
                sp.dma_start(farI, far_in).then_inc(s_load, 16)
                if o == "s":
                    sp.dma_start(relI, A["typ"]).then_inc(s_load, 16)
                sp.wait_ge(s_v, v0 + 2)
                rv = rec.rearrange("(p t) w -> p (t w)", p=P)
                for k in range(0, TG, FG):
                    w = min(FG, TG - k) * G * W
                    sp.dma_start(rv[:, k * G * W:k * G * W + w], fill[:, 0:w]).then_inc(s_dma, 16)
                sp.wait_ge(s_dma, d0 + 16 * fills)

            def pool(pl):
                pl.wait_ge(s_v, v0 + 1)
                nc.gpsimd.iota(iota_t, pattern=[[1, T]], base=0, channel_multiplier=0,
                               allow_small_or_imprecise_dtypes=True).then_inc(s_pe, 1)

            def vector(dve):
                c = Chain(dve, s_v)
                c.n = v0
                c.link(nc.vector.memset(fill, 0.0))
                c.link(nc.vector.memset(fill.rearrange("p (t w) -> p t w", w=W)[:, :, 1], -1.0))
                dve.wait_ge(s_load, l0 + 16 * nload)
                c.inc(nc.vector.tensor_scalar(tmpI, nearI, P - 1, None, ALU.bitwise_and))
                c.link(nc.vector.tensor_scalar(posI, nearI, 7, None, ALU.logical_shift_right))
                c.inc(nc.vector.tensor_copy(pay[:, :, 1], tmpI))
                if o == "s":
                    c.inc(nc.vector.tensor_copy(pay[:, :, 2], relI))
                c.wait()
                c.inc(nc.vector.tensor_scalar(nearI, posI, 1, None, ALU.bitwise_and))
                c.link(nc.vector.tensor_scalar(tmpI, posI, 1, None, ALU.logical_shift_right))
                c.inc(nc.vector.tensor_copy(odd, nearI))
                c.link(nc.vector.tensor_copy(pair, tmpI))
                c.inc(nc.vector.tensor_scalar(weight, odd, PACK - 1.0, 1.0, ALU.mult, ALU.add))
                c.inc(nc.vector.tensor_scalar(tmpI, farI, P - 1, None, ALU.bitwise_and))
                c.link(nc.vector.tensor_scalar(posI, farI, 7, None, ALU.logical_shift_right))
                c.inc(nc.vector.tensor_copy(scan, tmpI))
                c.link(nc.vector.tensor_copy(mask, posI))
                c.link(nc.vector.scalar_tensor_tensor(out=scan, in0=scan, scalar=float(NB), in1=mask,
                                                      op0=ALU.mult, op1=ALU.add))
                c.link(nc.vector.tensor_copy(payI[:, :, 0], scan))
                c.inc(nc.vector.memset(pos, 0.0))
                c.inc(nc.vector.memset(zero, 0.0))
                c.link(nc.vector.tensor_copy(pair_no[:], iota_n[:, 0:UP]))
                with dve.Fori(0, PAIRS // UP, 1) as i:
                    c.enter(i, 5 * UP + 1)
                    for j in range(UP):
                        number = pair_no[:, j:j + 1]
                        c.link(nc.vector.scalar_tensor_tensor(out=mask, in0=pair, scalar=number, in1=weight,
                                                              op0=ALU.is_equal, op1=ALU.mult))
                        c.link(nc.vector.tensor_tensor_scan(scan, ones[:, 0:1].to_broadcast([P, J]), mask, zero,
                                                            ALU.mult, ALU.add))
                        c.inc(nc.vector.tensor_scalar(counts2[:, bass.ds(i * UP + j, 1)], scan[:, J - 1:J], 0.0, None,
                                                      ALU.add))
                        c.link(nc.vector.scalar_tensor_tensor(out=mask, in0=pair, scalar=number, in1=scan,
                                                              op0=ALU.is_equal, op1=ALU.mult))
                        c.link(nc.vector.tensor_tensor(pos, pos, mask, ALU.add))
                    c.link(nc.vector.tensor_scalar(pair_no[:], pair_no[:], float(UP), None, ALU.add))
                c.leave(PAIRS // UP)
                c.link(nc.vector.tensor_copy(packed.bitcast(I32), counts2[:]))
                c.inc(nc.vector.tensor_scalar(low.bitcast(I32), packed.bitcast(I32), PACK - 1, None, ALU.bitwise_and))
                c.link(nc.vector.tensor_scalar(high.bitcast(I32), packed.bitcast(I32), PACK_BITS, None,
                                               ALU.logical_shift_right))
                cnt2 = cnt[:].rearrange("p (q t) -> p q t", t=2)
                c.inc(nc.vector.tensor_copy(cnt2[:, :, 0], low.bitcast(I32)))
                c.link(nc.vector.tensor_copy(cnt2[:, :, 1], high.bitcast(I32)))
                after["cnt"] = c.n
                dve.wait_ge(s_pe, p0 + 2)
                totI = small[0:NB, 2:3].bitcast(I32)
                c.link(nc.vector.tensor_scalar(totI, ps[0][0:NB, 0:1], float(P - 1), None, ALU.add))
                c.link(nc.vector.tensor_scalar(totI, totI, 7, None, ALU.logical_shift_right))
                c.link(nc.vector.tensor_copy(small[0:NB, 3:4], totI))
                after["tiles"] = c.n
                dve.wait_ge(s_pe, p0 + 3)
                c.link(nc.vector.tensor_copy(small[0:NB, 4:5], ps[1][0:NB, 0:1]))
                c.inc(nc.vector.tensor_scalar(cmp[0:NB, :], iota_t[0:NB, :], small[0:NB, 4:5], None, ALU.is_ge))
                c.link(nc.vector.tensor_scalar(S[0][0:NB, 0:NB], ident[0:NB, 0:NB], small[0:NB, 4:5], float(P),
                                               ALU.mult, ALU.mult))
                after["diag"] = c.n
                dve.wait_ge(s_pe, p0 + 4)
                c.inc(nc.vector.tensor_scalar(base[:], ps[2][:, 0:NB], -1.0, None, ALU.add))
                for q in range(7):
                    row = tblk[o].rearrange("p (g w) -> p g w", w=8)[:, 34 * q:34 * q + 34, 0:G]
                    src = ps[3 + q // 2][0:1, (q % 2) * 256:(q % 2) * 256 + 238].rearrange("p (g w) -> p g w", w=G)
                    c.inc(nc.vector.tensor_scalar(row, src, -1.0, None, ALU.add))
                c.link(nc.vector.tensor_copy(posI, pos))
                c.inc(nc.vector.tensor_scalar(tmpI, posI, PACK - 1, None, ALU.bitwise_and))
                c.link(nc.vector.tensor_scalar(posI, posI, PACK_BITS, None, ALU.logical_shift_right))
                c.inc(nc.vector.tensor_copy(scan, tmpI))
                c.link(nc.vector.tensor_copy(mask, posI))
                c.link(nc.vector.tensor_tensor(mask, mask, scan, ALU.subtract))
                c.link(nc.vector.tensor_tensor(mask, mask, odd, ALU.mult))
                c.inc(nc.vector.tensor_tensor(pos, scan, mask, ALU.add))
                base2 = base[:].rearrange("p (q t) -> p q t", t=2)
                c.inc(nc.vector.tensor_tensor(step_up, base2[:, :, 1], base2[:, :, 0], ALU.subtract))
                c.inc(nc.vector.tensor_copy(low, base2[:, :, 0]))
                c.link(nc.vector.tensor_copy(pair_no[:], iota_n[:, 0:UP]))
                with dve.Fori(0, PAIRS // UP, 1) as i:
                    c.enter(i, 3 * UP + 1)
                    for j in range(UP):
                        q = bass.ds(i * UP + j, 1)
                        c.link(nc.vector.tensor_scalar(first, odd, step_up[:, q], low[:, q], ALU.mult, ALU.add))
                        c.link(nc.vector.scalar_tensor_tensor(out=mask, in0=pair, scalar=pair_no[:, j:j + 1], in1=first,
                                                              op0=ALU.is_equal, op1=ALU.mult))
                        c.link(nc.vector.tensor_tensor(pos, pos, mask, ALU.add))
                    c.link(nc.vector.tensor_scalar(pair_no[:], pair_no[:], float(UP), None, ALU.add))
                c.leave(PAIRS // UP)
                c.link(nc.vector.tensor_copy(posI, pos))
                c.inc(nc.vector.tensor_scalar(tmpI, posI, 7, None, ALU.logical_shift_right))
                c.link(nc.vector.tensor_scalar(posI, posI, P - 1, None, ALU.bitwise_and))
                c.inc(nc.vector.tensor_copy(scan, tmpI))
                c.link(nc.vector.tensor_copy(mask, posI))
                c.link(nc.vector.scalar_tensor_tensor(out=scan, in0=mask, scalar=float(T), in1=scan,
                                                      op0=ALU.mult, op1=ALU.add))
                c.link(nc.vector.tensor_copy(posI, scan))
                vn[0] = c.n

            def tensor(pe):
                pe.wait_ge(s_pe, p0 + 1)
                pe.wait_ge(s_v, after["cnt"])
                nc.tensor.matmul(ps[0][0:NB, 0:1], cnt[:], ones[:, 0:1], start=True, stop=True).then_inc(s_pe, 1)
                pe.wait_ge(s_v, after["tiles"])
                nc.tensor.matmul(ps[1][0:NB, 0:1], before[0:NB, 0:NB], small[0:NB, 3:4], start=True,
                                 stop=True).then_inc(s_pe, 1)
                pe.wait_ge(s_v, after["diag"])
                nc.tensor.matmul(ps[2][:, 0:NB], ones[0:NB, :], S[0][0:NB, 0:NB], start=True, stop=False)
                nc.tensor.matmul(ps[2][:, 0:NB], before[:], cnt[:], start=False, stop=True)
                for q in range(7):
                    last = nc.tensor.matmul(ps[3 + q // 2][0:1, (q % 2) * 256:(q % 2) * 256 + 238],
                                            ones[0:NB, 0:1], cmp[0:NB, 238 * q:238 * q + 238],
                                            start=True, stop=True)
                last.then_inc(s_pe, 1)

            dma_n[0] += 16 * fills
            load_n[0] += 16 * nload
            pen[0] += 4
            return sync, pool, vector, tensor

        def scatter(o):
            W, PW, rec = width[o], pay_width[o], recs[o]
            posI = slot_row[o]
            pay = pay_at[o].rearrange("p (j w) -> p j w", w=PW)
            stage = [M2[h][:, 0:G * W].rearrange("p (g w) -> p g w", w=W) for h in range(2)]
            eabuf = [M[h][:, 0:G * EA].rearrange("p (g w) -> p g w", w=EA) for h in range(2)]
            st0, sc0, ea0, ac0 = n_sort["st"], n_sort["scat"], n_sort["ea"], n_sort["ac"]
            TR = JG // 2
            NC = 3 if o == "d" else 2

            def sync(sp):
                ea_v = A["ea"].rearrange("(p j) w -> p (j w)", p=P)

                def load(i, h, first):
                    if not first:
                        sp.wait_ge(s_st[h], st0 + i)
                    sp.dma_start(M[h][:, 0:G * EA], ea_v[:, bass.ds((2 * i + h) * (G * EA), G * EA)]
                                 ).then_inc(s_ea[h], 16)

                for h in range(2):
                    load(0, h, True)
                with sp.Fori(1, TR, 1) as i:
                    for h in range(2):
                        load(i, h, False)

            def scalar(act):
                def stage_group(i, h, first):
                    if not first:
                        act.wait_ge(s_scat[h], sc0 + i * (16 * G))
                    g = 2 * i + h
                    nc.scalar.copy(nidx[h][:], posI[:, bass.ds(g * G, G)]).then_inc(s_ac[h], 1)
                    nc.scalar.copy(stage[h][:, :, 0:PW], pay[:, bass.ds(g * G, G), :]).then_inc(s_ac[h], 1)
                    if o == "d":
                        act.wait_ge(s_ea[h], ea0 + 16 * i + 16)
                        nc.scalar.copy(stage[h][:, :, 2:W], eabuf[h]).then_inc(s_ac[h], 1)
                    act.wait_ge(s_ac[h], ac0 + NC * i + NC)
                    act.sem_inc(s_st[h], 1)

                for h in range(2):
                    stage_group(0, h, True)
                with act.Fori(1, TR, 1) as i:
                    for h in range(2):
                        stage_group(i, h, False)

            def pool(pl):
                with pl.Fori(0, TR, 1) as i:
                    for h in range(2):
                        pool_wait(pl, s_st[h], st0 + i + 1)
                        for k in range(G):
                            pl.indirect_dma_start(rec[:, :], bass.IndirectOffsetOnAxis(nidx[h][:, k:k + 1], 0),
                                                  stage[h][:, k, :], None).then_inc(s_scat[h], 16)
                for h in range(2):
                    pl.wait_ge(s_scat[h], sc0 + 16 * G * TR)

            n_sort["st"] += TR
            n_sort["scat"] += 16 * G * TR
            n_sort["ea"] += 16 * TR if o == "d" else 0
            n_sort["ac"] += NC * TR
            return sync, scalar, pool

        def readback_d():
            W, CT = width["d"], 49
            trips = T // CT // 2
            buf = [nodes[1][:, h * CT * W:(h + 1) * CT * W] for h in range(2)]
            rv = rec_d.rearrange("(p t) w -> p (t w)", p=P)

            def sync(sp):
                def load(i, h, first):
                    if not first:
                        sp.wait_ge(s_cp[h], i * 2)
                    sp.dma_start(buf[h], rv[:, bass.ds((2 * i + h) * (CT * W), CT * W)]).then_inc(s_rd[h], 16)
                for h in range(2):
                    load(0, h, True)
                with sp.Fori(1, trips, 1) as i:
                    for h in range(2):
                        load(i, h, False)

            def vector(dve):
                with dve.Fori(0, trips, 1) as i:
                    for h in range(2):
                        dve.wait_ge(s_rd[h], 16 * i + 16)
                        col = bass.ds((2 * i + h) * CT, CT)
                        records = buf[h].rearrange("p (t w) -> p t w", w=W)
                        rows = buf[h].bitcast(I32).rearrange("p (t w) -> p t w", w=W)[:, :, 0]
                        nc.vector.tensor_copy(far["d"][:, col], rows).then_inc(s_cp[h], 1)
                        nc.vector.tensor_copy(loc["d"][:, col], records[:, :, 1]).then_inc(s_cp[h], 1)
            return sync, vector

        acc = nodes[3][:, 0:NB * (D + 1)].rearrange("p (b w) -> p b w", w=D + 1)
        X, H, Y, Z = (nodes[i][:, 0:NA].rearrange("p (b w) -> p b w", w=D) for i in (0, 1, 2, 4))

        work = sb("work", [P, 2 * 8 * (D + 1)])
        ct = [S[h][:, 0:4 * P].rearrange("p (b w) -> p b w", w=P) for h in range(2)]
        ctT = [ST[h][:, 0:4 * P] for h in range(2)]
        wts = {n: sb(f"w_{n}", list(A[n].shape)) for n in ("w0a", "w0b", "w3a", "w3c", "WT", "relT")}
        bias = {n: sb(f"b_{n}", [P, D]) for n in ("b0a", "b0b", "b3a")}
        pq_w = sb("pq_w", [D, 2 * REL])
        rcnt = cnt
        nv = [sb(f"nv{i}", [P, NB]) for i in range(3)]
        dinv = sb("dinv", [P, NB])
        s_lc, s_lt, s_la, s_lm, s_lo = (sem(n) for n in ("s_lc", "s_lt", "s_la", "s_lm", "s_lo"))
        lin_n, lin_c = [0], [0]

        def node_linear(inA, scale, inB, w, bias_ap, relu, dst):
            K = P if inB is not None else D
            halves = 1 if inB is None else 2
            n0, c0 = lin_n[0], lin_c[0]
            R = NB // 4

            def exists(i):
                return not isinstance(i, int) or 0 <= i < R

            def pieces(eng, step):
                for i in range(2):
                    step(i, i)
                with eng.Fori(1, R // 2 - 1, 1) as r:
                    for h in range(2):
                        step(2 * r + h, h)
                for i in range(R - 3, R):
                    step(i, i % 2)

            with nc.Block() as block:
                @block.vector
                def _(dve):
                    def inputs(i, h):
                        if exists(i - 2):
                            dve.wait_ge(s_lt, n0 + i - 1)
                        b4 = bass.ds(i * 4, 4)
                        if scale is None:
                            a = nc.vector.tensor_copy(ct[h][:, :, 0:D], inA[:, b4, 0:D])
                        else:
                            a = nc.vector.tensor_tensor(ct[h][:, :, 0:D], inA[:, b4, 0:D],
                                                        scale[:, b4].unsqueeze(2).to_broadcast([P, 4, D]), ALU.mult)
                        a.then_inc(s_lc, 1)
                        if inB is not None:
                            nc.vector.tensor_copy(ct[h][:, :, D:P], inB[:, b4, 0:D]).then_inc(s_lc, 1)

                    def step(i, h):
                        if exists(i + 2):
                            inputs(i + 2, h)
                        dve.wait_ge(s_lm, n0 + i + 1)
                        b4 = bass.ds(i * 4, 4)
                        src = ps[2 + h][:, 0:4 * D].rearrange("p (b w) -> p b w", w=D)
                        if bias_ap is not None:
                            ins = nc.vector.tensor_tensor(dst[:, b4, :], src,
                                                          bias_ap.unsqueeze(1).to_broadcast([P, 4, D]), ALU.add)
                        else:
                            ins = nc.vector.tensor_copy(dst[:, b4, :], src)
                        ins.then_inc(s_lo, 1)

                    inputs(0, 0)
                    inputs(1, 1)
                    pieces(dve, step)
                    if relu:
                        dve.wait_ge(s_lo, n0 + R)
                        nc.vector.tensor_scalar(dst[:, :, :], dst[:, :, :], 0.0, None, ALU.max)

                @block.tensor
                def _(pe):
                    def turn(i, h):
                        pe.wait_ge(s_lc, c0 + halves * (i + 1))
                        if exists(i - 2):
                            pe.wait_ge(s_la, n0 + i - 1)
                        for k in range(4):
                            last = nc.tensor.transpose(ps[h][:, k * P:(k + 1) * P], ct[h][:, k, :], ident[:])
                        last.then_inc(s_lt, 1)

                    def step(i, h):
                        if exists(i + 1):
                            turn(i + 1, 1 - h)
                        pe.wait_ge(s_la, n0 + i + 1)
                        if exists(i - 2):
                            pe.wait_ge(s_lo, n0 + i - 1)
                        for k in range(4):
                            last = nc.tensor.matmul(ps[2 + h][:, k * D:(k + 1) * D], ctT[h][0:K, k * P:(k + 1) * P],
                                                    w, start=True, stop=True)
                        last.then_inc(s_lm, 1)
                    turn(0, 0)
                    pieces(pe, step)

                @block.scalar
                def _(act):
                    def step(i, h):
                        act.wait_ge(s_lt, n0 + i + 1)
                        if exists(i - 2):
                            act.wait_ge(s_lm, n0 + i - 1)
                        nc.scalar.copy(ctT[h][0:K, :], ps[h][0:K, :]).then_inc(s_la, 1)
                    pieces(act, step)
            lin_n[0] += R
            lin_c[0] += halves * R

        def vector_steps(f):
            with nc.Block() as block:
                @block.vector
                def _(dve):
                    c = Chain(dve, s_v)
                    c.n = vn[0]
                    f(c)
                    vn[0] = c.n

        def bc(v):
            return v[:, :].unsqueeze(2).to_broadcast([P, NB, D])

        s_sq = sem("s_sq")
        sq_n = [0]

        def root(v, r):
            with nc.Block() as block:
                @block.scalar
                def _(act):
                    nc.scalar.activation(r[:], v[:], ACT.Sqrt).then_inc(s_sq, 1)

                @block.vector
                def _(dve):
                    dve.wait_ge(s_sq, sq_n[0] + 1)
                    c = Chain(dve, s_v)
                    c.n = vn[0]
                    c.link(nc.vector.tensor_scalar(r[:], r[:], 1e-30, None, ALU.max))
                    c.link(nc.vector.reciprocal(nv[2][:], r[:]))
                    c.link(nc.vector.tensor_tensor(nv[2][:], v[:], nv[2][:], ALU.mult))
                    c.link(nc.vector.tensor_tensor(r[:], r[:], nv[2][:], ALU.add))
                    c.link(nc.vector.tensor_scalar(r[:], r[:], 0.5, None, ALU.mult))
                    vn[0] = c.n
            sq_n[0] += 1

        def layernorm(a, b, dst):
            def moments(c):
                c.link(nc.vector.tensor_reduce(nv[0][:], a, AX, ALU.add))
                c.link(nc.vector.tensor_scalar(nv[0][:], nv[0][:], 1.0 / D, None, ALU.mult))
                c.link(nc.vector.tensor_tensor(a, a, bc(nv[0]), ALU.subtract))
                c.link(nc.vector.tensor_tensor(b, a, a, ALU.mult))
                c.link(nc.vector.tensor_reduce(nv[0][:], b, AX, ALU.add))
                c.link(nc.vector.tensor_scalar(nv[0][:], nv[0][:], 1.0 / D, EPS_LN, ALU.mult, ALU.add))

            def scale(c):
                c.link(nc.vector.reciprocal(nv[1][:], nv[1][:]))
                c.link(nc.vector.tensor_tensor(dst, a, bc(nv[1]), ALU.mult))
            vector_steps(moments)
            root(nv[0], nv[1])
            vector_steps(scale)

        def l2norm(a, b, dst):
            def squares(c):
                c.link(nc.vector.tensor_tensor(b, a, a, ALU.mult))
                c.link(nc.vector.tensor_reduce(nv[0][:], b, AX, ALU.add))

            def scale(c):
                c.link(nc.vector.tensor_scalar(nv[1][:], nv[1][:], EPS_L2, None, ALU.max))
                c.link(nc.vector.reciprocal(nv[1][:], nv[1][:]))
                c.link(nc.vector.tensor_tensor(dst, a, bc(nv[1]), ALU.mult))
            vector_steps(squares)
            root(nv[0], nv[1])
            vector_steps(scale)

        def store_table(tab, parts):
            with nc.Block() as block:
                @block.sync
                def _(sp):
                    tv = tab.rearrange("(p b) w -> p b w", p=P)
                    for src, lo, hi in parts:
                        sp.dma_start(tv[:, :, lo:hi], src).then_inc(s_dma, 16)
                    sp.wait_ge(s_dma, dma_n[0] + 16 * len(parts))
            dma_n[0] += 16 * len(parts)

        s_ix = [sem(f"s_ix{h}") for h in range(2)]
        ga = [[sem(f"s_ga{n}_{h}") for h in range(2)] for n in range(5)]
        s_oh = sem("s_oh")
        s_grp = sem("s_grp")
        s_add = sem("s_add")
        s_acc = sem("s_acc")
        n_ix, n_pass, n_g, n_acc = [0], [0], [0], [0]
        R = TG // 2
        iota_b = iota16[:, :].unsqueeze(1).to_broadcast([P, G, P])

        def tile_blocks(engine, o, g):
            return nc.values_load_multi_w_load_instructions(
                tblk[o][:, bass.ds(g * 8, G)], engines=[engine], min_val=0, max_val=NB - 1,
                skip_runtime_bounds_check_because="a tile's block is a count of buckets minus one")[1]

        def stage_indices(act, o, i, h, first):
            g = 2 * i + h
            if not first:
                act.wait_ge(s_grp, n_g[0] + 2 * i + h - 1)
            nc.scalar.copy(nidx[h][:], far[o][:, bass.ds(g * G, G)]).then_inc(s_ix[h], 1)

        def gather_rows(pool, s_ga, tab, i, h, stride, w):
            pool_wait(pool, s_ix[h], n_ix[0] + i + 1)
            for k in range(G):
                pool.indirect_dma_start(M[h][:, k * stride:k * stride + w], None, tab[:, :],
                                        bass.IndirectOffsetOnAxis(nidx[h][:, k:k + 1], 0)).then_inc(s_ga[h], 16)

        def onehot(dve, o, i, h, first):
            g = 2 * i + h
            if not first:
                dve.wait_ge(s_grp, n_g[0] + 2 * i + h - 1)
            near = loc[o][:, bass.ds(g * G, G)].unsqueeze(2).to_broadcast([P, G, P])
            nc.vector.tensor_tensor(S[h][:].rearrange("p (g n) -> p g n", g=G), iota_b, near,
                                    ALU.is_equal).then_inc(s_oh, 1)

        def add_tiles(dve, o, i, h, bank):
            g = 2 * i + h
            blk = tile_blocks(mybir.EngineType.DVE, o, g)
            dve.wait_ge(s_grp, n_g[0] + g + 1)
            for k in range(G):
                a = acc[:, bass.ds(blk[k], 1), :]
                nc.vector.tensor_tensor(a, a, bank[:, k * 65:(k + 1) * 65].unsqueeze(1), ALU.add).then_inc(s_add, 1)
                dve.wait_ge(s_add, (n_acc[0] + g) * G + k + 1)
            dve.sem_inc(s_acc, 1)

        def seg_pass(o, tab, first_steps=None):
            s_ga = ga[n_pass[0]]
            with nc.Block() as block:
                @block.scalar
                def _(act):
                    for h in range(2):
                        stage_indices(act, o, 0, h, True)
                    with act.Fori(1, R, 1) as i:
                        for h in range(2):
                            stage_indices(act, o, i, h, False)

                @block.gpsimd
                def _(pool):
                    with pool.Fori(0, R, 1) as i:
                        for h in range(2):
                            gather_rows(pool, s_ga, tab, i, h, 65, D)
                    for h in range(2):
                        pool.wait_ge(s_ga[h], 16 * G * R)

                @block.vector
                def _(dve):
                    onehot(dve, o, 0, 0, True)
                    onehot(dve, o, 0, 1, True)
                    if first_steps:
                        c = Chain(dve, s_v)
                        c.n = vn[0]
                        first_steps(c)
                        c.wait()
                        vn[0] = c.n
                    add_tiles(dve, o, 0, 0, ps[0])
                    with dve.Fori(1, R, 1) as i:
                        onehot(dve, o, i, 0, False)
                        add_tiles(dve, o, i - 1, 1, ps[1])
                        onehot(dve, o, i, 1, False)
                        add_tiles(dve, o, i, 0, ps[0])
                    add_tiles(dve, o, R - 1, 1, ps[1])

                @block.tensor
                def _(pe):
                    def group(i, h, first):
                        g = 2 * i + h
                        pe.wait_ge(s_oh, n_g[0] + g + 1)
                        if not first:
                            pe.wait_ge(s_acc, n_acc[0] + g - 1)
                        pe.wait_ge(s_ga[h], 16 * G * (i + 1))
                        for k in range(G):
                            last = nc.tensor.matmul(ps[h][:, k * 65:(k + 1) * 65], S[h][:, k * P:(k + 1) * P],
                                                    M[h][:, k * 65:(k + 1) * 65], start=True, stop=True)
                        last.then_inc(s_grp, 1)
                    for h in range(2):
                        group(0, h, True)
                    with pe.Fori(1, R, 1) as i:
                        for h in range(2):
                            group(i, h, False)
            n_ix[0] += R
            n_pass[0] += 1
            n_g[0] += TG
            n_acc[0] += TG

        def clear_acc(c):
            c.inc(nc.vector.memset(nodes[3][:], 0.0))

        def ones_column(c):
            for h in range(2):
                c.inc(nc.vector.memset(M[h][:, 0:G * 65].rearrange("p (g w) -> p g w", w=65)[:, :, D], 1.0))

        rank_sync, rank_pool, rank_vector, rank_tensor = rank("d")
        with nc.Block() as block:
            block.sync(rank_sync)
            block.gpsimd(rank_pool)
            block.vector(rank_vector)
            block.tensor(rank_tensor)

        scat_sync, scat_scalar, scat_pool = scatter("d")
        rank_sync, rank_pool, rank_vector, rank_tensor = rank("s")
        with nc.Block() as block:
            @block.sync
            def _(sp):
                rank_sync(sp)
                scat_sync(sp)

            @block.gpsimd
            def _(pool):
                rank_pool(pool)
                scat_pool(pool)
            block.scalar(scat_scalar)
            block.vector(rank_vector)
            block.tensor(rank_tensor)

        _, scat_scalar, scat_pool = scatter("s")
        read_sync, read_vector = readback_d()
        loads = 16 * (1 + len(wts) + len(bias))
        with nc.Block() as block:
            @block.sync
            def _(sp):
                sp.dma_start(X, A["x"].rearrange("(b p) w -> p b w", p=P)).then_inc(s_dma, 16)
                for n in wts:
                    sp.dma_start(wts[n][:], A[n]).then_inc(s_dma, 16)
                for n in bias:
                    sp.dma_start(bias[n][:], A[n].partition_broadcast(P)).then_inc(s_dma, 16)
                read_sync(sp)
                sp.wait_ge(s_dma, dma_n[0] + loads)
                sp.dma_start(table[0].rearrange("(p b) w -> p b w", p=P), X).then_inc(s_dma, 16)
                sp.wait_ge(s_dma, dma_n[0] + loads + 16)
            block.scalar(scat_scalar)
            block.gpsimd(scat_pool)
            block.vector(read_vector)
        dma_n[0] += loads + 16

        sorted_s = nodes[2][:, 0:T * 3]
        with nc.Block() as block:
            @block.sync
            def _(sp):
                sp.dma_start(sorted_s, rec_s.rearrange("(p t) w -> p (t w)", p=P)).then_inc(s_dma, 16)

            @block.vector
            def _(dve):
                c = Chain(dve, s_v)
                c.n = vn[0]
                c.inc(nc.vector.tensor_copy(iota16[:], iota_n[:]))
                clear_acc(c)
                ones_column(c)
                dve.wait_ge(s_dma, dma_n[0] + 16)
                records = sorted_s.rearrange("p (t w) -> p t w", w=3)
                c.inc(nc.vector.tensor_copy(far["s"][:, :],
                                            sorted_s.bitcast(I32).rearrange("p (t w) -> p t w", w=3)[:, :, 0]))
                c.inc(nc.vector.tensor_copy(loc["s"][:, :], records[:, :, 1]))
                c.inc(nc.vector.tensor_copy(rel[:, :], records[:, :, 2]))
                c.wait()
                vn[0] = c.n
        dma_n[0] += 16

        seg_pass("d", table[0])

        def counts(c):
            c.link(nc.vector.tensor_scalar(cnt[:, :], acc[:, :, D], 1.0, None, ALU.max))

        def count_roots(c):
            c.inc(nc.vector.reciprocal(dinv[:, :], nv[1][:, :]))
            c.link(nc.vector.reciprocal(rcnt[:, :], cnt[:, :]))
        vector_steps(counts)
        root(cnt, nv[1])
        vector_steps(count_roots)
        node_linear(acc, rcnt, X, wts["w0a"][:], bias["b0a"][:], True, H)
        store_table(table[1], [(H, 0, D)])
        seg_pass("d", table[1], clear_acc)
        node_linear(acc, rcnt, H, wts["w0b"][:], bias["b0b"][:], False, Y)

        vector_steps(lambda c: c.link(nc.vector.tensor_tensor(Y, Y, X, ALU.add)))
        layernorm(Y, H, X)

        def l1_start(c):
            c.inc(nc.vector.tensor_copy(H, X))
            c.link(nc.vector.tensor_tensor(Z, X, bc(dinv), ALU.mult))
        vector_steps(l1_start)
        for layer in range(3):
            store_table(table[layer % 2], [(Z, 0, D)])

            def l1_sum(c):
                if layer == 0:
                    c.inc(nc.vector.tensor_copy(Y, X))
                else:
                    c.inc(nc.vector.tensor_tensor(Y, Y, H, ALU.add))
                clear_acc(c)
            seg_pass("s", table[layer % 2], l1_sum)

            def l1_step(c):
                c.link(nc.vector.tensor_tensor(acc[:, :, 0:D], acc[:, :, 0:D], bc(dinv), ALU.mult))
                c.link(nc.vector.tensor_tensor(H, acc[:, :, 0:D], H, ALU.add))
            vector_steps(l1_step)
            l2norm(H, Z, H)
            if layer < 2:
                vector_steps(lambda c: c.link(nc.vector.tensor_tensor(Z, H, bc(dinv), ALU.mult)))

        def l1_end(c):
            c.link(nc.vector.tensor_tensor(Y, Y, H, ALU.add))
            c.link(nc.vector.scalar_tensor_tensor(out=Y, in0=Y, scalar=0.25, in1=X, op0=ALU.mult, op1=ALU.add))
        vector_steps(l1_end)
        layernorm(Y, H, X)

        V0 = sb("V0", [P, GP])
        run3 = [sb(f"run3_{h}", [P, 3, G], BF16) for h in range(2)]
        rest = sb("rest", [P, G])
        sums = [work[:, h * 8 * (D + 1):(h + 1) * 8 * (D + 1)].rearrange("p (g w) -> p g w", w=D + 1) for h in range(2)]
        ty = sb("ty", [P, G * REL])
        sc = [sb(f"sc{h}", [P, G]) for h in range(4)]
        mt = sb("mt", [P, G])
        run = [sb(f"run{h}", [P, G + 1]) for h in range(2)]
        fac = [sb(f"fac{h}", [P, G]) for h in range(4)]
        fresh = far["d"][:].bitcast(F32)
        s_at = {n: sem("s_at_" + n) for n in ("st", "stc", "p", "mask", "v", "vt", "max", "me", "arg", "ex", "w",
                                              "fac", "own", "acc", "s32", "out")}
        n_at = [0, 0]
        SL = 4
        ga4 = [[sem(f"s_gb{n}_{h}") for h in range(SL)] for n in range(2)]
        s_ix4 = [sem(f"s_iy{h}") for h in range(SL)]

        def need(eng, s, v):
            if not isinstance(v, int) or v > 0:
                eng.wait_ge(s, v)

        def schedule(eng, step, extra, enter=None, leave=None):
            PEEL = SL + 2
            for t in range(PEEL):
                step(t, t % SL, t // SL)
            LOOPS = (TG - PEEL) // SL - 1
            with eng.Fori(0, LOOPS, 1) as i:
                if enter:
                    enter(i)
                for u in range(SL):
                    step(i * SL + (PEEL + u), (PEEL + u) % SL, i + (PEEL + u) // SL)
            if leave:
                leave(LOOPS)
            for t in range(PEEL + SL * LOOPS, TG + extra):
                step(t, t % SL, t // SL)

        def there(t, lo=0, hi=TG):
            return not isinstance(t, int) or lo <= t < hi

        def attention_pass(hop, tab, P3):
            S4, S16, more = slots(nodes[0])
            V = [V0[:], more[:, 0:GP]]
            M4 = [M[0][:], M[1][:], more[:, GP:GP + G * 96], more[:, GP + G * 96:GP + 2 * G * 96]]
            s_ga = ga4[hop]
            q = s_at
            b0, own0 = n_at
            turned = ps[0][:].bitcast(BF16)[:, 0:GP]
            ix0 = [hop * len(range(u, TG, SL)) for u in range(SL)]

            with nc.Block() as block:
                @block.gpsimd
                def _(pool):
                    def step(t, u, turn):
                        pool_wait(pool, s_ix4[u], ix0[u] + turn + 1)
                        for k in range(G):
                            pool.indirect_dma_start(M4[u][:, k * 96:(k + 1) * 96], None, tab[:, :],
                                                    bass.IndirectOffsetOnAxis(nidx[u][:, k:k + 1], 0)
                                                    ).then_inc(s_ga[u], 16)
                    schedule(pool, step, 0)
                    for u in range(SL):
                        pool.wait_ge(s_ga[u], 16 * G * len(range(u, TG, SL)))

                @block.scalar
                def _(act):
                    def stage(g, u):
                        need(act, q["w"], b0 + g - SL + 1 if not isinstance(g, int) or g >= SL else 0)
                        nc.scalar.copy(nidx[u][:], far["s"][:, bass.ds(g * G, G)]).then_inc(s_ix4[u], 1)

                    def step(t, u, turn):
                        w = (u + 1) % SL
                        v = (u + 2) % SL
                        x = (u + 3) % SL
                        if there(t + 1):
                            act.wait_ge(q["st"], b0 + t + 2)
                            nc.scalar.copy(ST16[w], turned).then_inc(q["stc"], 1)
                            act.wait_ge(s_oh, n_g[0] + t + 2)
                            if there(t - 1):
                                act.wait_ge(q["vt"], b0 + t)
                            nc.scalar.activation(V[w % 2], S16[w], ACT.Copy, bias=-BIG,
                                                 scale=BIG).then_inc(q["mask"], 1)
                        if there(t - 2):
                            act.wait_ge(q["max"], b0 + t - 1)
                            nc.scalar.activation(fac[v][:], fac[v][:], ACT.Exp).then_inc(q["fac"], 1)
                            act.wait_ge(q["arg"], b0 + t - 1)
                            if there(t - 4):
                                act.wait_ge(s_grp, n_g[0] + t - 3)
                            Wv = M2[v % 2][:, 0:G * 65].rearrange("p (g w) -> p g w", w=65)
                            nc.scalar.activation(Wv[:, :, D], sc[v][:], ACT.Exp).then_inc(q["ex"], 1)
                            act.wait_ge(q["ex"], b0 + t - 1)
                        if there(t - 5):
                            g = t - 5
                            blk = tile_blocks(mybir.EngineType.Activation, "s", g)
                            act.wait_ge(q["acc"], b0 + g + 1)
                        for k in range(G):
                            if there(t - 2):
                                ins = nc.scalar.activation(Wv[:, k, 0:D], M4[v][:, k * 96:k * 96 + D], ACT.Copy,
                                                           scale=Wv[:, k, D:D + 1])
                                if k == G - 1:
                                    ins.then_inc(q["w"], 1)
                            if there(t - 5):
                                need(act, q["out"], (b0 + g) * G + k)
                                nc.scalar.copy(acc[:, bass.ds(blk[k], 1), :],
                                               sums[x % 2][:, k + 1:k + 2, :]).then_inc(q["out"], 1)
                        if there(t + 1):
                            if there(t - 3):
                                act.wait_ge(s_grp, n_g[0] + t - 2)
                            nc.scalar.copy(S4[w], S16[w]).then_inc(q["s32"], 1)
                        if there(t - 2) and there(t + 2):
                            stage(t + 2, v)

                    def stage_first(act):
                        act.wait_ge(q["st"], b0 + 1)
                        nc.scalar.copy(ST16[0], turned).then_inc(q["stc"], 1)
                        act.wait_ge(s_oh, n_g[0] + 1)
                        nc.scalar.activation(V[0], S16[0], ACT.Copy, bias=-BIG, scale=BIG).then_inc(q["mask"], 1)
                        nc.scalar.copy(S4[0], S16[0]).then_inc(q["s32"], 1)

                    for g in range(SL):
                        stage(g, g)
                    stage_first(act)
                    schedule(act, step, 5)

                @block.tensor
                def _(pe):
                    def turn_onehots(g, u):
                        pe.wait_ge(s_oh, n_g[0] + g + 1)
                        need(pe, q["stc"], b0 + g)
                        for k in range(G):
                            last = nc.tensor.transpose(turned[:, k * P:(k + 1) * P],
                                                       S16[u][:, k * P:(k + 1) * P], ident16[:])
                        last.then_inc(q["st"], 1)

                    def near_part(g, u):
                        blk = tile_blocks(mybir.EngineType.PE, "s", g)
                        pe.wait_ge(q["stc"], b0 + g + 1)
                        if there(g - 2):
                            pe.wait_ge(q["v"], b0 + g - 1)
                        for k in range(G):
                            for j in range(3):
                                last = nc.tensor.matmul(ps[4 + u % 2][:, k * REL:(k + 1) * REL],
                                                        ST16[u][:, k * P:(k + 1) * P],
                                                        P3[:, bass.ds(blk[k], 1), j * REL:(j + 1) * REL],
                                                        start=(j == 0), stop=(j == 2))
                        last.then_inc(q["p"], 1)

                    def step(t, u, turn):
                        v, w = (u + 3) % SL, (u + 1) % SL
                        if there(t + 1):
                            turn_onehots(t + 1, w)
                        if there(t - 3):
                            x = (u + 1) % SL
                            pe.wait_ge(q["w"], b0 + t - 2)
                            pe.wait_ge(q["s32"], b0 + t - 2)
                            if there(t - 5):
                                pe.wait_ge(q["acc"], b0 + t - 4)
                            for k in range(G):
                                last = nc.tensor.matmul(ps[6 + x % 2][:, k * 65:(k + 1) * 65],
                                                        S4[x][:, k * P:(k + 1) * P],
                                                        M2[x % 2][:, k * 65:(k + 1) * 65], start=True, stop=True)
                            last.then_inc(s_grp, 1)
                        if there(t + 1):
                            near_part(t + 1, w)
                        if there(t - 1):
                            pe.wait_ge(q["max"], b0 + t)
                            for k in range(G):
                                for j in range(3):
                                    last = nc.tensor.matmul(ps[4 + v % 2][:, 256 + k:257 + k],
                                                            ST16[v][:, k * P:(k + 1) * P],
                                                            run3[v % 2][:, j, k:k + 1], start=(j == 0), stop=(j == 2))
                            last.then_inc(q["me"], 1)
                        if there(t):
                            pe.wait_ge(q["v"], b0 + t + 1)
                            for k in range(G):
                                last = nc.tensor.transpose(ps[2 + k // 4][:, (k % 4) * P:(k % 4 + 1) * P],
                                                           V[u % 2][:, k * P:(k + 1) * P], ident[:])
                            last.then_inc(q["vt"], 1)

                    turn_onehots(0, 0)
                    near_part(0, 0)
                    schedule(pe, step, 3)

                @block.vector
                def _(dve):
                    c = Chain(dve, q["own"])
                    c.n = own0

                    def onehot4(g, u):
                        if there(g - SL):
                            dve.wait_ge(q["s32"], b0 + g - SL + 1)
                            dve.wait_ge(q["st"], b0 + g - SL + 1)
                        near = loc["s"][:, bass.ds(g * G, G)].unsqueeze(2).to_broadcast([P, G, P])
                        nc.vector.tensor_tensor(S16[u].rearrange("p (g n) -> p g n", g=G), iota_b, near,
                                                ALU.is_equal).then_inc(s_oh, 1)

                    def exponents(g, u):
                        s1 = sc[u]
                        dve.wait_ge(q["me"], b0 + g + 1)
                        c.link(nc.vector.tensor_tensor(s1[:], s1[:], ps[4 + u % 2][:, 256:256 + G],
                                                       ALU.subtract))
                        nc.vector.tensor_scalar(s1[:], s1[:], 0.0, None, ALU.min).then_inc(q["arg"], 1)

                    def step(t, u, turn):
                        if there(t + 2):
                            onehot4(t + 2, (u + 2) % SL)
                        m, a = t - 1, t - 4
                        um, ua = (u + 3) % SL, u
                        sum_at = [0]

                        def tile_sum(k):
                            if there(a):
                                c.wait_for(sum_at[0])
                                sum_at[0] = c.inc(nc.vector.scalar_tensor_tensor(
                                    out=R1[:, k + 1, :], in0=R1[:, k, :], scalar=fac[ua][:, k:k + 1],
                                    in1=ps[6 + ua % 2][:, k * 65:(k + 1) * 65], op0=ALU.mult, op1=ALU.add))

                        R0, R1 = sums[1 - ua % 2], sums[ua % 2]
                        if there(a):
                            if there(a - 2):
                                dve.wait_ge(q["out"], (b0 + a - 1) * G)
                            sum_at[0] = c.inc(nc.vector.tensor_copy(R1[:, 0, :], R0[:, G, :]))
                        if there(t):
                            tv = ty[:].rearrange("p (g r) -> p g r", r=REL)
                            one = [P, G, REL]
                            c.inc(nc.vector.tensor_tensor(tv, iota_n[:, 0:REL].unsqueeze(1).to_broadcast(one),
                                                          rel[:, bass.ds(t * G, G)].unsqueeze(2).to_broadcast(one),
                                                          ALU.is_equal))
                        if there(m):
                            new, old = run[um % 2], run[1 - um % 2]
                            fr = fresh[:, bass.ds(m * G, G)]
                            r3, top = run3[um % 2], new[:, 1:G + 1]
                            dve.wait_ge(q["vt"], b0 + m + 1)
                            c.inc(nc.vector.tensor_copy(new[:, 0:1], old[:, G:G + 1]))
                            c.inc(nc.vector.tensor_reduce(mt[:, 0:4],
                                                          ps[2][:, 0:512].rearrange("p (g n) -> p g n", n=P),
                                                          AX, ALU.max))
                            c.link(nc.vector.tensor_reduce(mt[:, 4:G],
                                                           ps[3][:, 0:3 * P].rearrange("p (g n) -> p g n", n=P),
                                                           AX, ALU.max))
                            max_at = c.inc(nc.vector.tensor_tensor_scan(top, fr, mt[:], new[:, 0:1], ALU.add, ALU.max))
                        if there(a):
                            dve.wait_ge(q["fac"], b0 + a + 1)
                            dve.wait_ge(s_grp, n_g[0] + a + 1)
                        tile_sum(0)
                        if there(m):
                            c.wait_for(max_at)
                            c.inc(nc.vector.tensor_tensor(fac[um][:], new[:, 0:G], fr, ALU.add))
                            max_at = c.inc(nc.vector.tensor_copy(r3[:, 0, :], top))
                        tile_sum(1)
                        if there(m):
                            c.wait_for(max_at)
                            c.inc(nc.vector.tensor_tensor(fac[um][:], fac[um][:], top, ALU.subtract))
                            max_at = c.inc(nc.vector.tensor_tensor(rest[:], top, r3[:, 0, :], ALU.subtract))
                        tile_sum(2)
                        if there(m):
                            c.wait_for(max_at)
                            max_at = c.inc(nc.vector.tensor_copy(r3[:, 1, :], rest[:]))
                        tile_sum(3)
                        if there(m):
                            c.wait_for(max_at)
                            nc.vector.tensor_tensor(r3[:, 2, :], rest[:], r3[:, 1, :],
                                                    ALU.subtract).then_inc(q["max"], 1)
                        tile_sum(4)
                        if there(t):
                            Mv = M4[u].rearrange("p (g w) -> p g w", w=96)
                            uv = V2[:].rearrange("p (g r) -> p g r", r=REL)
                            dve.wait_ge(s_ga[u], 16 * G * (turn + 1))
                            dve.wait_ge(q["p"], b0 + t + 1)
                            uv_at = c.inc(nc.vector.tensor_tensor(
                                uv, Mv[:, :, D:D + REL],
                                ps[4 + u % 2][:, 0:G * REL].rearrange("p (g r) -> p g r", r=REL), ALU.add))
                        tile_sum(5)
                        if there(t):
                            c.wait_for(uv_at)
                            uv_at = c.inc(nc.vector.tensor_tensor(uv, uv, tv, ALU.mult))
                        tile_sum(6)
                        if there(t):
                            s1 = sc[u]
                            if there(t - SL):
                                dve.wait_ge(q["ex"], b0 + t - SL + 1)
                            c.wait_for(uv_at)
                            c.inc(nc.vector.tensor_reduce(s1[:], uv, AX, ALU.add))
                        c.wait()
                        if there(a):
                            dve.sem_inc(q["acc"], 1)
                        if there(t):
                            c.link(nc.vector.scalar_tensor_tensor(out=s1[:], in0=s1[:], scalar=0.2, in1=s1[:],
                                                                  op0=ALU.mult, op1=ALU.max))
                            dve.wait_ge(q["mask"], b0 + t + 1)
                            Vv = V[u % 2].rearrange("p (g n) -> p g n", n=P)
                            nc.vector.tensor_tensor(Vv, Vv, s1[:].unsqueeze(2).to_broadcast([P, G, P]),
                                                    ALU.add).then_inc(q["v"], 1)
                        if there(m):
                            exponents(m, um)

                    steps = SL * (5 + 9 + 1 + 1 + G)
                    onehot4(0, 0)
                    onehot4(1, 1)
                    schedule(dve, step, 4, lambda i: c.enter(i, steps), lambda n: c.leave(n))
                    n_at[1] = c.n
            n_g[0] += TG
            n_at[0] += TG

        V2 = sb("V2", [P, G * REL])
        acc3 = nodes[3][:, 0:NB * 3 * REL // 2].bitcast(BF16).rearrange("p (b w) -> p b w", w=3 * REL)

        def split3(c, a, parts):
            c.link(nc.vector.tensor_copy(parts[0], a))
            c.link(nc.vector.tensor_tensor(a, a, parts[0], ALU.subtract))
            c.link(nc.vector.tensor_copy(parts[1], a))
            c.link(nc.vector.tensor_tensor(parts[2], a, parts[1], ALU.subtract))

        with nc.Block() as block:
            @block.tensor
            def _(pe):
                nc.tensor.matmul(ps[0][0:D, 0:REL], wts["WT"][:, 0:D], wts["relT"][:], start=True, stop=True)
                nc.tensor.matmul(ps[0][0:D, REL:2 * REL], wts["WT"][:, D:2 * D], wts["relT"][:], start=True,
                                 stop=True).then_inc(s_pe, 1)

            @block.vector
            def _(dve):
                dve.wait_ge(s_pe, pen[0] + 1)
                nc.vector.tensor_copy(pq_w[:], ps[0][0:D, 0:2 * REL]).then_inc(s_v, 1)
                dve.wait_ge(s_v, vn[0] + 1)
        pen[0] += 1
        vn[0] += 1

        def l2_start(c):
            c.inc(nc.vector.tensor_copy(ident16[:], ident[:]))
            c.inc(nc.vector.tensor_copy(Y, X))
            c.inc(nc.vector.tensor_copy(H, X))
            row = nodes[4][0:1, 0:T]
            c.link(nc.vector.tensor_copy(row.rearrange("p (g w) -> p g w", w=G),
                                         tblk["s"].rearrange("p (g w) -> p g w", w=8)[:, :, 0:G]))
            c.link(nc.vector.tensor_tensor(nodes[4][0:1, T + 1:2 * T], row[:, 1:T], row[:, 0:T - 1], ALU.not_equal))
            c.link(nc.vector.memset(nodes[4][0:1, T:T + 1], 1.0))
        vector_steps(l2_start)
        with nc.Block() as block:
            CH = 476

            @block.tensor
            def _(pe):
                for n, k in enumerate(range(0, T, CH)):
                    w = min(CH, T - k)
                    nc.tensor.matmul(ps[n][:, 0:w], ones[0:1, :], nodes[4][0:1, T + k:T + k + w], start=True,
                                     stop=True).then_inc(s_pe, 1)

            @block.vector
            def _(dve):
                for n, k in enumerate(range(0, T, CH)):
                    w = min(CH, T - k)
                    dve.wait_ge(s_pe, pen[0] + n + 1)
                    nc.vector.tensor_scalar(fresh[:, k:k + w], ps[n][:, 0:w], -BIG, None, ALU.mult)
        pen[0] += 4
        for hop in range(2):
            node_linear(Y, None, None, pq_w[:], None, False, Z)
            t2 = table[2 + hop]
            store_table(t2, [(Y, 0, D), (Z[:, :, REL:2 * REL], D, D + REL)])

            def hop_start(c):
                near, near3 = Z[:, :, 0:REL], acc3[:, :, :]
                split3(c, near, [near3[:, :, j * REL:(j + 1) * REL] for j in range(3)])
                words = NB * 3 * REL // 2
                c.link(nc.vector.tensor_copy(nodes[4][:, 0:words], nodes[3][:, 0:words]))
                clear_acc(c)
                c.inc(nc.vector.memset(sums[1], 0.0))
                c.link(nc.vector.memset(run[1][:], -BIG))
            vector_steps(hop_start)
            attention_pass(hop, t2, nodes[4][:, 0:NB * 3 * REL // 2].bitcast(BF16).rearrange("p (b w) -> p b w", w=3 * REL))

            def hop_sum(c):
                c.link(nc.vector.tensor_scalar(nv[0][:, :], acc[:, :, D], 1e-30, None, ALU.max))
                c.link(nc.vector.reciprocal(nv[0][:], nv[0][:]))
                c.link(nc.vector.tensor_tensor(Z, acc[:, :, 0:D], bc(nv[0]), ALU.mult))
                c.link(nc.vector.tensor_tensor(Y, Y, Z, ALU.add))
            vector_steps(hop_sum)
            l2norm(Y, Z, Y)
            vector_steps(lambda c: c.link(nc.vector.scalar_tensor_tensor(out=H, in0=H, scalar=0.5, in1=Y, op0=ALU.mult,
                                                                         op1=ALU.add)))
        with nc.Block() as block:
            @block.sync
            def _(sp):
                sp.dma_start(X, table[2].rearrange("(p b) w -> p b w", p=P)[:, :, 0:D]).then_inc(s_dma, 16)
                sp.wait_ge(s_dma, dma_n[0] + 16)
        dma_n[0] += 16
        vector_steps(lambda c: c.link(nc.vector.tensor_tensor(Y, X, H, ALU.add)))
        layernorm(Y, H, X)

        EW = G * (2 + EA)
        KE = 3 * EA
        hT = [V0[0:D + 1, :], work[0:D + 1, 0:GP]]
        w_ea = sb("w_ea", [KE, D])
        w_ea3 = [sb(f"w_ea3_{j}", [KE, D], BF16) for j in range(3)]
        q3 = {n: sem("s_m_" + n) for n in ("eb0", "eb1", "eb2", "eb3", "own", "split", "st", "et", "s32", "uc", "h", "hc",
                                           "m", "mc")}
        s_eb = [q3[f"eb{k}"] for k in range(4)]

        def edge_mlp_pass(U3):
            q = q3
            S4, S16, more = slots(nodes[4])
            eb = [more[:, k * EW:(k + 1) * EW] for k in range(4)]
            at = 4 * EW
            HE = G * KE // 2
            e16 = [more[:, at + k * HE:at + (k + 1) * HE].bitcast(BF16).rearrange("p (g w) -> p g w", w=KE)
                   for k in range(2)]
            at += 2 * HE
            eT = [more[0:KE, at + k * (GP // 2):at + (k + 1) * (GP // 2)].bitcast(BF16) for k in range(2)]
            assert at + GP <= NA - 4 * GP
            UW = 3 * D // 2
            uc = [M[k][:, 0:G * UW] for k in range(2)]
            uc16 = [w.bitcast(BF16).rearrange("p (g w) -> p g w", w=3 * D) for w in uc]
            U3w = U3.rearrange("p (b w) -> p b w", w=UW)
            turned = ps[0][:].bitcast(BF16)[:, 0:GP]
            e_turned = ps[1][0:KE, :].bitcast(BF16)[:, 0:GP]
            rv = rec_d.rearrange("(p t) w -> p (t w)", p=P)
            g0 = n_g[0]
            with nc.Block() as block:
                @block.sync
                def _(sp):
                    def step(t, u, turn):
                        if there(t - SL):
                            sp.wait_ge(q["split"], t - SL + 1)
                        sp.dma_start(eb[u], rv[:, bass.ds(t * EW, EW)]).then_inc(s_eb[u], 16)
                    for t in range(4):
                        step(t, t, 0)
                    with sp.Fori(1, TG // SL, 1) as i:
                        for u in range(SL):
                            step(i * SL + u, u, i)
                    for t in range(TG // SL * SL, TG):
                        step(t, t % SL, t // SL)

                @block.vector
                def _(dve):
                    c = Chain(dve, q["own"])

                    def one_hots(g, u):
                        if there(g - SL):
                            dve.wait_ge(q["s32"], g - SL + 1)
                            dve.wait_ge(q["st"], g - SL + 1)
                        near = loc["d"][:, bass.ds(g * G, G)].unsqueeze(2).to_broadcast([P, G, P])
                        nc.vector.tensor_tensor(S16[u].rearrange("p (g n) -> p g n", g=G), iota_b, near,
                                                ALU.is_equal).then_inc(s_oh, 1)

                    def split(g, u, turn):
                        dve.wait_ge(s_eb[u], 16 * (turn + 1))
                        if there(g - 2):
                            dve.wait_ge(q["st"], g - 1)
                        a = eb[u].rearrange("p (g w) -> p g w", w=2 + EA)[:, :, 2:2 + EA]
                        part = [e16[u % 2][:, :, j * EA:(j + 1) * EA] for j in range(3)]
                        r = V2[:].rearrange("p (g w) -> p g w", w=EA)
                        c.link(nc.vector.tensor_copy(part[0], a))
                        c.link(nc.vector.tensor_tensor(r, a, part[0], ALU.subtract))
                        c.link(nc.vector.tensor_copy(part[1], r))
                        nc.vector.tensor_tensor(part[2], r, part[1], ALU.subtract).then_inc(q["split"], 1)

                    def accumulate(g, u):
                        blk = tile_blocks(mybir.EngineType.DVE, "d", g)
                        dve.wait_ge(s_grp, g0 + g + 1)
                        for k in range(G):
                            a = acc[:, bass.ds(blk[k], 1), :]
                            c.link(nc.vector.tensor_tensor(a, a, ps[6 + u % 2][:, k * 65:(k + 1) * 65].unsqueeze(1),
                                                           ALU.add))
                        dve.sem_inc(s_acc, 1)

                    def step(t, u, turn):
                        w = (u + 1) % SL
                        if there(t + 1):
                            one_hots(t + 1, w)
                            split(t + 1, w, turn + (u + 1) // SL)
                        if there(t - 3):
                            accumulate(t - 3, w)
                    one_hots(0, 0)
                    split(0, 0, 0)
                    steps = SL * (3 + G)
                    schedule(dve, step, 3, lambda i: c.enter(i, steps), lambda n: c.leave(n))

                @block.scalar
                def _(act):
                    def copies(g, u):
                        blk = tile_blocks(mybir.EngineType.Activation, "d", g)
                        if there(g - 2):
                            act.wait_ge(q["h"], g - 1)
                        for k in range(G):
                            ins = nc.scalar.copy(uc[u % 2][:, k * UW:(k + 1) * UW].unsqueeze(1),
                                                 U3w[:, bass.ds(blk[k], 1), :])
                        ins.then_inc(q["uc"], 1)
                        act.wait_ge(q["st"], g + 1)
                        nc.scalar.copy(ST16[u], turned).then_inc(q["et"], 1)
                        nc.scalar.copy(eT[u % 2], e_turned).then_inc(q["et"], 1)
                        if there(g - SL):
                            act.wait_ge(s_grp, g0 + g - SL + 1)
                        nc.scalar.copy(S4[u], S16[u]).then_inc(q["s32"], 1)

                    def step(t, u, turn):
                        w, v = (u + 1) % SL, (u + 3) % SL
                        if there(t + 1):
                            copies(t + 1, w)
                        if there(t):
                            act.wait_ge(q["h"], t + 1)
                            if there(t - 2):
                                act.wait_ge(q["m"], t - 1)
                            nc.scalar.activation(hT[u % 2][0:D, 0:512], ps[2][0:D, 0:512],
                                                 ACT.Relu).then_inc(q["hc"], 1)
                            nc.scalar.activation(hT[u % 2][0:D, 512:GP], ps[3][0:D, 0:GP - 512],
                                                 ACT.Relu).then_inc(q["hc"], 1)
                        if there(t - 1):
                            act.wait_ge(q["m"], t)
                            if there(t - 3):
                                act.wait_ge(s_grp, g0 + t - 2)
                            nc.scalar.activation(M2[v % 2][:, 0:G * 65].rearrange("p (g w) -> p g w", w=65)[:, :, 0:D],
                                                 ps[4][:, 0:G * D].rearrange("p (g w) -> p g w", w=D),
                                                 ACT.Relu).then_inc(q["mc"], 1)
                    copies(0, 0)
                    schedule(act, step, 1)

                @block.tensor
                def _(pe):
                    def turn_over(g, u):
                        pe.wait_ge(s_oh, g0 + g + 1)
                        pe.wait_ge(q["split"], g + 1)
                        if there(g - 1):
                            pe.wait_ge(q["et"], 2 * g)
                        for k in range(G):
                            nc.tensor.transpose(turned[:, k * P:(k + 1) * P], S16[u][:, k * P:(k + 1) * P], ident16[:])
                        for k in range(G):
                            last = nc.tensor.transpose(e_turned[:, k * P:(k + 1) * P], e16[u % 2][:, k, :], ident16[:])
                        last.then_inc(q["st"], 1)

                    def step(t, u, turn):
                        w, v, x = (u + 1) % SL, (u + 3) % SL, (u + 2) % SL
                        if there(t + 1):
                            turn_over(t + 1, w)
                        if there(t):
                            pe.wait_ge(q["et"], 2 * (t + 1))
                            pe.wait_ge(q["uc"], t + 1)
                            if there(t - 1):
                                pe.wait_ge(q["hc"], 2 * t)
                            for k in range(G):
                                o_ap = ps[2 + k // 4][0:D, (k % 4) * P:(k % 4 + 1) * P]
                                for j in range(3):
                                    nc.tensor.matmul(o_ap, uc16[u % 2][:, k, j * D:(j + 1) * D],
                                                     ST16[u][:, k * P:(k + 1) * P], start=(j == 0), stop=False)
                                for j in range(3):
                                    last = nc.tensor.matmul(o_ap, w_ea3[j][:], eT[u % 2][:, k * P:(k + 1) * P],
                                                            start=False, stop=(j == 2))
                            last.then_inc(q["h"], 1)
                        if there(t - 1):
                            pe.wait_ge(q["hc"], 2 * t)
                            if there(t - 2):
                                pe.wait_ge(q["mc"], t - 1)
                            for k in range(G):
                                last = nc.tensor.matmul(ps[4][:, k * D:(k + 1) * D], hT[v % 2][:, k * P:(k + 1) * P],
                                                        wts["w3c"][:], start=True, stop=True)
                            last.then_inc(q["m"], 1)
                        if there(t - 2):
                            pe.wait_ge(q["mc"], t - 1)
                            pe.wait_ge(q["s32"], t - 1)
                            if there(t - 4):
                                pe.wait_ge(s_acc, n_acc[0] + t - 3)
                            for k in range(G):
                                last = nc.tensor.matmul(ps[6 + x % 2][:, k * 65:(k + 1) * 65],
                                                        S4[x][:, k * P:(k + 1) * P],
                                                        M2[x % 2][:, k * 65:(k + 1) * 65], start=True, stop=True)
                            last.then_inc(s_grp, 1)
                    turn_over(0, 0)
                    schedule(pe, step, 2)
            n_g[0] += TG
            n_acc[0] += TG

        with nc.Block() as block:
            @block.sync
            def _(sp):
                for j in range(3):
                    sp.dma_start(w_ea[j * EA:(j + 1) * EA, :], A["w3b"]).then_inc(s_dma, 16)
                sp.wait_ge(s_dma, dma_n[0] + 48)
        dma_n[0] += 48

        node_linear(X, None, None, wts["w3a"][:], bias["b3a"][:], False, Z)

        def l3_start(c):
            clear_acc(c)
            for h in range(2):
                c.inc(nc.vector.memset(hT[h][D:D + 1, :], 1.0))
                c.inc(nc.vector.memset(M2[h][:, 0:G * 65].rearrange("p (g w) -> p g w", w=65)[:, :, D], 1.0))
            split3(c, w_ea[:], [w[:] for w in w_ea3])
            c.inc(nc.vector.memset(w_ea3[1][2 * EA:KE, :], 0.0))
            c.inc(nc.vector.memset(w_ea3[2][EA:2 * EA, :], 0.0))
            c.inc(nc.vector.memset(w_ea3[2][2 * EA:KE, :], 0.0))
            split3(c, Z, [u3[:, :, j * D:(j + 1) * D] for j in range(3)])
        U3 = nodes12[:, 0:NB * 3 * D // 2]
        u3 = U3.bitcast(BF16).rearrange("p (b w) -> p b w", w=3 * D)
        vector_steps(l3_start)
        edge_mlp_pass(U3)

        def l3_end(c):
            c.link(nc.vector.tensor_tensor(Y, acc[:, :, 0:D], bc(rcnt), ALU.mult))
            c.link(nc.vector.scalar_tensor_tensor(out=Y, in0=X, scalar=2.0, in1=Y, op0=ALU.mult, op1=ALU.add))
        vector_steps(l3_end)
        layernorm(Y, H, X)

        with nc.Block() as block:
            @block.sync
            def _(sp):
                sp.dma_start(out[0:97 * P, :].rearrange("(b p) w -> p b w", p=P), X[:, 0:97, :]).then_inc(s_dma, 16)
                sp.dma_start(out[97 * P:NODES, :], X[0:NODES - 97 * P, 97, :]).then_inc(s_dma, 16)
                sp.wait_ge(s_dma, dma_n[0] + 32)


def kernel(**inputs):
    import numpy as np
    import concourse.bacc as bacc
    from concourse.bass_utils import run_bass_kernel_spmd as run

    def pad(a, n, v):
        a = np.ascontiguousarray(a)
        return np.concatenate([a, np.full((n - a.shape[0],) + a.shape[1:], v, a.dtype)])

    nc = bacc.Bacc("TRN2", target_bir_lowering=False, num_devices=1)
    E = P * J
    arrays = {
        "x": pad(inputs["x"], ROWS, 0),
        "src": pad(inputs["src"], E, PAD_NODE).reshape(P, J),
        "dst": pad(inputs["dst"], E, PAD_NODE).reshape(P, J),
        "typ": pad(inputs["edge_type_32"], E, 0).reshape(P, J),
        "ea": pad(inputs["edge_attr_32"], E, 0),
        "w0a": np.concatenate([np.asarray(inputs["L0_gnn_W1_l"]).T, np.asarray(inputs["L0_gnn_W1_r"]).T]),
        "w0b": np.concatenate([np.asarray(inputs["L0_gnn_W2_l"]).T, np.asarray(inputs["L0_gnn_W2_r"]).T]),
        "b0a": np.ascontiguousarray(inputs["L0_gnn_b1"]),
        "b0b": np.ascontiguousarray(inputs["L0_gnn_b2"]),
        "relT": np.ascontiguousarray(np.asarray(inputs["L2_gnn_relation_emb"]).T),
        "WT": np.ascontiguousarray(np.asarray(inputs["L2_gnn_W"]).T),
        "w3a": np.ascontiguousarray(np.asarray(inputs["L3_gnn_W1"])[0:D]),
        "w3b": np.ascontiguousarray(np.asarray(inputs["L3_gnn_W1"])[D:]),
        "b3a": np.ascontiguousarray(inputs["L3_gnn_b1"]),
        "w3c": np.concatenate([np.asarray(inputs["L3_gnn_W2"]), np.asarray(inputs["L3_gnn_b2"])[None]]),
    }
    args, feed = {}, {}
    for name, a in arrays.items():
        feed[f"in_{name}"] = a
        args[name] = nc.dram_tensor(f"in_{name}", a.shape, mybir.dt.from_np(a.dtype), kind="ExternalInput").ap()
    out = nc.dram_tensor("out_x", (NODES, D), F32, kind="ExternalOutput").ap()
    build(nc, args, out)
    r = run(nc, [feed], core_ids=[0])
    return r.results[0]["out_x"]
```
